# Optimizing a Trainium2 kernel written in Bass

```python
import numpy as np
import jax
import jax.numpy as jnp

def _softmax(x, axis=-1):
    return jax.nn.softmax(x, axis=axis)

def _gelu(x):
    return jax.nn.gelu(x, approximate=True)

def _silu(x):
    return jax.nn.silu(x)

def _sigmoid(x):
    return jax.nn.sigmoid(x)

def _layernorm(x, axis=-1, eps=1e-05):
    m = jnp.mean(x, axis=axis, keepdims=True)
    v = jnp.var(x, axis=axis, keepdims=True)
    return (x - m) / jnp.sqrt(v + eps)

def _scatter_add(tgt, idx, src, axis=0):
    return tgt.at[idx].add(src)

def _segment_sum(src, seg, n):
    return jax.ops.segment_sum(src, seg, n)
kernel_name = 'mk_perceiver_d2_seqx_r8_c82c2b'

def setup_inputs(seed: int=0):
    np.random.seed(seed)
    _w = jnp.asarray

    def _rec_inputs():
        import jax
        import jax.numpy as jnp
        _rk = jax.random.key(seed)
        x = 7.22e-05 + 1 * jax.random.normal(jax.random.fold_in(_rk, 1), (128, 32, 128), jnp.float32)
        _lenS = 32 - jax.random.randint(jax.random.fold_in(_rk, 7), (128,), 0, max(1, 32 // 4) + 1, jnp.int32)
        _lenS2 = 257 - jax.random.randint(jax.random.fold_in(_rk, 8), (128,), 0, max(1, 257 // 4) + 1, jnp.int32)
        _ctx_768P = jax.random.normal(jax.random.fold_in(_rk, 11), (128, 16, 96), jnp.float32)
        _ctx_768c = jax.random.dirichlet(jax.random.fold_in(_rk, 511), 0.3 * jnp.ones((16,), jnp.float32), (128, 257))
        _ctx_768t = jnp.einsum('bsk,bkd->bsd', _ctx_768c, _ctx_768P)
        _ctx_768t = _ctx_768t * jax.lax.rsqrt(jnp.mean(jnp.square(_ctx_768t)) + 1e-12) * 0.953939
        ctx_768 = 2.09791e-05 + 1.00001 * (_ctx_768t + 0.3 * jax.random.normal(jax.random.fold_in(_rk, 611), (128, 257, 96), jnp.float32))
        return (x, ctx_768)
    x, ctx_768 = _rec_inputs()

    def _L0_xattn_setup():
        import jax, jax.numpy as jnp
        import numpy as np
        HEADS = 16
        DIM_HEAD = 64
        key = jax.random.key(seed)
        ks = jax.random.split(key, 7)
        B, Nq, Dq = (4, 256, 128)
        Nk, Dc = (128, 96)
        inner = HEADS * DIM_HEAD
        sq = 1.0 / np.sqrt(Dq)
        sc = 1.0 / np.sqrt(Dc)
        si = 1.0 / np.sqrt(inner)
        return {'x': jax.random.normal(ks[0], (B, Nq, Dq), dtype=jnp.float32), 'context': jax.random.normal(ks[1], (B, Nk, Dc), dtype=jnp.float32), 'Wq': jax.random.normal(ks[2], (Dq, inner), dtype=jnp.float32) * sq, 'Wk': jax.random.normal(ks[3], (Dc, inner), dtype=jnp.float32) * sc, 'Wv': jax.random.normal(ks[4], (Dc, inner), dtype=jnp.float32) * sc, 'Wo': jax.random.normal(ks[5], (inner, Dq), dtype=jnp.float32) * si, 'bo': jax.random.normal(ks[6], (Dq,), dtype=jnp.float32) * 0.01}
    _L0_xattn_all = _L0_xattn_setup()
    _L0_xattn_in = {k: v for k, v in _L0_xattn_all.items() if k in ('Wq', 'Wk', 'Wv', 'Wo', 'bo')}
    del _L0_xattn_all

    def _L0_attn_setup():
        import jax, jax.numpy as jnp
        import numpy as np
        B, N, D = (4, 512, 128)
        H, DH = (16, 64)
        DFF = 512
        M = 64
        EPS_KERN = 1e-06
        EPS_LN = 1e-06

        def _softmax_kernel_feats(data, proj, is_query):
            dn = 1.0 / jnp.sqrt(jnp.sqrt(jnp.float32(data.shape[-1])))
            ratio = 1.0 / jnp.sqrt(jnp.float32(proj.shape[0]))
            data_dash = jnp.einsum('bnhd,md->bnhm', data * dn, proj)
            diag = jnp.sum(jnp.square(data), axis=-1, keepdims=True) * (dn * dn) / 2.0
            if is_query:
                mx = jnp.max(data_dash, axis=-1, keepdims=True)
            else:
                mx = jnp.max(data_dash)
            return ratio * (jnp.exp(data_dash - diag - mx) + EPS_KERN)

        def _layernorm(x, g, b):
            mu = jnp.mean(x, axis=-1, keepdims=True)
            var = jnp.mean(jnp.square(x - mu), axis=-1, keepdims=True)
            return (x - mu) * jax.lax.rsqrt(var + EPS_LN) * g + b

        def _encoder_forward(x, Wq, Wk, Wv, Wo, proj, W1, b1, W2, b2, ln1_g, ln1_b, ln2_g, ln2_b):
            q = jnp.einsum('bnd,dhk->bnhk', x, Wq)
            k = jnp.einsum('bnd,dhk->bnhk', x, Wk)
            v = jnp.einsum('bnd,dhk->bnhk', x, Wv)
            qf = _softmax_kernel_feats(q, proj, True)
            kf = _softmax_kernel_feats(k, proj, False)
            kv = jnp.einsum('bnhm,bnhd->bhmd', kf, v)
            num = jnp.einsum('bnhm,bhmd->bnhd', qf, kv)
            den = jnp.einsum('bnhm,bhm->bnh', qf, jnp.sum(kf, axis=1))
            attn = num / den[..., None]
            attn_out = jnp.einsum('bnhd,hdo->bno', attn, Wo)
            out1 = _layernorm(x + attn_out, ln1_g, ln1_b)
            h = jax.nn.elu(out1 @ W1 + b1)
            ffn_out = h @ W2 + b2
            return _layernorm(out1 + ffn_out, ln2_g, ln2_b)
        key = jax.random.key(seed)
        ks = jax.random.split(key, 12)
        s = 0.02
        inp = {'x': jax.random.normal(ks[0], (B, N, D), jnp.float32), 'Wq': jax.random.normal(ks[1], (D, H, DH), jnp.float32) * s, 'Wk': jax.random.normal(ks[2], (D, H, DH), jnp.float32) * s, 'Wv': jax.random.normal(ks[3], (D, H, DH), jnp.float32) * s, 'Wo': jax.random.normal(ks[4], (H, DH, D), jnp.float32) * s, 'proj': jax.random.normal(ks[5], (M, DH), jnp.float32), 'W1': jax.random.normal(ks[6], (D, DFF), jnp.float32) * s, 'b1': jnp.zeros((DFF,), jnp.float32), 'W2': jax.random.normal(ks[7], (DFF, D), jnp.float32) * s, 'b2': jnp.zeros((D,), jnp.float32), 'ln1_g': jnp.ones((D,), jnp.float32), 'ln1_b': jnp.zeros((D,), jnp.float32), 'ln2_g': jnp.ones((D,), jnp.float32), 'ln2_b': jnp.zeros((D,), jnp.float32)}
        return inp
    _L0_attn_all = _L0_attn_setup()
    _L0_attn_in = {k: v for k, v in _L0_attn_all.items() if k in ('Wq', 'Wk', 'Wv', 'Wo', 'proj', 'W1', 'b1', 'W2', 'b2', 'ln1_g', 'ln1_b', 'ln2_g', 'ln2_b')}
    del _L0_attn_all

    def _L0_ffn_setup():
        import jax, jax.numpy as jnp
        import numpy as np
        D = 128
        H = 128
        E = 8
        K = 2
        I = 2 * 128
        ROUTE_SCALE = 1.0
        key = jax.random.key(seed)
        ks = jax.random.split(key, 12)
        s = lambda *sh: 1.0 / np.sqrt(sh[-1])
        return {'x': jax.random.normal(ks[0], (1, 256, D), jnp.float32), 'gate_w': jax.random.normal(ks[1], (E, D), jnp.float32) * s(E, D), 'w1': jax.random.normal(ks[2], (E, H, D), jnp.float32) * s(H, D), 'b1': jax.random.normal(ks[3], (E, H), jnp.float32) * 0.01, 'w2': jax.random.normal(ks[4], (E, D, H), jnp.float32) * s(D, H), 'b2': jax.random.normal(ks[5], (E, D), jnp.float32) * 0.01, 'w3': jax.random.normal(ks[6], (E, H, D), jnp.float32) * s(H, D), 'b3': jax.random.normal(ks[7], (E, H), jnp.float32) * 0.01, 'sw1': jax.random.normal(ks[8], (I, D), jnp.float32) * s(I, D), 'sw2': jax.random.normal(ks[9], (I, D), jnp.float32) * s(I, D), 'sw3': jax.random.normal(ks[10], (D, I), jnp.float32) * s(D, I)}
    _L0_ffn_all = _L0_ffn_setup()
    _L0_ffn_in = {k: v for k, v in _L0_ffn_all.items() if k in ('gate_w', 'w1', 'b1', 'w2', 'b2', 'w3', 'b3', 'sw1', 'sw2', 'sw3')}
    del _L0_ffn_all

    def _L1_xattn_setup():
        import jax, jax.numpy as jnp
        import numpy as np
        NUM_HEADS = 16
        key = jax.random.key(seed)
        ks = jax.random.split(key, 8)
        dim, cond_dim = (128, 96)
        B, N, condN = (4, 256, 128)
        s = lambda k, shp, fan: jax.random.normal(k, shp, dtype=jnp.float32) * fan ** (-0.5)
        return {'x': jax.random.normal(ks[0], (B, N, dim), dtype=jnp.float32), 'cond': jax.random.normal(ks[1], (B, condN, cond_dim), dtype=jnp.float32), 'q_w': s(ks[2], (dim, dim), dim), 'q_b': jnp.zeros((dim,), jnp.float32), 'kv_w': s(ks[3], (cond_dim, 2 * dim), cond_dim), 'kv_b': jnp.zeros((2 * dim,), jnp.float32), 'proj_w': s(ks[4], (dim, dim), dim), 'proj_b': jnp.zeros((dim,), jnp.float32)}
    _L1_xattn_all = _L1_xattn_setup()
    _L1_xattn_in = {k: v for k, v in _L1_xattn_all.items() if k in ('q_w', 'q_b', 'kv_w', 'kv_b', 'proj_w', 'proj_b')}
    del _L1_xattn_all

    def _L1_attn_setup():
        import jax, jax.numpy as jnp
        import numpy as np
        H = 16

        def _alibi_slopes(n):
            start = 2.0 ** (-2.0 ** (-(np.log2(n) - 3)))
            return np.array([start * start ** i for i in range(n)], dtype=np.float32)
        key = jax.random.key(seed)
        ks = jax.random.split(key, 6)
        B, L, C = (2, 256, 128)
        scale = 0.02
        return {'q': jax.random.normal(ks[0], (B, L, C), dtype=jnp.float32), 'Wq': jax.random.normal(ks[1], (C, C), dtype=jnp.float32) * scale, 'Wk': jax.random.normal(ks[2], (C, C), dtype=jnp.float32) * scale, 'Wv': jax.random.normal(ks[3], (C, C), dtype=jnp.float32) * scale, 'Wo': jax.random.normal(ks[4], (C, C), dtype=jnp.float32) * scale, 'bo': jax.random.normal(ks[5], (C,), dtype=jnp.float32) * scale}
    _L1_attn_all = _L1_attn_setup()
    _L1_attn_in = {k: v for k, v in _L1_attn_all.items() if k in ('Wq', 'Wk', 'Wv', 'Wo', 'bo')}
    del _L1_attn_all

    def _L1_ffn_setup():
        import jax, jax.numpy as jnp
        import numpy as np
        B, S, D = (4, 128, 128)
        I = 64
        E = 32
        TOP_K = 8
        N_GROUP = 8
        TOPK_GROUP = 4

        def _group_topk(scores):
            T = scores.shape[0]
            epg = E // N_GROUP
            group_scores = scores.reshape(T, N_GROUP, epg).sum(axis=-1)
            _, top_groups = jax.lax.top_k(group_scores, TOPK_GROUP)
            group_mask = jnp.zeros((T, N_GROUP), scores.dtype).at[jnp.arange(T)[:, None], top_groups].set(1.0)
            expert_mask = jnp.repeat(group_mask, epg, axis=1)
            masked_scores = scores * expert_mask
            topk_w, topk_i = jax.lax.top_k(masked_scores, TOP_K)
            return (topk_w, topk_i)

        def _reference_tuple_inner(hidden_states, gate_w, expert_gate, expert_up, expert_down, shared_gate_w, shared_up_w, shared_down_w):
            b, s, d = hidden_states.shape
            flat = hidden_states.reshape(-1, d)
            T = flat.shape[0]
            logits = flat @ gate_w.T
            scores = jax.nn.sigmoid(logits)
            topk_w, topk_i = _group_topk(scores)
            topk_w = topk_w / jnp.clip(topk_w.sum(axis=-1, keepdims=True), 1e-12)
            combine = jnp.zeros((T, E), flat.dtype).at[jnp.arange(T)[:, None], topk_i].add(topk_w)

            def body(acc, expert):
                wg, wu, wd, w = expert
                h = jax.nn.silu(flat @ wg.T) * (flat @ wu.T)
                return (acc + w[:, None] * (h @ wd.T), None)
            out, _ = jax.lax.scan(body, jnp.zeros_like(flat), (expert_gate, expert_up, expert_down, combine.T))
            shared = jax.nn.silu(flat @ shared_gate_w.T) * (flat @ shared_up_w.T) @ shared_down_w.T
            out = out + shared
            return (out.reshape(b, s, d), logits)
        key = jax.random.key(seed)
        ks = jax.random.split(key, 8)
        scale = 0.02
        return {'hidden_states': jax.random.normal(ks[0], (B, S, D), jnp.float32), 'gate_w': jax.random.normal(ks[1], (E, D), jnp.float32) * scale, 'expert_gate': jax.random.normal(ks[2], (E, I, D), jnp.float32) * scale, 'expert_up': jax.random.normal(ks[3], (E, I, D), jnp.float32) * scale, 'expert_down': jax.random.normal(ks[4], (E, D, I), jnp.float32) * scale, 'shared_gate_w': jax.random.normal(ks[5], (I, D), jnp.float32) * scale, 'shared_up_w': jax.random.normal(ks[6], (I, D), jnp.float32) * scale, 'shared_down_w': jax.random.normal(ks[7], (D, I), jnp.float32) * scale}
    _L1_ffn_all = _L1_ffn_setup()
    _L1_ffn_in = {k: v for k, v in _L1_ffn_all.items() if k in ('gate_w', 'expert_gate', 'expert_up', 'expert_down', 'shared_gate_w', 'shared_up_w', 'shared_down_w')}
    del _L1_ffn_all
    return {'x': x, 'ctx_768': ctx_768, 'L0_xattn_Wq': _L0_xattn_in['Wq'], 'L0_xattn_Wk': _L0_xattn_in['Wk'], 'L0_xattn_Wv': _L0_xattn_in['Wv'], 'L0_xattn_Wo': _L0_xattn_in['Wo'], 'L0_xattn_bo': _L0_xattn_in['bo'], 'L0_attn_Wq': _L0_attn_in['Wq'], 'L0_attn_Wk': _L0_attn_in['Wk'], 'L0_attn_Wv': _L0_attn_in['Wv'], 'L0_attn_Wo': _L0_attn_in['Wo'], 'L0_attn_proj': _L0_attn_in['proj'], 'L0_attn_W1': _L0_attn_in['W1'], 'L0_attn_b1': _L0_attn_in['b1'], 'L0_attn_W2': _L0_attn_in['W2'], 'L0_attn_b2': _L0_attn_in['b2'], 'L0_attn_ln1_g': _L0_attn_in['ln1_g'], 'L0_attn_ln1_b': _L0_attn_in['ln1_b'], 'L0_attn_ln2_g': _L0_attn_in['ln2_g'], 'L0_attn_ln2_b': _L0_attn_in['ln2_b'], 'L0_ffn_gate_w': _L0_ffn_in['gate_w'], 'L0_ffn_w1': _L0_ffn_in['w1'], 'L0_ffn_b1': _L0_ffn_in['b1'], 'L0_ffn_w2': _L0_ffn_in['w2'], 'L0_ffn_b2': _L0_ffn_in['b2'], 'L0_ffn_w3': _L0_ffn_in['w3'], 'L0_ffn_b3': _L0_ffn_in['b3'], 'L0_ffn_sw1': _L0_ffn_in['sw1'], 'L0_ffn_sw2': _L0_ffn_in['sw2'], 'L0_ffn_sw3': _L0_ffn_in['sw3'], 'L1_xattn_q_w': _L1_xattn_in['q_w'], 'L1_xattn_q_b': _L1_xattn_in['q_b'], 'L1_xattn_kv_w': _L1_xattn_in['kv_w'], 'L1_xattn_kv_b': _L1_xattn_in['kv_b'], 'L1_xattn_proj_w': _L1_xattn_in['proj_w'], 'L1_xattn_proj_b': _L1_xattn_in['proj_b'], 'L1_attn_Wq': _L1_attn_in['Wq'], 'L1_attn_Wk': _L1_attn_in['Wk'], 'L1_attn_Wv': _L1_attn_in['Wv'], 'L1_attn_Wo': _L1_attn_in['Wo'], 'L1_attn_bo': _L1_attn_in['bo'], 'L1_ffn_gate_w': _L1_ffn_in['gate_w'], 'L1_ffn_expert_gate': _L1_ffn_in['expert_gate'], 'L1_ffn_expert_up': _L1_ffn_in['expert_up'], 'L1_ffn_expert_down': _L1_ffn_in['expert_down'], 'L1_ffn_shared_gate_w': _L1_ffn_in['shared_gate_w'], 'L1_ffn_shared_up_w': _L1_ffn_in['shared_up_w'], 'L1_ffn_shared_down_w': _L1_ffn_in['shared_down_w']}

def reference(x, ctx_768, L0_xattn_Wq, L0_xattn_Wk, L0_xattn_Wv, L0_xattn_Wo, L0_xattn_bo, L0_attn_Wq, L0_attn_Wk, L0_attn_Wv, L0_attn_Wo, L0_attn_proj, L0_attn_W1, L0_attn_b1, L0_attn_W2, L0_attn_b2, L0_attn_ln1_g, L0_attn_ln1_b, L0_attn_ln2_g, L0_attn_ln2_b, L0_ffn_gate_w, L0_ffn_w1, L0_ffn_b1, L0_ffn_w2, L0_ffn_b2, L0_ffn_w3, L0_ffn_b3, L0_ffn_sw1, L0_ffn_sw2, L0_ffn_sw3, L1_xattn_q_w, L1_xattn_q_b, L1_xattn_kv_w, L1_xattn_kv_b, L1_xattn_proj_w, L1_xattn_proj_b, L1_attn_Wq, L1_attn_Wk, L1_attn_Wv, L1_attn_Wo, L1_attn_bo, L1_ffn_gate_w, L1_ffn_expert_gate, L1_ffn_expert_up, L1_ffn_expert_down, L1_ffn_shared_gate_w, L1_ffn_shared_up_w, L1_ffn_shared_down_w):
    import jax
    import jax.numpy as jnp

    def _L0_xattn_ref(x, context, Wq, Wk, Wv, Wo, bo):
        import jax, jax.numpy as jnp
        import numpy as np
        HEADS = 16
        DIM_HEAD = 64
        B, Nq, _ = x.shape
        Nk = context.shape[1]
        h, dh = (HEADS, DIM_HEAD)
        q = (x @ Wq).reshape(B, Nq, h, dh)
        k = (context @ Wk).reshape(B, Nk, h, dh)
        v = (context @ Wv).reshape(B, Nk, h, dh)
        scale = 1.0 / jnp.sqrt(jnp.asarray(dh, dtype=x.dtype))
        scores = jnp.einsum('bqhd,bkhd->bhqk', q, k) * scale
        attn = jax.nn.softmax(scores, axis=-1)
        out = jnp.einsum('bhqk,bkhd->bqhd', attn, v).reshape(B, Nq, h * dh)
        return out @ Wo + bo

    def _L0_attn_ref(x, Wq, Wk, Wv, Wo, proj, W1, b1, W2, b2, ln1_g, ln1_b, ln2_g, ln2_b):
        import jax, jax.numpy as jnp
        import numpy as np
        B, N, D = (4, 512, 128)
        H, DH = (16, 64)
        DFF = 512
        M = 64
        EPS_KERN = 1e-06
        EPS_LN = 1e-06

        def _softmax_kernel_feats(data, proj, is_query):
            dn = 1.0 / jnp.sqrt(jnp.sqrt(jnp.float32(data.shape[-1])))
            ratio = 1.0 / jnp.sqrt(jnp.float32(proj.shape[0]))
            data_dash = jnp.einsum('bnhd,md->bnhm', data * dn, proj)
            diag = jnp.sum(jnp.square(data), axis=-1, keepdims=True) * (dn * dn) / 2.0
            if is_query:
                mx = jnp.max(data_dash, axis=-1, keepdims=True)
            else:
                mx = jnp.max(data_dash)
            return ratio * (jnp.exp(data_dash - diag - mx) + EPS_KERN)

        def _layernorm(x, g, b):
            mu = jnp.mean(x, axis=-1, keepdims=True)
            var = jnp.mean(jnp.square(x - mu), axis=-1, keepdims=True)
            return (x - mu) * jax.lax.rsqrt(var + EPS_LN) * g + b

        def _encoder_forward(x, Wq, Wk, Wv, Wo, proj, W1, b1, W2, b2, ln1_g, ln1_b, ln2_g, ln2_b):
            q = jnp.einsum('bnd,dhk->bnhk', x, Wq)
            k = jnp.einsum('bnd,dhk->bnhk', x, Wk)
            v = jnp.einsum('bnd,dhk->bnhk', x, Wv)
            qf = _softmax_kernel_feats(q, proj, True)
            kf = _softmax_kernel_feats(k, proj, False)
            kv = jnp.einsum('bnhm,bnhd->bhmd', kf, v)
            num = jnp.einsum('bnhm,bhmd->bnhd', qf, kv)
            den = jnp.einsum('bnhm,bhm->bnh', qf, jnp.sum(kf, axis=1))
            attn = num / den[..., None]
            attn_out = jnp.einsum('bnhd,hdo->bno', attn, Wo)
            out1 = _layernorm(x + attn_out, ln1_g, ln1_b)
            h = jax.nn.elu(out1 @ W1 + b1)
            ffn_out = h @ W2 + b2
            return _layernorm(out1 + ffn_out, ln2_g, ln2_b)
        return _encoder_forward(x, Wq, Wk, Wv, Wo, proj, W1, b1, W2, b2, ln1_g, ln1_b, ln2_g, ln2_b)

    def _L0_ffn_ref(x, gate_w, w1, b1, w2, b2, w3, b3, sw1, sw2, sw3):
        import jax, jax.numpy as jnp
        import numpy as np
        D = 128
        H = 128
        E = 8
        K = 2
        I = 2 * 128
        ROUTE_SCALE = 1.0
        B, S, _ = x.shape
        xt = x.reshape(-1, D)
        logits = xt @ gate_w.T
        scores = jax.nn.softmax(logits.astype(jnp.float32), axis=-1)
        top_vals, idx = jax.lax.top_k(scores, K)
        weights = jnp.take_along_axis(scores, idx, axis=1).astype(x.dtype) * ROUTE_SCALE
        xs = xt[:, None, :] * weights[:, :, None]
        y = jnp.zeros_like(xt)
        for e in range(E):
            mask = (idx == e).astype(x.dtype)
            h = jax.nn.silu(jnp.einsum('tkd,hd->tkh', xs, w1[e]) + b1[e])
            x2 = jnp.einsum('tkh,dh->tkd', h, w2[e]) + b2[e]
            x3 = jnp.einsum('tkd,hd->tkh', xs, w3[e]) + b3[e]
            y = y + jnp.sum(x2 * x3 * mask[:, :, None], axis=1)
        z = jax.nn.silu(xt @ sw1.T) * (xt @ sw2.T) @ sw3.T
        return (y + z).reshape(B, S, D)

    def _L1_xattn_ref(x, cond, q_w, q_b, kv_w, kv_b, proj_w, proj_b):
        import jax, jax.numpy as jnp
        import numpy as np
        NUM_HEADS = 16
        B, N, C = x.shape
        condN = cond.shape[1]
        H = NUM_HEADS
        hd = C // H
        scale = hd ** (-0.5)
        q = (x @ q_w + q_b).reshape(B, N, H, hd).transpose(0, 2, 1, 3)
        kv = (cond @ kv_w + kv_b).reshape(B, condN, 2, H, hd)
        k = kv[:, :, 0].transpose(0, 2, 1, 3)
        v = kv[:, :, 1].transpose(0, 2, 1, 3)
        attn = jnp.einsum('bhnd,bhmd->bhnm', q * scale, k)
        attn = jax.nn.softmax(attn, axis=-1)
        out = jnp.einsum('bhnm,bhmd->bhnd', attn, v)
        out = out.transpose(0, 2, 1, 3).reshape(B, N, C)
        return out @ proj_w + proj_b

    def _L1_attn_ref(q, Wq, Wk, Wv, Wo, bo):
        import jax, jax.numpy as jnp
        import numpy as np
        H = 16

        def _alibi_slopes(n):
            start = 2.0 ** (-2.0 ** (-(np.log2(n) - 3)))
            return np.array([start * start ** i for i in range(n)], dtype=np.float32)
        B, L, C = q.shape
        D = C // H
        inv_sqrt_d = jnp.asarray(D, q.dtype) ** (-0.5)

        def proj(x, W):
            return (x @ W.T).reshape(B, L, H, D).transpose(0, 2, 1, 3)
        qh, kh, vh = (proj(q, Wq), proj(q, Wk), proj(q, Wv))
        pos = jnp.arange(L)
        rel = jnp.abs(pos[None, :] - pos[:, None]).astype(q.dtype)
        slopes = jnp.asarray(_alibi_slopes(H), dtype=q.dtype)
        bias = (-slopes)[:, None, None] * rel
        scores = jnp.einsum('bhld,bhsd->bhls', qh, kh) * inv_sqrt_d + bias[None]
        attn = jax.nn.softmax(scores, axis=-1)
        out = jnp.einsum('bhls,bhsd->bhld', attn, vh)
        out = out.transpose(0, 2, 1, 3).reshape(B, L, C)
        return out @ Wo.T + bo

    def _L1_ffn_ref(hidden_states, gate_w, expert_gate, expert_up, expert_down, shared_gate_w, shared_up_w, shared_down_w):
        import jax, jax.numpy as jnp
        import numpy as np
        B, S, D = (4, 128, 128)
        I = 64
        E = 32
        TOP_K = 8
        N_GROUP = 8
        TOPK_GROUP = 4

        def _group_topk(scores):
            T = scores.shape[0]
            epg = E // N_GROUP
            group_scores = scores.reshape(T, N_GROUP, epg).sum(axis=-1)
            _, top_groups = jax.lax.top_k(group_scores, TOPK_GROUP)
            group_mask = jnp.zeros((T, N_GROUP), scores.dtype).at[jnp.arange(T)[:, None], top_groups].set(1.0)
            expert_mask = jnp.repeat(group_mask, epg, axis=1)
            masked_scores = scores * expert_mask
            topk_w, topk_i = jax.lax.top_k(masked_scores, TOP_K)
            return (topk_w, topk_i)

        def _reference_tuple_inner(hidden_states, gate_w, expert_gate, expert_up, expert_down, shared_gate_w, shared_up_w, shared_down_w):
            b, s, d = hidden_states.shape
            flat = hidden_states.reshape(-1, d)
            T = flat.shape[0]
            logits = flat @ gate_w.T
            scores = jax.nn.sigmoid(logits)
            topk_w, topk_i = _group_topk(scores)
            topk_w = topk_w / jnp.clip(topk_w.sum(axis=-1, keepdims=True), 1e-12)
            combine = jnp.zeros((T, E), flat.dtype).at[jnp.arange(T)[:, None], topk_i].add(topk_w)

            def body(acc, expert):
                wg, wu, wd, w = expert
                h = jax.nn.silu(flat @ wg.T) * (flat @ wu.T)
                return (acc + w[:, None] * (h @ wd.T), None)
            out, _ = jax.lax.scan(body, jnp.zeros_like(flat), (expert_gate, expert_up, expert_down, combine.T))
            shared = jax.nn.silu(flat @ shared_gate_w.T) * (flat @ shared_up_w.T) @ shared_down_w.T
            out = out + shared
            return (out.reshape(b, s, d), logits)
        return _reference_tuple_inner(hidden_states, gate_w, expert_gate, expert_up, expert_down, shared_gate_w, shared_up_w, shared_down_w)[0]
    x = x + _L0_xattn_ref(_layernorm(x, axis=-1), ctx_768, L0_xattn_Wq, L0_xattn_Wk, L0_xattn_Wv, L0_xattn_Wo, L0_xattn_bo)
    x = x + _L0_attn_ref(_layernorm(x, axis=-1), L0_attn_Wq, L0_attn_Wk, L0_attn_Wv, L0_attn_Wo, L0_attn_proj, L0_attn_W1, L0_attn_b1, L0_attn_W2, L0_attn_b2, L0_attn_ln1_g, L0_attn_ln1_b, L0_attn_ln2_g, L0_attn_ln2_b)
    x = x + _L0_ffn_ref(_layernorm(x, axis=-1), L0_ffn_gate_w, L0_ffn_w1, L0_ffn_b1, L0_ffn_w2, L0_ffn_b2, L0_ffn_w3, L0_ffn_b3, L0_ffn_sw1, L0_ffn_sw2, L0_ffn_sw3)
    x = x + _L1_xattn_ref(_layernorm(x, axis=-1), ctx_768, L1_xattn_q_w, L1_xattn_q_b, L1_xattn_kv_w, L1_xattn_kv_b, L1_xattn_proj_w, L1_xattn_proj_b)
    x = x + _L1_attn_ref(_layernorm(x, axis=-1), L1_attn_Wq, L1_attn_Wk, L1_attn_Wv, L1_attn_Wo, L1_attn_bo)
    x = x + _L1_ffn_ref(_layernorm(x, axis=-1), L1_ffn_gate_w, L1_ffn_expert_gate, L1_ffn_expert_up, L1_ffn_expert_down, L1_ffn_shared_gate_w, L1_ffn_shared_up_w, L1_ffn_shared_down_w)
    return x

_drawn_inputs = setup_inputs


def setup_inputs(seed=0):
    import zlib

    import numpy as np

    out = dict(_drawn_inputs(seed))
    spreads = {'L0_attn_b1': (0.0, 0.44),
     'L0_attn_b2': (0.0, 0.1),
     'L0_attn_ln1_g': (1.0, 0.2),
     'L0_attn_ln1_b': (0.0, 0.1),
     'L0_attn_ln2_g': (1.0, 0.2),
     'L0_attn_ln2_b': (0.0, 0.1),
     'L1_xattn_q_b': (0.0, 0.728),
     'L1_xattn_kv_b': (0.0, 0.1),
     'L1_xattn_proj_b': (0.0, 0.1)}
    factors = {'L0_xattn_bo': 5.941,
     'L0_attn_Wq': 64.0,
     'L0_attn_Wk': 64.0,
     'L0_attn_proj': 64.0,
     'L0_ffn_b1': 8.0,
     'L0_ffn_b2': 8.0,
     'L0_ffn_b3': 8.0,
     'L1_attn_Wq': 8.0,
     'L1_attn_Wk': 8.0,
     'L1_attn_Wv': 4.811,
     'L1_attn_Wo': 4.857,
     'L1_attn_bo': 5.561,
     'L1_ffn_gate_w': 8.0,
     'L1_ffn_expert_gate': 8.0,
     'L1_ffn_expert_up': 8.0,
     'L1_ffn_expert_down': 8.0,
     'L1_ffn_shared_gate_w': 8.0,
     'L1_ffn_shared_up_w': 8.0,
     'L1_ffn_shared_down_w': 8.0}
    for name, (base, spread) in spreads.items():
        noise = np.random.default_rng([zlib.crc32(name.encode()), seed]).standard_normal(out[name].shape)
        drawn = base * np.exp(spread * noise) if base else spread * noise
        out[name] = jnp.asarray(drawn.astype(out[name].dtype))
    for name, factor in factors.items():
        out[name] = (out[name] * factor).astype(out[name].dtype)
    return out
```

```python
from contextlib import ExitStack

import numpy as np
import concourse.bass as bass
from concourse import mybir

F32 = mybir.dt.float32
ACT = mybir.ActivationFunctionType
ALU = mybir.AluOpType
AX = mybir.AxisListType

B, N, D = 128, 32, 128
P = 128
T = B * N // P
SEQ = P // N
C, CA = 96, 97
NK = 257
H = 16
HG = 4
DH0 = 64
DH1 = D // H
EPS_LN = 1e-5
EPS_ENC = 1e-6
EPS_KERN = 1e-6
FF = 512
E0, E1 = 8, 32
I1 = 64


def at(ap, t):
    return ap[:, bass.ds(t, 1), :].rearrange("p t n -> p (t n)")


class Chain:

    def __init__(self, eng, sem, per_tile):
        self.eng, self.sem, self.per, self.base, self.n = eng, sem, per_tile, 0, 0

    def tile(self, t):
        self.base, self.n = t * self.per, 0

    def done(self, ins):
        self.n += 1
        ins.then_inc(self.sem, 1)
        self.eng.wait_ge(self.sem, self.base + self.n)

    def end(self):
        assert self.n == self.per, (self.n, self.per)


class Core:

    def __init__(self, nc, ctx):
        self.nc = nc
        sb = lambda n, s: ctx.enter_context(nc.sbuf_tensor(n, s, F32))
        self.x = sb("x", [P, T, D])
        self.stats = sb("stats", [P, T, 6])
        self.mean = sb("mean", [P, T])
        self.half = sb("half", [P, 5, T])
        self.var_eps = sb("var_eps", [P, T])
        self.std = sb("std", [P, T])
        self.rstd = sb("rstd", [P, T])
        self.ident = sb("ident", [P, P])
        self.sems = []
        self.ps = ctx.enter_context(nc.psum_tensor("ps", [P, 8, 512], F32))

    def sem(self, name):
        self.sems.append(self.nc.alloc_semaphore(name))
        return self.sems[-1]

    def clear_sems(self):
        self.nc.clear_and_free_semaphores(self.sems)
        self.nc.all_engine_barrier()
        self.sems = []


def add_to_x_and_count(nc, k, chain, t, psum, bias, xs=None):
    xt = at(k.x, t)
    chain.done(nc.vector.tensor_tensor(xt, psum, xt, ALU.add))
    chain.done(nc.vector.tensor_tensor(xt, xt, bias, ALU.add))
    nc.vector.nop(nofuse=True)
    return nc.vector.bn_stats(at(k.stats, t), xt)


def stage_load(nc, k, x_dram, ident_dram):
    with ExitStack() as ctx:
        x_in = k.sem("x_in")
        id_in = k.sem("id_in")
        steps = k.sem("load_steps")
        block = ctx.enter_context(nc.Block())

        @block.sync
        def _(sp):
            sp.dma_start(k.x[:, :, :], x_dram.rearrange("(t p) d -> p t d", p=P)).then_inc(x_in, 16)
            sp.dma_start(k.ident[:, :], ident_dram).then_inc(id_in, 16)
            sp.wait_ge(id_in, 16)

        @block.vector
        def _(dve):
            dve.wait_ge(x_in, 16)
            with dve.Fori(0, T) as t:
                nc.vector.bn_stats(at(k.stats, t), at(k.x, t)).then_inc(steps, 1)
            dve.wait_ge(steps, T)


def rstd_dve(nc, k, dve, ln, eps):
    col = lambda n: k.stats[:, :, n:n + 1].rearrange("p t o -> p (t o)")
    h = k.half
    nc.vector.tensor_tensor(h[:, 0, :], col(1), col(4), ALU.add)
    nc.vector.tensor_tensor(h[:, 1, :], col(1), col(4), ALU.subtract)
    nc.vector.tensor_tensor(h[:, 2, :], col(2), col(5), ALU.add).then_inc(ln, 1)
    dve.wait_ge(ln, 1)
    nc.vector.tensor_scalar(k.mean[:, :], h[:, 0, :], 0.5, None, ALU.mult)
    nc.vector.tensor_tensor(h[:, 3, :], h[:, 1, :], h[:, 1, :], ALU.mult)
    nc.vector.tensor_scalar(h[:, 4, :], h[:, 2, :], 1.0 / D, eps, ALU.mult, ALU.add).then_inc(ln, 1)
    dve.wait_ge(ln, 2)
    nc.vector.scalar_tensor_tensor(k.var_eps[:, :], h[:, 3, :], 0.25, h[:, 4, :], ALU.mult, ALU.add).then_inc(ln, 1)
    dve.wait_ge(ln, 4)
    nc.vector.reciprocal(k.rstd[:, :], k.std[:, :]).then_inc(ln, 1)
    dve.wait_ge(ln, 5)


def rstd_act(nc, k, act, ln):
    act.wait_ge(ln, 3)
    nc.scalar.activation(k.std[:, :], k.var_eps[:, :], ACT.Sqrt).then_inc(ln, 1)


def normalise(nc, k, out, t):
    return nc.vector.tensor_scalar(out, at(k.x, t), k.mean[:, bass.ds(t, 1)], k.rstd[:, bass.ds(t, 1)],
                                   ALU.subtract, ALU.mult)


def stage_xattn(nc, k, name, w, ctx_t, ctx_k, ctx_x):
    first = name == "l0"
    with ExitStack() as ctx:
        sb = lambda n, s: ctx.enter_context(nc.sbuf_tensor(f"{name}_{n}", s, F32))
        sem = lambda n: k.sem(f"{name}_{n}")
        A = sb("A", [P, H, CA])
        U = sb("U", [CA, H, D])
        qbias = sb("qbias", [CA, H])
        bo = sb("bo", [P, D])
        w_in = sem("w_in")
        ps = k.ps

        with ExitStack() as prep:
            psb = lambda n, s: prep.enter_context(nc.sbuf_tensor(f"{name}_{n}", s, F32))
            psem = lambda n: k.sem(f"{name}_{n}")
            made = psem("made")
            moved = psem("moved")
            masked = psem("masked")
            if first:
                wqT, wkT = psb("wqT", [P, H // 2, D]), psb("wkT", [P, H // 2, CA])
                wvT, wo = psb("wvT", [P, H // 2, CA]), psb("wo", [P, H // 2, D])
                scale = DH0 ** -0.5
                loads = [(wqT, w["wqT"]), (wkT, w["wkT"]), (wvT, w["wvT"]), (wo, w["wo"])]
            else:
                wqT, kaT, vaT, wo = psb("wqT", [P, D]), psb("kaT", [P, CA]), psb("vaT", [P, CA]), psb("wo", [P, D])
                hm, qb = psb("hm", [P, H]), psb("qb", [P, 1])
                kam, vam, qbm = psb("kam", [P, H, CA]), psb("vam", [P, H, CA]), psb("qbm", [P, H])
                scale = DH1 ** -0.5
                loads = [(wqT, w["wqT"]), (kaT, w["kaT"]), (vaT, w["vaT"]), (wo, w["wo"]),
                         (hm, w["head_mask"]), (qb, w["qb"])]
            block = prep.enter_context(nc.Block())

            @block.sync
            def _(sp):
                for dst, src in loads + [(bo, w["bo"])]:
                    sp.dma_start(dst[:], src).then_inc(w_in, 16)
                sp.wait_ge(w_in, 16 * (len(loads) + 1))

            @block.vector
            def _(dve):
                if first:
                    nc.vector.memset(qbias[:, :], 0.0).then_inc(masked, 1)
                else:
                    dve.wait_ge(w_in, 16 * (len(loads) + 1))
                    for dst, src in ((kam, kaT), (vam, vaT)):
                        nc.vector.tensor_tensor(dst[:, :, :], src[:, None, :].to_broadcast([P, H, CA]),
                                                hm[:, :, None].to_broadcast([P, H, CA]),
                                                ALU.mult).then_inc(masked, 1)
                    nc.vector.tensor_scalar(qbm[:, :], hm[:, :], qb[:, 0:1], None, ALU.mult).then_inc(masked, 1)

            @block.tensor
            def _(pe):
                pe.wait_ge(w_in, 16 * (len(loads) + 1))
                if first:
                    for h in range(H):
                        c, r = h // 2, 64 * (h % 2)
                        bank = 2 * (h % 2) + c // 4
                        last = nc.tensor.matmul(ps[:, bank, (c % 4) * P:(c % 4) * P + CA], wqT[r:r + 64, c, :],
                                                wkT[r:r + 64, c, :], start=True, stop=True)
                    last.then_inc(made, 1)
                    for h in range(H):
                        c, r = h // 2, 64 * (h % 2)
                        bank = 4 + 2 * (h % 2) + c // 4
                        last = nc.tensor.matmul(ps[0:CA, bank, (c % 4) * P:(c % 4) * P + P], wvT[r:r + 64, c, :],
                                                wo[r:r + 64, c, :], start=True, stop=True)
                    last.then_inc(made, 1)
                else:
                    pe.wait_ge(masked, 3)
                    for g in range(4):
                        last = nc.tensor.matmul(ps[:, g, 0:HG * CA], wqT[:, :], kam[:, HG * g:HG * g + HG, :],
                                                start=True, stop=True)
                    last.then_inc(made, 1)
                    for h in range(H):
                        last = nc.tensor.matmul(ps[0:CA, 4 + h // 4, (h % 4) * P:(h % 4) * P + P], vam[:, h, :],
                                                wo[:, :], start=True, stop=True)
                    last.then_inc(made, 1)
                    pe.wait_ge(moved, 1)
                    nc.tensor.matmul(ps[0:CA, 0, 0:H], kaT[:, :], qbm[:, :], start=True, stop=True).then_inc(made, 1)

            @block.scalar
            def _(act):
                act.wait_ge(made, 1)
                if first:
                    for par in range(2):
                        for g in range(2):
                            nc.scalar.mul(A[:, 8 * g + par:8 * g + 8:2, :],
                                          ps[:, 2 * par + g, :].rearrange("p (c n) -> p c n", c=4)[:, :, 0:CA], scale)
                else:
                    for g in range(4):
                        last = nc.scalar.mul(A[:, HG * g:HG * g + HG, :], ps[:, g, 0:HG * CA].rearrange(
                            "p (c n) -> p c n", c=4), scale)
                    last.then_inc(moved, 1)
                act.wait_ge(made, 2)
                for par in range(2):
                    for g in range(2):
                        if first:
                            nc.scalar.copy(U[:, 8 * g + par:8 * g + 8:2, :],
                                           ps[0:CA, 4 + 2 * par + g, :].rearrange("p (c n) -> p c n", c=4))
                        else:
                            nc.scalar.copy(U[:, 4 * (2 * par + g):4 * (2 * par + g) + 4, :],
                                           ps[0:CA, 4 + 2 * par + g, :].rearrange("p (c n) -> p c n", c=4))
                if not first:
                    act.wait_ge(made, 3)
                    nc.scalar.mul(qbias[:, :], ps[0:CA, 0, 0:H], scale)

        ctxT = sb("ctxT", [CA, 2, SEQ * NK])
        ctxK = sb("ctxK", [P, 2, SEQ * 2 * CA])
        ctxX = sb("ctxX", [SEQ, 2, SEQ * CA])
        xn = sb("xn", [P, D])
        xnT = sb("xnT", [P, P])
        q1 = sb("q1", [CA, SEQ, HG * N])
        probs = sb("probs", [P, 2, SEQ, NK])
        nmax = sb("nmax", [P, 2, SEQ])
        den = sb("den", [P, 2, SEQ])
        rden = sb("rden", [P, 2, SEQ])
        pT = sb("pT", [P, 2, SEQ * P])
        pX = sb("pX", [SEQ, P])
        oT = sb("oT", [CA, H, SEQ, N])
        S_B, T_B, M_B, O_B = 0, 4, 6, 7

        ln, xn_ok, xt_mm, xt_sb = sem("ln"), sem("xn_ok"), sem("xt_mm"), sem("xt_sb")
        q_mm, q_sb, s_mm, nm_ok = sem("q_mm"), sem("q_sb"), sem("s_mm"), sem("nm_ok")
        exp_ok, rd_ok, norm_ok, t_mm = sem("exp_ok"), sem("rd_ok"), sem("norm_ok"), sem("t_mm")
        pt_a, pt_v, o_mm, o_sb = sem("pt_a"), sem("pt_v"), sem("o_mm"), sem("o_sb")
        out_mm, x_ok, steps = sem("out_mm"), sem("x_ok"), sem("steps")
        ctx_free = sem("ctx_free")
        ctx_in = [sem("ctx_in0"), sem("ctx_in1")]
        block = ctx.enter_context(nc.Block())

        @block.sync
        def _(sp):
            with sp.Fori(0, T // 2) as i:
                for j in range(2):
                    sp.wait_ge(ctx_free, 2 * i + j + 1)
                    sp.dma_start(ctxT[:, j, :], ctx_t[bass.ds(2 * i + j, 1), :, :].rearrange(
                        "t c n -> c (t n)")).then_inc(ctx_in[j], 16)
                    sp.dma_start(ctxK[:, j, :], ctx_k[bass.ds(2 * i + j, 1), :, :].rearrange(
                        "t c n -> c (t n)")).then_inc(ctx_in[j], 16)
                    sp.dma_start(ctxX[:, j, :], ctx_x[bass.ds(2 * i + j, 1), :, :].rearrange(
                        "t c n -> c (t n)")).then_inc(ctx_in[j], 16)

        def queries(pe, t, hg):
            for h in range(HG):
                last = nc.tensor.matmul(ps[0:CA, M_B, h * P:h * P + P], A[:, HG * hg + h, :], xnT[:, :],
                                        start=True, stop=True)
            last.then_inc(q_mm, 1)

        def scores(pe, j):
            for b in range(SEQ):
                last = nc.tensor.matmul(ps[:, S_B + b, 0:NK], q1[:, b, :], ctxT[:, j, b * NK:b * NK + NK],
                                        start=True, stop=True)
            last.then_inc(s_mm, 1)

        def pe_tile(pe, i, j, last_tile=False):
            t = 2 * i + j
            for hg in range(HG):
                u = 4 * t + hg
                nxt = hg < HG - 1 or not last_tile
                if nxt:
                    if hg == 0:
                        pe.wait_ge(x_ok, t + 1)
                    if hg == HG - 1:
                        pe.wait_ge(xt_sb, t + 2)
                    queries(pe, t, (hg + 1) % HG)
                    pe.wait_ge(q_sb, u + 2)
                pe.wait_ge(norm_ok, u + 1)
                for kt in range(2):
                    for b in range(SEQ):
                        nc.tensor.transpose(ps[:, T_B + kt, b * P:b * P + P],
                                            probs[:, hg % 2, b, kt * P:kt * P + P], k.ident[:, :])
                nc.tensor.transpose(ps[0:SEQ, M_B, 0:P], probs[:, hg % 2, :, NK - 1:NK].rearrange("p b o -> p (b o)"),
                                    k.ident[:, :]).then_inc(t_mm, 1)
                if nxt:
                    if hg == HG - 1:
                        pe.wait_ge(ctx_in[1 - j], 48 * (i + j) + 48)
                    scores(pe, j if hg < HG - 1 else 1 - j)
                pe.wait_ge(pt_a, u + 1)
                pe.wait_ge(pt_v, u + 1)
                pe.wait_ge(o_sb, u + 1)
                for b in range(SEQ):
                    out = ps[0:CA, O_B, b * P:b * P + P]
                    for kt in range(2):
                        at_k = (b * 2 + kt) * CA
                        nc.tensor.matmul(out, ctxK[:, j, at_k:at_k + CA], pT[:, kt, b * P:b * P + P],
                                         start=kt == 0, stop=False)
                    last = nc.tensor.matmul(out, ctxX[:, j, b * CA:b * CA + CA], pX[:, :], start=False, stop=True)
                last.then_inc(o_mm, 1)
                if hg == HG - 1:
                    pass
                if hg == HG - 2 and not last_tile:
                    pe.wait_ge(xn_ok, t + 2)
                    nc.tensor.transpose(ps[:, M_B, 0:P], xn[:, :], k.ident[:, :]).then_inc(xt_mm, 1)
            pe.wait_ge(o_sb, 4 * t + 5)
            for h in range(H):
                last = nc.tensor.matmul(ps[:, M_B, 0:D], oT[:, h, :, :].rearrange("c b n -> c (b n)"), U[:, h, :],
                                        start=h == 0, stop=h == H - 1)
            last.then_inc(out_mm, 1)

        @block.tensor
        def _(pe):
            pe.wait_ge(xn_ok, 1)
            nc.tensor.transpose(ps[:, M_B, 0:P], xn[:, :], k.ident[:, :]).then_inc(xt_mm, 1)
            pe.wait_ge(xt_sb, 1)
            queries(pe, 0, 0)
            pe.wait_ge(q_sb, 1)
            pe.wait_ge(ctx_in[0], 48)
            scores(pe, 0)
            with pe.Fori(0, T // 2 - 1) as i:
                pe_tile(pe, i, 0)
                pe_tile(pe, i, 1)
            pe_tile(pe, T // 2 - 1, 0)
            pe_tile(pe, T // 2 - 1, 1, last_tile=True)

        def dve_queries(dve, u, hg):
            dve.wait_ge(q_mm, u + 1)
            nc.vector.tensor_tensor(q1[:, :, :].rearrange("c b (h n) -> c h b n", h=HG),
                                    ps[0:CA, M_B, :].rearrange("c (h b n) -> c h b n", h=HG, b=SEQ),
                                    qbias[:, HG * hg:HG * hg + HG, None, None].to_broadcast([CA, HG, SEQ, N]),
                                    ALU.add).then_inc(q_sb, 1)

        def dve_max(dve, u, par):
            dve.wait_ge(s_mm, u + 1)
            nc.vector.tensor_reduce(nmax[:, par, :], ps[:, S_B:S_B + SEQ, 0:NK], AX.X, ALU.max,
                                    negate=True).then_inc(nm_ok, 1)

        def dve_tile(dve, chain, t, last_tile=False):
            chain.tile(t)
            for hg in range(HG):
                u = 4 * t + hg
                nxt = hg < HG - 1 or not last_tile
                if nxt:
                    dve_queries(dve, u + 1, (hg + 1) % HG)
                dve.wait_ge(exp_ok, 4 * u + 4)
                nc.vector.reciprocal(rden[:, hg % 2, :], den[:, hg % 2, :]).then_inc(rd_ok, 1)
                dve.wait_ge(t_mm, u + 1)
                nc.vector.tensor_copy(pX[:, :], ps[0:SEQ, M_B, 0:P])
                nc.vector.tensor_copy(pT[:, 1, :], ps[:, T_B + 1, :]).then_inc(pt_v, 1)
                if nxt:
                    dve_max(dve, u + 1, (hg + 1) % 2)
                if hg == 1 and not last_tile:
                    normalise(nc, k, xn[:, :], t + 1).then_inc(xn_ok, 1)
                dve.wait_ge(o_mm, u + 1)
                nc.vector.tensor_copy(oT[:, HG * hg:HG * hg + HG, :, :],
                                      ps[0:CA, O_B, :].rearrange("c (b h n) -> c h b n", b=SEQ, h=HG)).then_inc(o_sb, 1)
            dve.wait_ge(out_mm, t + 1)
            add_to_x_and_count(nc, k, chain, t, ps[:, M_B, 0:D], bo[:, :]).then_inc(x_ok, 1)
            chain.end()

        @block.vector
        def _(dve):
            dve.sem_inc(o_sb, 1)
            dve.sem_inc(x_ok, 1)
            rstd_dve(nc, k, dve, ln, EPS_LN)
            normalise(nc, k, xn[:, :], 0).then_inc(xn_ok, 1)
            dve_queries(dve, 0, 0)
            dve_max(dve, 0, 0)
            chain = Chain(dve, steps, 2)
            with dve.Fori(0, T - 1) as t:
                dve_tile(dve, chain, t)
            dve_tile(dve, chain, T - 1, last_tile=True)

        def exps(act, u, par):
            act.wait_ge(nm_ok, u + 1)
            for b in range(SEQ):
                nc.scalar.activation(probs[:, par, b, :], ps[:, S_B + b, 0:NK], ACT.Exp, bias=nmax[:, par, b:b + 1],
                                     accum_out=den[:, par, b:b + 1]).then_inc(exp_ok, 1)

        def act_tile(act, t, last_tile=False):
            for hg in range(HG):
                u = 4 * t + hg
                act.wait_ge(t_mm, u + 1)
                nc.scalar.copy(pT[:, 0, :], ps[:, T_B, :]).then_inc(pt_a, 1)
                if hg < HG - 1 or not last_tile:
                    exps(act, u + 1, (hg + 1) % 2)
                if hg == HG - 2 and not last_tile:
                    act.wait_ge(xt_mm, t + 2)
                    nc.scalar.copy(xnT[:, :], ps[:, M_B, 0:P]).then_inc(xt_sb, 1)

        @block.scalar
        def _(act):
            rstd_act(nc, k, act, ln)
            act.wait_ge(xt_mm, 1)
            nc.scalar.copy(xnT[:, :], ps[:, M_B, 0:P]).then_inc(xt_sb, 1)
            exps(act, 0, 0)
            with act.Fori(0, T - 1) as t:
                act_tile(act, t)
            act_tile(act, T - 1, last_tile=True)

        @block.gpsimd
        def _(pool):
            pool.sem_inc(ctx_free, 2)
            with pool.Fori(0, T) as t:
                for hg in range(HG):
                    pool.wait_ge(rd_ok, 4 * t + hg + 1)
                    pr = probs[:, hg % 2, :, :]
                    nc.gpsimd.tensor_tensor(pr, pr, rden[:, hg % 2, :, None].to_broadcast([P, SEQ, NK]),
                                            ALU.mult).then_inc(norm_ok, 1)
                pool.wait_ge(out_mm, t + 1)
                pool.sem_inc(ctx_free, 1)


def stage_performer(nc, k, w):
    HALF = 8 * DH0
    dn = float(DH0) ** -0.25
    with ExitStack() as ctx:
        sb = lambda n, s: ctx.enter_context(nc.sbuf_tensor(f"enc_{n}", s, F32))
        ps = k.ps
        res = sb("res", [P, T, D])
        negmx = sb("negmx", [P, 1])

        with ExitStack() as att:
            sb = lambda n, s: att.enter_context(nc.sbuf_tensor(f"enc_{n}", s, F32))
            sem = lambda n: k.sem(f"enc_{n}")
            wq, wk, wv = sb("wq", [P, H * DH0]), sb("wk", [P, H * DH0]), sb("wv", [P, H * DH0])
            pq, pk = sb("pq", [P, H * DH0]), sb("pk", [P, H * DH0])
            wo = sb("wo", [P, H // 2, D])
            blocks = sb("blocks", [P, P])
            mask = sb("mask", [P, P])
            ones = sb("ones", [1, P])

            with ExitStack() as prep:
                psb = lambda n, s: prep.enter_context(nc.sbuf_tensor(f"enc_{n}", s, F32))
                psem = lambda n: k.sem(f"enc_{n}")
                wqT, wkT, projT = psb("wqT", [P, H // 2, D]), psb("wkT", [P, H // 2, D]), psb("projT", [P, DH0])
                xn4 = psb("xn4", [P, 2, 4, D])
                xnT4 = psb("xnT4", [P, 2, 4 * P])
                tmp, acc = psb("tmp", [P, 2]), psb("acc", [P, 2])
                rowmax = psb("rowmax", [P, 1])
                allmax = psb("allmax", [1, 1])
                w_in, w_in2, made, moved, ln = psem("w_in"), psem("w_in2"), psem("made"), psem("moved"), psem("ln_a")
                xn_ok, xt_mm, xt_sb = psem("xn_ok_a"), psem("xt_mm_a"), psem("xt_sb_a")
                d_mm, max_ok, steps, fin = psem("d_mm"), psem("max_ok"), psem("steps_a"), psem("fin")
                block = prep.enter_context(nc.Block())
                loads = [(wqT, w["wqT"]), (wkT, w["wkT"]), (projT, w["projT"])]
                loads2 = [(wq, w["wq"]), (wk, w["wk"]), (wv, w["wv"]), (wo, w["wo"]), (blocks, w["blocks"]),
                          (mask, w["mask"])]

                @block.sync
                def _(sp):
                    for dst, src in loads:
                        sp.dma_start(dst[:], src).then_inc(w_in, 16)
                    for dst, src in loads2:
                        sp.dma_start(dst[:], src).then_inc(w_in2, 16)
                    sp.wait_ge(w_in2, 16 * len(loads2))

                @block.tensor
                def _(pe):
                    pe.wait_ge(w_in, 16 * len(loads))
                    for n, wT in ((0, wqT), (1, wkT)):
                        for h in range(H):
                            c, r = h // 2, 64 * (h % 2)
                            last = nc.tensor.matmul(ps[:, 2 * n + h % 2, c * DH0:c * DH0 + DH0], wT[r:r + 64, c, :],
                                                    projT[r:r + 64, :], start=True, stop=True)
                        last.then_inc(made, 1)
                    pe.wait_ge(moved, 2)
                    with pe.Fori(0, T // 8) as i:
                        for j in range(2):
                            g = 2 * i + j
                            pe.wait_ge(xn_ok, g + 1)
                            for n in range(4):
                                last = nc.tensor.transpose(ps[:, 4 + j, n * P:n * P + P], xn4[:, j, n, :], k.ident[:, :])
                            last.then_inc(xt_mm, 1)
                            pe.wait_ge(xt_sb, g + 1)
                            for s in range(4):
                                pe.wait_ge(max_ok, 4 * g + s + 1)
                                for c in range(2):
                                    last = nc.tensor.matmul(ps[:, 2 * (s % 2) + c, :],
                                                            pk[:, (2 * s + c) * P:(2 * s + c) * P + P], xnT4[:, j, :],
                                                            start=True, stop=True)
                                last.then_inc(d_mm, 1)
                    pe.wait_ge(fin, 1)
                    nc.tensor.transpose(ps[0:1, 6, 0:P], rowmax[:, :], k.ident[:, :]).then_inc(made, 1)
                    pe.wait_ge(fin, 2)
                    nc.tensor.matmul(ps[:, 7, 0:1], ones[:, :], allmax[:, :], start=True, stop=True).then_inc(made, 1)

                @block.vector
                def _(dve):
                    dve.sem_inc(max_ok, 2)
                    nc.vector.memset(ones[:, :], 1.0)
                    nc.vector.memset(acc[:, :], -3.0e38).then_inc(steps, 1)
                    dve.wait_ge(steps, 1)
                    rstd_dve(nc, k, dve, ln, EPS_LN)
                    
                    with dve.Fori(0, T // 8) as i:
                        for j in range(2):
                            g = 2 * i + j
                            for n in range(4):
                                last = normalise(nc, k, xn4[:, j, n, :], 4 * g + n)
                            last.then_inc(xn_ok, 1)
                            for s in range(4):
                                dve.wait_ge(d_mm, 4 * g + s + 1)
                                b = 2 * (s % 2)
                                nc.vector.tensor_reduce(tmp[:, :], ps[:, b:b + 2, :], AX.X, ALU.max).then_inc(max_ok, 1)
                                dve.wait_ge(max_ok, 4 * g + s + 3)
                                nc.vector.tensor_tensor(acc[:, :], acc[:, :], tmp[:, :], ALU.max).then_inc(steps, 1)
                                dve.wait_ge(steps, 4 * g + s + 2)
                    nc.vector.tensor_reduce(rowmax[:, :], acc[:, :], AX.X, ALU.max).then_inc(fin, 1)
                    dve.wait_ge(made, 3)
                    nc.vector.tensor_reduce(allmax[:, :], ps[0:1, 6, 0:P], AX.X, ALU.max, negate=True).then_inc(fin, 1)
                    dve.wait_ge(made, 4)
                    nc.vector.tensor_copy(negmx[:, :], ps[:, 7, 0:1])

                @block.scalar
                def _(act):
                    for n, dst in ((0, pq), (1, pk)):
                        act.wait_ge(made, n + 1)
                        for par in range(2):
                            last = nc.scalar.mul(dst[:, :].rearrange("p (c r m) -> p r c m", r=2, m=DH0)[:, par],
                                                 ps[:, 2 * n + par, :].rearrange("p (c m) -> p c m", m=DH0), dn)
                        last.then_inc(moved, 1)
                    rstd_act(nc, k, act, ln)
                    with act.Fori(0, T // 8) as i:
                        for j in range(2):
                            act.wait_ge(xt_mm, 2 * i + j + 1)
                            nc.scalar.copy(xnT4[:, j, :], ps[:, 4 + j, :]).then_inc(xt_sb, 1)

            xn, xr = sb("xn", [P, D]), sb("xr", [P, D])
            xnT = sb("xnT", [P, P])
            ksq, qsq = sb("ksq", [P, 1024]), sb("qsq", [P, 1024])
            eq, kf = sb("eq", [P, 1024]), sb("kf", [P, 1024])
            qfT = sb("qfT", [P, 1024])
            va = sb("va", [P, H, DH0 + 1])
            sm = sb("sm", [P, 4, 512])
            at_sb, atT = sb("at", [P, 1024]), sb("atT", [P, 1024])
            diag, mx, cc = sb("diag", [P, H]), sb("mx", [P, H]), sb("cc", [P, H])
            rden = sb("rden", [P, H])
            eps_col, eps_ok = sb("eps_col", [P, 1]), sem("eps_ok")
            FA, FB, RA, RB = 0, 2, 4, 6
            (xn_ok, xt_mm, xt_sb, k_mm, ksq_ok, q_mm, qsq_ok, dq_mm, sub_ok, eq_ok, dk_mm, kf_raw, kf_ok, v_mm, v_ok,
             qt_mm, qt_ok, s_mm, sm_ok, o_mm, at_ok, at_mm, atT_ok, wo_mm, res_ok, xr_ok, steps, steps_d) = [sem(n) for n in (
                 "xn_ok xt_mm xt_sb k_mm ksq_ok q_mm qsq_ok dq_mm sub_ok eq_ok dk_mm kf_raw kf_ok v_mm v_ok "
                 "qt_mm qt_ok s_mm sm_ok o_mm at_ok at_mm atT_ok wo_mm res_ok xr_ok steps steps_d").split()]
            block = att.enter_context(nc.Block())
            both = lambda pair: ps[:, pair:pair + 2, :].rearrange("p a b -> p (a b)")

            def feature_major(pair, wt, sem):
                for c in range(8):
                    last = nc.tensor.matmul(ps[:, pair + c // 4, (c % 4) * P:(c % 4) * P + P], wt[:, c * P:c * P + P],
                                            xnT[:, :], start=True, stop=True)
                last.then_inc(sem, 1)

            def token_major(pair, wt, sem):
                for c in range(2):
                    last = nc.tensor.matmul(ps[:, pair + c, :], xnT[:, :], wt[:, c * 512:c * 512 + 512],
                                            start=True, stop=True)
                last.then_inc(sem, 1)

            def pe_front(pe, t, part):
                if part == 0:
                    pe.wait_ge(xt_sb, t + 1)
                    feature_major(FA, wk, k_mm)
                elif part == 1:
                    token_major(FB, wq, q_mm)
                elif part == 2:
                    pe.wait_ge(ksq_ok, t + 1)
                    token_major(FA, pq, dq_mm)
                elif part == 3:
                    pe.wait_ge(qsq_ok, t + 1)
                    for c in range(8):
                        out = ps[:, FB + c // 4, (c % 4) * P:(c % 4) * P + P]
                        nc.tensor.matmul(out, pk[:, c * P:c * P + P], xnT[:, :], start=True, stop=False)
                        last = nc.tensor.matmul(out, blocks[:, :], ksq[:, c * P:c * P + P], start=False, stop=True)
                    last.then_inc(dk_mm, 1)
                else:
                    pe.wait_ge(sub_ok, t + 1)
                    token_major(FA, wv, v_mm)

            def pe_rear(pe, t, part, nxt=True):
                if part == 0:
                    pe.wait_ge(eq_ok, t + 1)
                    for c in range(8):
                        last = nc.tensor.transpose(ps[:, RA + c // 4, (c % 4) * P:(c % 4) * P + P],
                                                   eq[:, c * P:c * P + P], k.ident[:, :])
                    last.then_inc(qt_mm, 1)
                elif part in (1, 2):
                    if part == 1:
                        pe.wait_ge(kf_ok, t + 1)
                        pe.wait_ge(qt_ok, t + 1)
                    base = RB if part == 1 else RA
                    for n in range(4):
                        for par in range(2):
                            c, r = 4 * (part - 1) + n, 64 * par
                            last = nc.tensor.matmul(ps[:, base + par, n * P:n * P + P], kf[r:r + 64, c * P:c * P + P],
                                                    qfT[r:r + 64, c * P:c * P + P], start=True, stop=True)
                    last.then_inc(s_mm, 1)
                elif part == 3:
                    pe.wait_ge(v_ok, t + 1)
                    for half in range(2):
                        pe.wait_ge(sm_ok, 2 * t + half + 1)
                        if half:
                            pe.wait_ge(sm_ok, 2 * t + 2)
                        base = (RB, RA)[half]
                        for n in range(4):
                            for par in range(2):
                                h = 8 * half + 2 * n + par
                                last = nc.tensor.matmul(ps[:, base + par, n * 65:n * 65 + 65],
                                                        sm[:, 2 * half + par, n * P:n * P + P], va[:, h, :],
                                                        start=True, stop=True)
                        last.then_inc(o_mm, 1)
                elif part == 4:
                    pe.wait_ge(at_ok, 2 * t + 2)
                    for c in range(8):
                        last = nc.tensor.transpose(ps[:, RB + c // 4, (c % 4) * P:(c % 4) * P + P],
                                                   at_sb[:, c * P:c * P + P], k.ident[:, :])
                    last.then_inc(at_mm, 1)
                else:
                    pe.wait_ge(atT_ok, t + 1)
                    for c in range(8):
                        last = nc.tensor.matmul(ps[:, RA, 0:D], atT[:, c * P:c * P + P], wo[:, c, :],
                                                start=c == 0, stop=c == 7)
                    last.then_inc(wo_mm, 1)

            def pe_next_xT(pe, t):
                pe.wait_ge(xn_ok, t + 1)
                nc.tensor.transpose(ps[:, RA + 1, 0:P], xn[:, :], k.ident[:, :]).then_inc(xt_mm, 1)

            @block.tensor
            def _(pe):
                pe_next_xT(pe, 0)
                for part in range(5):
                    pe_front(pe, 0, part)
                pe_next_xT(pe, 1)

                def step(t, front=True, x_after=True):
                    if front:
                        pe.wait_ge(xt_sb, t + 2)
                    pe.wait_ge(res_ok, t + 1)
                    for part in range(5):
                        pe_rear(pe, t, part)
                        if front:
                            if part == 0:
                                pe.wait_ge(v_ok, t + 1)
                            if part == 1:
                                pe.wait_ge(kf_raw, t + 1)
                            pe_front(pe, t + 1, part)
                    pe_rear(pe, t, 5)
                    if x_after:
                        pe_next_xT(pe, t + 2)

                with pe.Fori(0, T - 2) as t:
                    step(t)
                step(T - 2, x_after=False)
                step(T - 1, front=False, x_after=False)

            @block.scalar
            def _(act):
                def front(t, part):
                    if part == 0:
                        act.wait_ge(k_mm, t + 1)
                        nc.scalar.activation(ksq[:, :], both(FA), ACT.Square).then_inc(ksq_ok, 1)
                    elif part == 1:
                        act.wait_ge(q_mm, t + 1)
                        nc.scalar.activation(qsq[:, :], both(FB), ACT.Square).then_inc(qsq_ok, 1)
                    elif part == 2:
                        act.wait_ge(sub_ok, t + 1)
                        nc.scalar.activation(eq[:, :], eq[:, :], ACT.Exp).then_inc(eq_ok, 1)
                    elif part == 3:
                        act.wait_ge(dk_mm, t + 1)
                        nc.scalar.activation(kf[:, :], both(FB), ACT.Exp, bias=negmx[:, 0:1]).then_inc(kf_raw, 1)
                    else:
                        act.wait_ge(v_mm, t + 1)
                        nc.scalar.copy(va[:, :, 0:DH0], both(FA).rearrange("p (h d) -> p h d", h=H)).then_inc(v_ok, 1)

                def x_next(t):
                    act.wait_ge(xt_mm, t + 1)
                    nc.scalar.copy(xnT[:, :], ps[:, RA + 1, 0:P]).then_inc(xt_sb, 1)

                def step(t, fr=True, x_after=True):
                    act.wait_ge(qt_mm, t + 1)
                    nc.scalar.activation(qfT[:, :], both(RA), ACT.Copy, bias=EPS_KERN).then_inc(qt_ok, 1)
                    if fr:
                        for part in range(5):
                            front(t + 1, part)
                    act.wait_ge(at_mm, t + 1)
                    nc.scalar.copy(atT[:, :], both(RB)).then_inc(atT_ok, 1)
                    if x_after:
                        x_next(t + 2)

                x_next(0)
                for part in range(5):
                    front(0, part)
                x_next(1)
                with act.Fori(0, T - 2) as t:
                    step(t)
                step(T - 2, x_after=False)
                step(T - 1, fr=False, x_after=False)

            @block.vector
            def _(dve):
                nc.vector.memset(va[:, :, DH0:DH0 + 1], 1.0)
                dve.sem_inc(res_ok, 1)
                q_steps, d_steps = Chain(dve, steps, 2), Chain(dve, steps_d, 2)
                heads = lambda ap: ap.rearrange("p (h d) -> p h d", h=H)

                def x_norm(t):
                    normalise(nc, k, xn[:, :], t).then_inc(xn_ok, 1)

                def front_q(t):
                    q_steps.tile(t)
                    dve.wait_ge(qsq_ok, t + 1)
                    nc.vector.tensor_reduce(diag[:, :], heads(qsq[:, :]), AX.X, ALU.add)
                    dve.wait_ge(dq_mm, t + 1)
                    q_steps.done(nc.vector.tensor_reduce(mx[:, :], heads(both(FA)), AX.X, ALU.max))
                    q_steps.done(nc.vector.scalar_tensor_tensor(cc[:, :], diag[:, :], dn * dn / 2, mx[:, :],
                                                                ALU.mult, ALU.add))
                    nc.vector.tensor_tensor(heads(eq[:, :]), heads(both(FA)),
                                            cc[:, :, None].to_broadcast([P, H, DH0]), ALU.subtract).then_inc(sub_ok, 1)

                def mask_s(t, half):
                    dve.wait_ge(s_mm, 2 * t + half + 1)
                    pair = (RB, RA)[half]
                    nc.vector.tensor_tensor(sm[:, 2 * half:2 * half + 2, :].rearrange("p a (n q) -> p (a n) q", q=P),
                                            ps[:, pair:pair + 2, :].rearrange("p a (n q) -> p (a n) q", q=P),
                                            mask[:, None, :].to_broadcast([P, 8, P]), ALU.mult).then_inc(sm_ok, 1)

                def divide(t, half):
                    dve.wait_ge(o_mm, 2 * t + half + 1)
                    pair = (RB, RA)[half]
                    for par in range(2):
                        src = ps[:, pair + par, 0:260].rearrange("p (n e) -> p n e", e=65)
                        rd = rden[:, 8 * half + 4 * par:8 * half + 4 * par + 4]
                        nc.vector.reciprocal(rd[:, :, None], src[:, :, 64:65]).then_inc(steps_d, 1)
                    dve.wait_ge(steps_d, 4 * t + 2 * half + 2)
                    for par in range(2):
                        src = ps[:, pair + par, 0:260].rearrange("p (n e) -> p n e", e=65)
                        rd = rden[:, 8 * half + 4 * par:8 * half + 4 * par + 4]
                        last = nc.vector.tensor_tensor(at_sb[:, 512 * half:512 * half + 512].rearrange(
                            "p (n r d) -> p r n d", r=2, d=DH0)[:, par], src[:, :, 0:64],
                            rd[:, :, None].to_broadcast([P, 4, DH0]), ALU.mult)
                    last.then_inc(at_ok, 1)

                def residual(t):
                    normalise(nc, k, xr[:, :], t).then_inc(xr_ok, 1)
                    dve.wait_ge(xr_ok, t + 1)
                    dve.wait_ge(wo_mm, t + 1)
                    nc.vector.tensor_tensor(at(res, t), ps[:, RA, 0:D], xr[:, :], ALU.add).then_inc(res_ok, 1)
                    dve.wait_ge(res_ok, t + 2)
                    nc.vector.nop(nofuse=True)
                    nc.vector.bn_stats(at(k.stats, t), at(res, t))

                def step(t, fr=True, x_after=True):
                    mask_s(t, 0)
                    mask_s(t, 1)
                    if fr:
                        front_q(t + 1)
                    if x_after:
                        dve.wait_ge(xt_mm, t + 2)
                        x_norm(t + 2)
                    divide(t, 0)
                    divide(t, 1)
                    residual(t)

                x_norm(0)
                front_q(0)
                dve.wait_ge(xt_mm, 1)
                x_norm(1)
                with dve.Fori(0, T - 2) as t:
                    step(t)
                step(T - 2, x_after=False)
                step(T - 1, fr=False, x_after=False)

            @block.gpsimd
            def _(pool):
                nc.gpsimd.memset(eps_col[:, :], EPS_KERN).then_inc(eps_ok, 1)
                pool.wait_ge(eps_ok, 1)
                with pool.Fori(0, T) as t:
                    pool.wait_ge(kf_raw, t + 1)
                    nc.gpsimd.tensor_tensor(kf[:, :], kf[:, :], eps_col[:, 0:1].to_broadcast([P, 1024]),
                                            ALU.add).then_inc(kf_ok, 1)

        with ExitStack() as net:
            sb = lambda n, s: net.enter_context(nc.sbuf_tensor(f"net_{n}", s, F32))
            sem = lambda n: k.sem(f"net_{n}")
            NF = FF // P
            w1, w2, b1 = sb("w1", [P, FF]), sb("w2", [P, NF, D]), sb("b1", [P, NF])
            rows = sb("rows", [P, 5, D])
            out1 = sb("out1", [P, 2, D])
            raw = sb("raw", [P, D])
            o1T = sb("o1T", [P, 2, P])
            z, zm, ez, hT = sb("z", [P, FF]), sb("zm", [P, FF]), sb("ez", [P, FF]), sb("hT", [P, 2, FF])
            w_in, ln, n1, n2, o1_ok = sem("w_in"), sem("ln"), sem("n1"), sem("n2"), sem("o1_ok")
            tr_mm, tr_ok, h_mm, z_ok, zm_ok, e_ok, h_ok, y_mm, y_ok, y2 = [sem(n) for n in (
                "tr_mm tr_ok h_mm z_ok zm_ok e_ok h_ok y_mm y_ok y2").split()]
            block = net.enter_context(nc.Block())
            loads = [(w1, w["w1"]), (w2, w["w2"]), (b1, w["b1"]), (rows, w["rows"])]

            @block.sync
            def _(sp):
                for dst, src in loads:
                    sp.dma_start(dst[:], src).then_inc(w_in, 16)
                sp.wait_ge(w_in, 16 * len(loads))

            @block.tensor
            def _(pe):
                pe.wait_ge(w_in, 16 * len(loads))

                def turn(j, t):
                    pe.wait_ge(o1_ok, t + 1)
                    nc.tensor.transpose(ps[:, j, 0:P], out1[:, j, :], k.ident[:, :]).then_inc(tr_mm, 1)

                def up(j, t):
                    pe.wait_ge(tr_ok, t + 1)
                    for c in range(NF):
                        last = nc.tensor.matmul(ps[:, 2 + j, c * P:c * P + P], w1[:, c * P:c * P + P], o1T[:, j, :],
                                                start=True, stop=True)
                    last.then_inc(h_mm, 1)

                def down(j, t):
                    pe.wait_ge(h_ok, t + 1)
                    for c in range(NF):
                        last = nc.tensor.matmul(ps[:, 4 + j, 0:D], hT[:, j, c * P:c * P + P], w2[:, c, :],
                                                start=c == 0, stop=c == NF - 1)
                    last.then_inc(y_mm, 1)

                turn(0, 0)
                up(0, 0)
                turn(1, 1)
                with pe.Fori(0, T // 2 - 1) as i:
                    for j in range(2):
                        up(1 - j, 2 * i + j + 1)
                        down(j, 2 * i + j)
                        turn(j, 2 * i + j + 2)
                up(1, T - 1)
                down(0, T - 2)
                down(1, T - 1)

            @block.vector
            def _(dve):
                dve.wait_ge(w_in, 16 * len(loads))
                rstd_dve(nc, k, dve, ln, EPS_ENC)

                def pre(j, t):
                    dve.wait_ge(n2, t + 1)
                    nc.vector.tensor_scalar(raw[:, :], at(res, t), k.mean[:, bass.ds(t, 1)], k.rstd[:, bass.ds(t, 1)],
                                            ALU.subtract, ALU.mult).then_inc(n1, 1)

                def mid(j, t):
                    dve.wait_ge(h_mm, t + 1)
                    nc.vector.tensor_tensor(z[:, :].rearrange("p (c q) -> p c q", c=NF),
                                            ps[:, 2 + j, :].rearrange("p (c q) -> p c q", c=NF),
                                            b1[:, :, None].to_broadcast([P, NF, P]), ALU.add).then_inc(z_ok, 1)
                    dve.wait_ge(z_ok, t + 1)
                    nc.vector.tensor_scalar(zm[:, :], z[:, :], 0.0, None, ALU.min).then_inc(zm_ok, 1)
                    nc.vector.tensor_scalar(hT[:, j, :], z[:, :], 0.0, -1.0, ALU.max, ALU.add).then_inc(y2, 1)
                    dve.wait_ge(e_ok, t + 1)
                    dve.wait_ge(y2, t + 1)
                    nc.vector.tensor_tensor(hT[:, j, :], hT[:, j, :], ez[:, :], ALU.add).then_inc(h_ok, 1)

                def post(j, t):
                    dve.wait_ge(y_mm, t + 1)
                    nc.vector.tensor_tensor(at(res, t), ps[:, 4 + j, 0:D], out1[:, j, :], ALU.add).then_inc(y_ok, 1)
                    dve.wait_ge(y_ok, 2 * t + 1)
                    nc.vector.tensor_tensor(at(res, t), at(res, t), rows[:, 2, :], ALU.add).then_inc(y_ok, 1)
                    dve.wait_ge(y_ok, 2 * t + 2)
                    nc.vector.nop(nofuse=True)
                    nc.vector.bn_stats(at(k.stats, t), at(res, t))

                pre(0, 0)
                pre(1, 1)
                mid(0, 0)
                with dve.Fori(0, T // 2 - 1) as i:
                    for j in range(2):
                        mid(1 - j, 2 * i + j + 1)
                        post(j, 2 * i + j)
                        pre(j, 2 * i + j + 2)
                mid(1, T - 1)
                post(0, T - 2)
                post(1, T - 1)

            @block.scalar
            def _(act):
                rstd_act(nc, k, act, ln)

                def turn(j, t):
                    act.wait_ge(tr_mm, t + 1)
                    nc.scalar.copy(o1T[:, j, :], ps[:, j, 0:P]).then_inc(tr_ok, 1)

                def expo(t):
                    act.wait_ge(zm_ok, t + 1)
                    nc.scalar.activation(ez[:, :], zm[:, :], ACT.Exp).then_inc(e_ok, 1)

                turn(0, 0)
                turn(1, 1)
                expo(0)
                with act.Fori(0, T // 2 - 1) as i:
                    for j in range(2):
                        expo(2 * i + j + 1)
                        turn(j, 2 * i + j + 2)
                expo(T - 1)

            @block.gpsimd
            def _(pool):
                pool.sem_inc(n2, 1)
                pool.wait_ge(w_in, 16 * len(loads))

                def gain(j, t):
                    pool.wait_ge(n1, t + 1)
                    nc.gpsimd.tensor_tensor(out1[:, j, :], raw[:, :], rows[:, 0, :], ALU.mult).then_inc(n2, 1)
                    pool.wait_ge(n2, t + 2)
                    nc.gpsimd.tensor_tensor(out1[:, j, :], out1[:, j, :], rows[:, 1, :], ALU.add).then_inc(o1_ok, 1)

                gain(0, 0)
                gain(1, 1)
                with pool.Fori(0, T // 2 - 1) as i:
                    for j in range(2):
                        pool.wait_ge(y_ok, 4 * i + 2 * j + 1)
                        gain(j, 2 * i + j + 2)

        with ExitStack() as end:
            sem = lambda n: k.sem(f"fin_{n}")
            rows = end.enter_context(nc.sbuf_tensor("fin_rows", [P, 5, D], F32))
            w_in, ln, sub, mul, gained, st = sem("w_in"), sem("ln"), sem("sub"), sem("mul"), sem("gained"), sem("st")
            block = end.enter_context(nc.Block())
            PARTS = 4
            TP = T // PARTS

            @block.sync
            def _(sp):
                sp.dma_start(rows[:, :, :], w["rows"]).then_inc(w_in, 16)
                sp.wait_ge(w_in, 16)

            @block.scalar
            def _(act):
                rstd_act(nc, k, act, ln)

            @block.gpsimd
            def _(pool):
                pool.wait_ge(w_in, 16)
                for n in range(PARTS):
                    r = res[:, n * TP:n * TP + TP, :]
                    pool.wait_ge(mul, n + 1)
                    nc.gpsimd.tensor_tensor(r, r, rows[:, 3:4, :].to_broadcast([P, TP, D]), ALU.mult).then_inc(gained, 1)

            @block.vector
            def _(dve):
                rstd_dve(nc, k, dve, ln, EPS_ENC)
                dve.wait_ge(w_in, 16)

                def first(n):
                    s = slice(n * TP, n * TP + TP)
                    nc.vector.tensor_tensor(res[:, s, :], res[:, s, :], k.mean[:, s, None].to_broadcast([P, TP, D]),
                                            ALU.subtract).then_inc(sub, 1)
                    dve.wait_ge(sub, n + 1)
                    nc.vector.tensor_tensor(res[:, s, :], res[:, s, :], k.rstd[:, s, None].to_broadcast([P, TP, D]),
                                            ALU.mult).then_inc(mul, 1)
                    nc.vector.tensor_tensor(k.x[:, s, :], k.x[:, s, :], rows[:, 4:5, :].to_broadcast([P, TP, D]),
                                            ALU.add).then_inc(st, 1)

                def second(n):
                    s = slice(n * TP, n * TP + TP)
                    dve.wait_ge(gained, n + 1)
                    dve.wait_ge(st, 2 * n + 2 if n < PARTS - 1 else 2 * n + 1)
                    nc.vector.tensor_tensor(k.x[:, s, :], k.x[:, s, :], res[:, s, :], ALU.add).then_inc(st, 1)

                first(0)
                for n in range(PARTS):
                    if n < PARTS - 1:
                        first(n + 1)
                    second(n)
                dve.wait_ge(st, 2 * PARTS)
                with dve.Fori(0, T) as t:
                    nc.vector.bn_stats(at(k.stats, t), at(k.x, t))


def ranked_mask(nc, dve, count, s, gt, eq, lower, mask, n, keep, base):
    shape = [P, T, n, n]
    mine, other = s[:, :, :, None].to_broadcast(shape), s[:, :, None, :].to_broadcast(shape)
    nc.vector.tensor_tensor(gt, other, mine, ALU.is_gt)
    nc.vector.tensor_tensor(eq, other, mine, ALU.is_equal).then_inc(count, 1)
    dve.wait_ge(count, base + 1)
    nc.vector.tensor_tensor(eq, eq, lower[:, None, :, :].to_broadcast(shape), ALU.mult).then_inc(count, 1)
    dve.wait_ge(count, base + 2)
    nc.vector.tensor_tensor(gt, gt, eq, ALU.add).then_inc(count, 1)
    dve.wait_ge(count, base + 3)
    nc.vector.tensor_reduce(mask, gt, AX.X, ALU.add).then_inc(count, 1)
    dve.wait_ge(count, base + 4)
    nc.vector.tensor_scalar(mask, mask, float(keep), None, ALU.is_lt).then_inc(count, 1)
    dve.wait_ge(count, base + 5)


def router_logits(nc, k, ctx, name, gate, gate_in, n_experts, logits, sb, sem):
    xn, xnT = sb("xn_r", [P, 2, D]), sb("xnT_r", [P, 2, P])
    xn_ok, xt_mm, xt_sb, lg_mm = sem("xn_ok_r"), sem("xt_mm_r"), sem("xt_sb_r"), sem("lg_mm")
    ps = k.ps

    def tensor(pe):
        pe.sem_inc(xt_mm, 2)
        pe.sem_inc(lg_mm, 2)
        with pe.Fori(0, T // 2) as i:
            for j in range(2):
                pe.wait_ge(xn_ok, 2 * i + j + 1)
                nc.tensor.transpose(ps[:, j, 0:P], xn[:, j, :], k.ident[:, :]).then_inc(xt_mm, 1)
            for j in range(2):
                pe.wait_ge(xt_sb, 2 * i + j + 1)
                nc.tensor.matmul(logits[:, bass.ds((2 * i + j) * n_experts, n_experts)], xnT[:, j, :], gate,
                                 start=True, stop=True).then_inc(lg_mm, 1)

    def vector(dve):
        with dve.Fori(0, T // 2) as i:
            for j in range(2):
                dve.wait_ge(xt_mm, 2 * i + j + 1)
                normalise(nc, k, xn[:, j, :], 2 * i + j).then_inc(xn_ok, 1)

    def scalar(act):
        with act.Fori(0, T // 2) as i:
            for j in range(2):
                act.wait_ge(xt_mm, 2 * i + j + 3)
                act.wait_ge(lg_mm, 2 * i + j + 1)
                nc.scalar.copy(xnT[:, j, :], ps[:, j, 0:P]).then_inc(xt_sb, 1)

    return tensor, vector, scalar, lg_mm


def stage_moe0(nc, k, w):
    ED = E0 * D
    with ExitStack() as ctx:
        sb = lambda n, s: ctx.enter_context(nc.sbuf_tensor(f"m0_{n}", s, F32))
        ps = k.ps
        score, mask = sb("score", [P, T, E0]), sb("mask", [P, T, E0])
        gain = sb("gain", [P, T, E0])
        w1, w2, w3 = sb("w1", [P, ED]), sb("w2", [P, ED]), sb("w3", [P, ED])
        b1, b2, b3 = sb("b1", [P, ED]), sb("b2", [P, ED]), sb("b3", [P, ED])
        sw12, sw3 = sb("sw12", [P, 4 * P]), sb("sw3", [P, 2, D])
        loads = [(w1, w["w1"]), (w2, w["w2"]), (w3, w["w3"]), (b1, w["b1"]), (b2, w["b2"]), (b3, w["b3"]),
                 (sw12, w["sw12"]), (sw3, w["sw3"])]

        with ExitStack() as r:
            rsb = lambda n, s: r.enter_context(nc.sbuf_tensor(f"m0_{n}", s, F32))
            rsem = lambda n: k.sem(f"m0_{n}")
            gate, lower = rsb("gate", [P, E0]), rsb("lower", [P, E0, E0])
            lg, mx = rsb("lg", [P, T, E0]), rsb("mx", [P, T])
            gt, eq = rsb("gt", [P, T, E0, E0]), rsb("eq", [P, T, E0, E0])
            g_in, w_in, ln, st, ex = rsem("g_in"), rsem("w_in"), rsem("ln"), rsem("st"), rsem("ex")
            logits = ps[:, 4, :]
            tensor, vector, scalar, lg_mm = router_logits(nc, k, r, "m0", gate[:, :], g_in, E0, logits, rsb, rsem)
            block = r.enter_context(nc.Block())

            @block.sync
            def _(sp):
                sp.dma_start(gate[:, :], w["gate"]).then_inc(g_in, 16)
                sp.dma_start(lower[:, :, :], w["lower"]).then_inc(g_in, 16)
                for dst, src in loads:
                    sp.dma_start(dst[:], src).then_inc(w_in, 16)
                sp.wait_ge(g_in, 32)
                sp.wait_ge(w_in, 16 * len(loads))

            @block.tensor
            def _(pe):
                pe.wait_ge(g_in, 32)
                tensor(pe)

            @block.scalar
            def _(act):
                rstd_act(nc, k, act, ln)
                scalar(act)
                act.wait_ge(st, 2)
                nc.scalar.activation(lg[:, :, :], lg[:, :, :], ACT.Exp).then_inc(ex, 1)

            @block.vector
            def _(dve):
                rstd_dve(nc, k, dve, ln, EPS_LN)
                vector(dve)
                wide = [P, T, E0]
                dve.wait_ge(lg_mm, T + 2)
                all_lg = logits[:, 0:T * E0].rearrange("p (t e) -> p t e", e=E0)
                nc.vector.tensor_reduce(mx[:, :], all_lg, AX.X, ALU.max).then_inc(st, 1)
                dve.wait_ge(st, 1)
                nc.vector.tensor_tensor(lg[:, :, :], all_lg, mx[:, :, None].to_broadcast(wide),
                                        ALU.subtract).then_inc(st, 1)
                dve.wait_ge(ex, 1)
                nc.vector.tensor_reduce(mx[:, :], lg[:, :, :], AX.X, ALU.add).then_inc(st, 1)
                dve.wait_ge(st, 3)
                nc.vector.reciprocal(mx[:, :], mx[:, :]).then_inc(st, 1)
                dve.wait_ge(st, 4)
                nc.vector.tensor_tensor(score[:, :, :], lg[:, :, :], mx[:, :, None].to_broadcast(wide),
                                        ALU.mult).then_inc(st, 1)
                dve.wait_ge(st, 5)
                dve.wait_ge(g_in, 32)
                ranked_mask(nc, dve, st, score, gt[:, :, :, :], eq[:, :, :, :], lower, mask[:, :, :], E0, 2, 5)
                nc.vector.tensor_tensor(gain[:, :, :], mask[:, :, :], score[:, :, :], ALU.mult)

        with ExitStack() as m:
            sb = lambda n, s: m.enter_context(nc.sbuf_tensor(f"m0_{n}", s, F32))
            sem = lambda n: k.sem(f"m0_{n}")
            xn, xnT = sb("xn", [P, D]), sb("xnT", [P, P])
            z, hT, g3, mb3, x2 = sb("z", [P, ED]), sb("hT", [P, ED]), sb("g3", [P, ED]), sb("mb3", [P, ED]), sb("x2", [P, ED])
            sa, sh, y = sb("sa", [P, 2 * P]), sb("sh", [P, 2 * P]), sb("y", [P, D])
            (xn_ok, xt_mm, xt_sb, h1_mm, z_raw, z_ok, h_ok, ht_mm, ht_ok, x3_mm, g3_raw, g3_ok, x2_mm, x2_ok, up_mm, sa_ok,
             sh_ok, zo_mm, x_ok, steps, mb3_ok) = [sem(n) for n in (
                 "xn_ok xt_mm xt_sb h1_mm z_raw z_ok h_ok ht_mm ht_ok x3_mm g3_raw g3_ok x2_mm x2_ok up_mm sa_ok "
                 "sh_ok zo_mm x_ok steps mb3_ok").split()]
            H1, X3, HT, UP, XT = 0, 2, 4, 6, 7
            both = lambda pair: ps[:, pair:pair + 2, :].rearrange("p a b -> p (a b)")
            ex = lambda ap: ap.rearrange("p (e d) -> p e d", e=E0)
            col = lambda a, t: at(a, t)[:, :, None].to_broadcast([P, E0, D])
            block = m.enter_context(nc.Block())

            @block.tensor
            def _(pe):
                def turn(t):
                    pe.wait_ge(xn_ok, t + 1)
                    nc.tensor.transpose(ps[:, XT, 0:P], xn[:, :], k.ident[:, :]).then_inc(xt_mm, 1)

                def wide(pair, wt, s):
                    for c in range(2):
                        last = nc.tensor.matmul(ps[:, pair + c, :], xnT[:, :], wt[:, 512 * c:512 * c + 512],
                                                start=True, stop=True)
                    last.then_inc(s, 1)

                def shared_up():
                    for c in range(4):
                        last = nc.tensor.matmul(ps[:, UP, c * P:c * P + P], sw12[:, c * P:c * P + P], xnT[:, :],
                                                start=True, stop=True)
                    last.then_inc(up_mm, 1)

                def step(t, nxt=True):
                    pe.wait_ge(x_ok, t + 1)
                    if nxt:
                        turn(t + 1)
                    pe.wait_ge(h_ok, t + 1)
                    for e in range(E0):
                        last = nc.tensor.transpose(ps[:, HT + e // 4, (e % 4) * P:(e % 4) * P + P],
                                                   z[:, e * P:e * P + P], k.ident[:, :])
                    last.then_inc(ht_mm, 1)
                    if nxt:
                        pe.wait_ge(xt_sb, t + 2)
                    pe.wait_ge(sh_ok, t + 1)
                    for c in range(2):
                        last = nc.tensor.matmul(ps[:, XT, P:P + D], sh[:, c * P:c * P + P], sw3[:, c, :],
                                                start=c == 0, stop=c == 1)
                    last.then_inc(zo_mm, 1)
                    if nxt:
                        wide(H1, w1, h1_mm)
                        shared_up()
                    pe.wait_ge(ht_ok, t + 1)
                    for e in range(E0):
                        last = nc.tensor.matmul(ps[:, HT + e // 4, (e % 4) * P:(e % 4) * P + P],
                                                hT[:, e * P:e * P + P], w2[:, e * D:e * D + D], start=True, stop=True)
                    last.then_inc(x2_mm, 1)
                    if nxt:
                        pe.wait_ge(g3_raw, t + 1)
                        wide(X3, w3, x3_mm)

                turn(0)
                pe.wait_ge(xt_sb, 1)
                wide(H1, w1, h1_mm)
                shared_up()
                wide(X3, w3, x3_mm)
                with pe.Fori(0, T - 1) as t:
                    step(t)
                step(T - 1, nxt=False)

            @block.scalar
            def _(act):
                def turn(t):
                    act.wait_ge(xt_mm, t + 1)
                    nc.scalar.copy(xnT[:, :], ps[:, XT, 0:P]).then_inc(xt_sb, 1)

                def silus(t):
                    act.wait_ge(up_mm, t + 1)
                    nc.scalar.activation(sa[:, :], ps[:, UP, 0:2 * P], ACT.Silu).then_inc(sa_ok, 1)
                    act.wait_ge(z_ok, t + 1)
                    nc.scalar.activation(z[:, :], z[:, :], ACT.Silu).then_inc(h_ok, 1)

                def step(t, nxt=True):
                    if nxt:
                        turn(t + 1)
                    act.wait_ge(ht_mm, t + 1)
                    nc.scalar.copy(hT[:, :], both(HT)).then_inc(ht_ok, 1)
                    if nxt:
                        silus(t + 1)

                turn(0)
                silus(0)
                with act.Fori(0, T - 1) as t:
                    step(t)
                step(T - 1, nxt=False)

            @block.vector
            def _(dve):
                dve.sem_inc(x_ok, 1)
                chain = Chain(dve, steps, 4)

                def weigh(t):
                    dve.wait_ge(h1_mm, t + 1)
                    nc.vector.tensor_tensor(ex(z[:, :]), ex(both(H1)), col(score, t), ALU.mult).then_inc(z_raw, 1)
                    dve.wait_ge(sa_ok, t + 1)
                    nc.vector.tensor_tensor(sh[:, :], ps[:, UP, 2 * P:4 * P], sa[:, :], ALU.mult).then_inc(sh_ok, 1)

                def step(t, nxt=True, nxt2=True):
                    chain.tile(t)
                    dve.wait_ge(x3_mm, t + 1)
                    nc.vector.tensor_tensor(ex(g3[:, :]), ex(both(X3)), col(gain, t), ALU.mult).then_inc(g3_raw, 1)
                    if nxt:
                        weigh(t + 1)
                    if nxt2:
                        dve.wait_ge(xt_mm, t + 2)
                        normalise(nc, k, xn[:, :], t + 2).then_inc(xn_ok, 1)
                    dve.wait_ge(x2_mm, t + 1)
                    chain.done(nc.vector.tensor_tensor(x2[:, :], both(HT), b2[:, :], ALU.add))
                    dve.wait_ge(g3_ok, t + 1)
                    chain.done(nc.vector.tensor_tensor(x2[:, :], x2[:, :], g3[:, :], ALU.mult))
                    nc.vector.tensor_reduce(y[:, :], x2[:, :].rearrange("p (e d) -> p d e", e=E0), AX.X,
                                            ALU.add).then_inc(x2_ok, 1)
                    dve.wait_ge(x2_ok, t + 1)
                    dve.wait_ge(zo_mm, t + 1)
                    add_to_x_and_count(nc, k, chain, t, ps[:, XT, P:P + D], y[:, :]).then_inc(x_ok, 1)
                    chain.end()

                normalise(nc, k, xn[:, :], 0).then_inc(xn_ok, 1)
                weigh(0)
                dve.wait_ge(xt_mm, 1)
                normalise(nc, k, xn[:, :], 1).then_inc(xn_ok, 1)
                with dve.Fori(0, T - 2) as t:
                    step(t)
                step(T - 2, nxt2=False)
                step(T - 1, nxt=False, nxt2=False)

            @block.gpsimd
            def _(pool):
                def bias1(t):
                    pool.wait_ge(z_raw, t + 1)
                    nc.gpsimd.tensor_tensor(z[:, :], z[:, :], b1[:, :], ALU.add).then_inc(z_ok, 1)

                def step(t, nxt=True):
                    nc.gpsimd.tensor_tensor(ex(mb3[:, :]), ex(b3[:, :]), col(mask, t), ALU.mult).then_inc(mb3_ok, 1)
                    pool.wait_ge(mb3_ok, t + 1)
                    pool.wait_ge(g3_raw, t + 1)
                    nc.gpsimd.tensor_tensor(g3[:, :], g3[:, :], mb3[:, :], ALU.add).then_inc(g3_ok, 1)
                    pool.wait_ge(g3_ok, t + 1)
                    if nxt:
                        bias1(t + 1)

                bias1(0)
                with pool.Fori(0, T - 1) as t:
                    step(t)
                step(T - 1, nxt=False)


def stage_alibi(nc, k, w):
    with ExitStack() as ctx:
        sb = lambda n, s: ctx.enter_context(nc.sbuf_tensor(f"al_{n}", s, F32))
        sem = lambda n: k.sem(f"al_{n}")
        ps = k.ps
        wq, wk, wv, wo, bo = [sb(n, [P, D]) for n in ("wq", "wk", "wv", "wo", "bo")]
        alibi = sb("alibi", [P, H, N])
        hm, bm = sb("hm", [P, H]), sb("bm", [P, SEQ])
        xn, xnT = sb("xn", [P, D]), sb("xnT", [P, P])
        qT, vs = sb("qT", [P, P]), sb("vs", [P, 2, D])
        kbd = sb("kbd", [P, SEQ, H, N])
        e, pT = sb("e", [P, H, N]), sb("pT", [P, H, N])
        pbd = sb("pbd", [P, H, SEQ, N])
        mx, den, rec = sb("mx", [P, H]), sb("den", [P, H]), sb("rec", [P, 2, H])
        a, aT = sb("a", [P, D]), sb("aT", [P, P])
        loads = [(wq, w["wq"]), (wk, w["wk"]), (wv, w["wv"]), (wo, w["wo"]), (bo, w["bo"]), (alibi, w["alibi"]),
                 (hm, w["hm"]), (bm, w["bm"])]
        (w_in, ln, xn_ok, xt_mm, xt_sb, qkv_mm, k_ok, qv_ok, s_mm, sub_ok, exp_ok, pt_ok, pbd_ok, o_mm, a_ok, at_mm, at_ok,
         wo_mm, x_ok, steps, steps_x) = [sem(n) for n in (
             "w_in ln xn_ok xt_mm xt_sb qkv_mm k_ok qv_ok s_mm sub_ok exp_ok pt_ok pbd_ok o_mm a_ok at_mm at_ok "
             "wo_mm x_ok steps steps_x").split()]
        XT, K_B, QV, S_B, O_B, AT, WO = 0, 1, 2, 3, 4, 5, 6
        block = ctx.enter_context(nc.Block())

        @block.sync
        def _(sp):
            for dst, src in loads:
                sp.dma_start(dst[:], src).then_inc(w_in, 16)
            sp.wait_ge(w_in, 16 * len(loads))

        @block.tensor
        def _(pe):
            pe.wait_ge(w_in, 16 * len(loads))

            def turn(t):
                pe.wait_ge(xn_ok, t + 1)
                nc.tensor.transpose(ps[:, XT, 0:P], xn[:, :], k.ident[:, :]).then_inc(xt_mm, 1)

            def front(t):
                pe.wait_ge(xt_sb, t + 1)
                nc.tensor.matmul(ps[:, K_B, 0:P], wk[:, :], xnT[:, :], start=True, stop=True)
                nc.tensor.matmul(ps[:, QV, 0:P], wq[:, :], xnT[:, :], start=True, stop=True)
                nc.tensor.matmul(ps[:, QV, P:2 * P], xnT[:, :], wv[:, :], start=True, stop=True).then_inc(qkv_mm, 1)

            def scores(t):
                pe.wait_ge(qv_ok, t + 1)
                pe.wait_ge(k_ok, t + 1)
                for b in range(SEQ):
                    last = nc.tensor.matmul(ps[N * b:N * b + N, S_B, :], qT[:, N * b:N * b + N],
                                            kbd[:, b, :, :], start=True, stop=True)
                last.then_inc(s_mm, 1)

            def rear(t, j):
                pe.wait_ge(pbd_ok, t + 2)
                for h in range(H):
                    last = nc.tensor.matmul(ps[:, O_B, DH1 * h:DH1 * h + DH1], pbd[:, h, :, :],
                                            vs[:, j, DH1 * h:DH1 * h + DH1], start=True, stop=True)
                last.then_inc(o_mm, 1)
                pe.wait_ge(a_ok, t + 1)
                nc.tensor.transpose(ps[:, AT, 0:P], a[:, :], k.ident[:, :]).then_inc(at_mm, 1)
                pe.wait_ge(at_ok, t + 1)
                pe.wait_ge(x_ok, t + 1)
                nc.tensor.matmul(ps[:, WO, 0:D], aT[:, :], wo[:, :], start=True, stop=True).then_inc(wo_mm, 1)

            def step(t, j, nxt=True, nxt2=True):
                if nxt:
                    front(t + 1)
                    if nxt2:
                        turn(t + 2)
                    pe.wait_ge(sub_ok, 2 * t + 2)
                    scores(t + 1)
                rear(t, j)

            pe.sem_inc(o_mm, 1)
            turn(0)
            front(0)
            turn(1)
            scores(0)
            with pe.Fori(0, T // 2 - 1) as i:
                for j in range(2):
                    step(2 * i + j, j)
            step(T - 2, 0, nxt2=False)
            step(T - 1, 1, nxt=False)

        @block.scalar
        def _(act):
            act.wait_ge(w_in, 16 * len(loads))
            rstd_act(nc, k, act, ln)

            def turn(t):
                act.wait_ge(xt_mm, t + 1)
                nc.scalar.copy(xnT[:, :], ps[:, XT, 0:P]).then_inc(xt_sb, 1)

            def front(t, j):
                act.wait_ge(qkv_mm, t + 1)
                nc.scalar.mul(qT[:, :], ps[:, QV, 0:P], DH1 ** -0.5)
                nc.scalar.copy(vs[:, j, :], ps[:, QV, P:2 * P]).then_inc(qv_ok, 1)

            def expo(t):
                act.wait_ge(sub_ok, 2 * t + 2)
                nc.scalar.activation(e[:, :, :], e[:, :, :], ACT.Exp).then_inc(exp_ok, 1)

            def step(t, j, nxt=True, nxt2=True):
                if nxt:
                    front(t + 1, 1 - j)
                    if nxt2:
                        turn(t + 2)
                act.wait_ge(at_mm, t + 1)
                nc.scalar.copy(aT[:, :], ps[:, AT, 0:P]).then_inc(at_ok, 1)
                if nxt:
                    expo(t + 1)

            turn(0)
            front(0, 0)
            turn(1)
            expo(0)
            with act.Fori(0, T // 2 - 1) as i:
                for j in range(2):
                    step(2 * i + j, j)
            step(T - 2, 0, nxt2=False)
            step(T - 1, 1, nxt=False)

        @block.vector
        def _(dve):
            dve.sem_inc(x_ok, 1)
            dve.wait_ge(w_in, 16 * len(loads))
            rstd_dve(nc, k, dve, ln, EPS_LN)
            soft, outs = Chain(dve, steps, 3), Chain(dve, steps_x, 2)
            hk = [P, H, N]

            def keys(t):
                dve.wait_ge(qkv_mm, t + 1)
                shape = [P, SEQ, H, N]
                nc.vector.tensor_tensor(kbd[:, :, :, :], ps[:, K_B, 0:P].rearrange("p (b n) -> p b n", b=SEQ)[
                    :, :, None, :].to_broadcast(shape), hm[:, None, :, None].to_broadcast(shape), ALU.mult).then_inc(k_ok, 1)

            def softmax(t, j):
                soft.tile(t)
                dve.wait_ge(s_mm, t + 1)
                nc.vector.tensor_tensor(e[:, :, :], ps[:, S_B, :].rearrange("p (h n) -> p h n", h=H), alibi[:, :, :],
                                        ALU.add).then_inc(sub_ok, 1)
                dve.wait_ge(sub_ok, 2 * t + 1)
                soft.done(nc.vector.tensor_reduce(mx[:, :], e[:, :, :], AX.X, ALU.max))
                nc.vector.tensor_tensor(e[:, :, :], e[:, :, :], mx[:, :, None].to_broadcast(hk),
                                        ALU.subtract).then_inc(sub_ok, 1)
                dve.wait_ge(exp_ok, t + 1)
                dve.wait_ge(pbd_ok, t + 1)
                nc.vector.transpose(pT[:, :, :].rearrange("p h n -> p (h n)"),
                                    e[:, :, :].rearrange("p h n -> p (h n)")).then_inc(pt_ok, 1)
                soft.done(nc.vector.tensor_reduce(den[:, :], e[:, :, :], AX.X, ALU.add))
                soft.done(nc.vector.reciprocal(rec[:, j, :], den[:, :]))
                soft.end()

            def step(t, j, nxt=True, nxt2=True, nxt3=True):
                if nxt:
                    keys(t + 1)
                if nxt2 and nxt3:
                    dve.wait_ge(xt_mm, t + 3)
                    normalise(nc, k, xn[:, :], t + 3).then_inc(xn_ok, 1)
                dve.wait_ge(o_mm, t + 2)
                nc.vector.tensor_tensor(a[:, :].rearrange("p (h d) -> p h d", h=H),
                                        ps[:, O_B, 0:D].rearrange("p (h d) -> p h d", h=H),
                                        rec[:, j, :, None].to_broadcast([P, H, DH1]), ALU.mult).then_inc(a_ok, 1)
                if nxt:
                    softmax(t + 1, 1 - j)
                outs.tile(t)
                dve.wait_ge(wo_mm, t + 1)
                add_to_x_and_count(nc, k, outs, t, ps[:, WO, 0:D], bo[:, :]).then_inc(x_ok, 1)

            normalise(nc, k, xn[:, :], 0).then_inc(xn_ok, 1)
            dve.wait_ge(xt_mm, 1)
            normalise(nc, k, xn[:, :], 1).then_inc(xn_ok, 1)
            keys(0)
            dve.wait_ge(xt_mm, 2)
            normalise(nc, k, xn[:, :], 2).then_inc(xn_ok, 1)
            softmax(0, 0)
            with dve.Fori(0, T // 2 - 2) as i:
                for j in range(2):
                    step(2 * i + j, j)
            step(T - 4, 0)
            step(T - 3, 1, nxt3=False)
            step(T - 2, 0, nxt2=False)
            step(T - 1, 1, nxt=False, nxt2=False)

        @block.gpsimd
        def _(pool):
            pool.sem_inc(pbd_ok, 1)
            shape = [P, H, SEQ, N]
            with pool.Fori(0, T) as t:
                pool.wait_ge(pt_ok, t + 1)
                pool.wait_ge(o_mm, t + 1)
                nc.gpsimd.tensor_tensor(pbd[:, :, :, :], pT[:, :, None, :].to_broadcast(shape),
                                        bm[:, None, :, None].to_broadcast(shape), ALU.mult).then_inc(pbd_ok, 1)


def stage_moe1(nc, k, w):
    EG = 8
    UNITS = [8, 8, 8, 8, 1]
    NU = len(UNITS)
    COLS = (E1 + 1) * I1
    NPAIR = E1 // 2
    with ExitStack() as ctx:
        sb = lambda n, s: ctx.enter_context(nc.sbuf_tensor(f"m1_{n}", s, F32))
        ps = k.ps
        comb = sb("comb", [P, T, E1 + 1])
        wg, wu, wd = sb("wg", [P, COLS]), sb("wu", [P, COLS]), sb("wd", [P, NPAIR + 1, D])
        loads = [(wg, w["wg"]), (wu, w["wu"]), (wd, w["wd"])]

        with ExitStack() as r:
            rsb = lambda n, s: r.enter_context(nc.sbuf_tensor(f"m1_{n}", s, F32))
            rsem = lambda n: k.sem(f"m1_{n}")
            gate, lower = rsb("gate", [P, E1]), rsb("lower", [P, 8, 8])
            sc, rest = rsb("sc", [P, T, E1]), rsb("rest", [P, T, E1])
            gs, gm = rsb("gs", [P, T, 8]), rsb("gm", [P, T, 8])
            top = rsb("top", [P, T, 8])
            tot = rsb("tot", [P, T])
            gt, eq = rsb("gt", [P, T, 8, 8]), rsb("eq", [P, T, 8, 8])
            g_in, w_in, ln, st, sg = rsem("g_in"), rsem("w_in"), rsem("ln"), rsem("st"), rsem("sg")
            logits = ps[:, 4:6, :].rearrange("p a b -> p (a b)")
            tensor, vector, scalar, lg_mm = router_logits(nc, k, r, "m1", gate[:, :], g_in, E1, logits, rsb, rsem)
            block = r.enter_context(nc.Block())

            @block.sync
            def _(sp):
                sp.dma_start(gate[:, :], w["gate"]).then_inc(g_in, 16)
                sp.dma_start(lower[:, :, :], w["lower"]).then_inc(g_in, 16)
                for dst, src in loads:
                    sp.dma_start(dst[:], src).then_inc(w_in, 16)
                sp.wait_ge(g_in, 32)
                sp.wait_ge(w_in, 16 * len(loads))

            @block.tensor
            def _(pe):
                pe.wait_ge(g_in, 32)
                tensor(pe)

            @block.scalar
            def _(act):
                rstd_act(nc, k, act, ln)
                scalar(act)
                act.wait_ge(lg_mm, T + 2)
                nc.scalar.activation(sc[:, :, :].rearrange("p t e -> p (t e)"), logits, ACT.Sigmoid).then_inc(sg, 1)

            @block.vector
            def _(dve):
                rstd_dve(nc, k, dve, ln, EPS_LN)
                vector(dve)
                dve.wait_ge(g_in, 32)
                dve.wait_ge(sg, 1)
                four = sc[:, :, :].rearrange("p t (g e) -> p t g e", g=8)
                nc.vector.tensor_reduce(gs[:, :, :], four, AX.X, ALU.add).then_inc(st, 1)
                dve.wait_ge(st, 1)
                ranked_mask(nc, dve, st, gs, gt[:, :, :, :], eq[:, :, :, :], lower, gm[:, :, :], 8, 4, 1)
                nc.vector.tensor_tensor(four, four, gm[:, :, :, None].to_broadcast([P, T, 8, 4]), ALU.mult).then_inc(st, 1)
                dve.wait_ge(st, 7)
                for t in range(T):
                    last = nc.vector.max(top[:, t, :], sc[:, t, :])
                last.then_inc(st, 1)
                dve.wait_ge(st, 8)
                for t in range(T):
                    last = nc.vector.match_replace(out=rest[:, t, :], in_to_replace=top[:, t, :], in_values=sc[:, t, :],
                                                   imm_value=-1.0)
                last.then_inc(st, 1)
                dve.wait_ge(st, 9)
                nc.vector.scalar_tensor_tensor(rest[:, :, :], rest[:, :, :], 0.0, sc[:, :, :], ALU.is_lt,
                                               ALU.mult).then_inc(st, 1)
                dve.wait_ge(st, 10)
                nc.vector.tensor_reduce(tot[:, :], rest[:, :, :], AX.X, ALU.add).then_inc(st, 1)
                dve.wait_ge(st, 11)
                nc.vector.tensor_scalar(tot[:, :], tot[:, :], 1e-12, None, ALU.max).then_inc(st, 1)
                dve.wait_ge(st, 12)
                nc.vector.reciprocal(tot[:, :], tot[:, :]).then_inc(st, 1)
                dve.wait_ge(st, 13)
                nc.vector.memset(comb[:, :, E1:E1 + 1], 1.0)
                nc.vector.tensor_tensor(comb[:, :, 0:E1], rest[:, :, :], tot[:, :, None].to_broadcast([P, T, E1]), ALU.mult)

        with ExitStack() as m:
            sb = lambda n, s: m.enter_context(nc.sbuf_tensor(f"m1_{n}", s, F32))
            sem = lambda n: k.sem(f"m1_{n}")
            xn, xnT = sb("xn", [P, D]), sb("xnT", [P, 2, P])
            sg, hh, hT = sb("sg", [P, 2, 512]), sb("hh", [P, 2, 512]), sb("hT", [P, 2, 512])
            comb_t = sb("comb_t", [P, 2, E1 + 1])
            (xn_ok, xt_mm, xt_sb, gu_mm, sg_ok, hh_raw, hh_ok, tr_mm, tr_ok, dn_mm, out_mm, x_ok, steps) = [sem(n) for n in (
                "xn_ok xt_mm xt_sb gu_mm sg_ok hh_raw hh_ok tr_mm tr_ok dn_mm out_mm x_ok steps").split()]
            G_B, T_B, ACC, XT = 0, 4, 6, 7
            block = m.enter_context(nc.Block())

            @block.tensor
            def _(pe):
                def turn(t):
                    pe.wait_ge(xn_ok, t + 1)
                    nc.tensor.transpose(ps[:, XT, 0:P], xn[:, :], k.ident[:, :]).then_inc(xt_mm, 1)

                def gates(g, j, v):
                    n, c = UNITS[g] * I1, EG * I1 * g
                    b = G_B + 2 * ((NU * j + g) % 2)
                    nc.tensor.matmul(ps[:, b, 0:n], xnT[:, j, :], wg[:, c:c + n], start=True, stop=True)
                    nc.tensor.matmul(ps[:, b + 1, 0:n], xnT[:, j, :], wu[:, c:c + n], start=True, stop=True).then_inc(gu_mm, 1)

                def turn_h(g, j, v):
                    par = (NU * j + g) % 2
                    pe.wait_ge(hh_ok, v + 1)
                    if UNITS[g] == 1:
                        nc.tensor.nop(nofuse=True)
                    for c in range(max(UNITS[g] // 2, 1)):
                        n = min(P, UNITS[g] * I1)
                        last = nc.tensor.transpose(ps[0:n, T_B + par, c * P:c * P + P], hh[:, par, c * P:c * P + n],
                                                   k.ident[:, :])
                    last.then_inc(tr_mm, 1)

                def down(g, j, v):
                    par = (NU * j + g) % 2
                    pe.wait_ge(tr_ok, v + 1)
                    for c in range(max(UNITS[g] // 2, 1)):
                        n = min(P, UNITS[g] * I1)
                        last = nc.tensor.matmul(ps[:, ACC, 0:D], hT[0:n, par, c * P:c * P + P], wd[0:n, 4 * g + c, :],
                                                start=g == 0 and c == 0, stop=g == NU - 1)
                    last.then_inc(dn_mm, 1)

                def tile(t, j, first=False, last=False):
                    for g in range(NU):
                        v = NU * t + g
                        if g < NU - 1:
                            gates(g + 1, j, v + 1)
                        elif not last:
                            pe.wait_ge(xt_sb, t + 2)
                            gates(0, 1 - j, v + 1)
                        if g == 1 and not last:
                            turn(t + 1)
                        if g > 0:
                            if g == 1 and not first:
                                pe.wait_ge(x_ok, t)
                            down(g - 1, j, v - 1)
                        elif not first:
                            down(NU - 1, 1 - j, v - 1)
                        turn_h(g, j, v)

                turn(0)
                pe.wait_ge(xt_sb, 1)
                gates(0, 0, 0)
                tile(0, 0, first=True)
                with pe.Fori(0, T // 2 - 1) as i:
                    tile(2 * i + 1, 1)
                    tile(2 * i + 2, 0)
                tile(T - 1, 1, last=True)
                down(NU - 1, 1, NU * T - 1)

            @block.scalar
            def _(act):
                def turn(t, j):
                    act.wait_ge(xt_mm, t + 1)
                    nc.scalar.copy(xnT[:, j, :], ps[:, XT, 0:P]).then_inc(xt_sb, 1)

                def silu(g, j, v):
                    par, n = (NU * j + g) % 2, UNITS[g] * I1
                    act.wait_ge(gu_mm, v + 1)
                    nc.scalar.activation(sg[:, par, 0:n], ps[:, G_B + 2 * par, 0:n], ACT.Silu).then_inc(sg_ok, 1)

                def moved(g, j, v):
                    par = (NU * j + g) % 2
                    p, n = (P, 512) if UNITS[g] > 1 else (I1, P)
                    act.wait_ge(tr_mm, v + 1)
                    nc.scalar.copy(hT[0:p, par, 0:n], ps[0:p, T_B + par, 0:n]).then_inc(tr_ok, 1)

                def tile(t, j, last=False):
                    for g in range(NU):
                        v = NU * t + g
                        if g < NU - 1:
                            silu(g + 1, j, v + 1)
                        elif not last:
                            silu(0, 1 - j, v + 1)
                        if g == 1 and not last:
                            turn(t + 1, 1 - j)
                        moved(g, j, v)

                turn(0, 0)
                silu(0, 0, 0)
                with act.Fori(0, T // 2 - 1) as i:
                    tile(2 * i, 0)
                    tile(2 * i + 1, 1)
                tile(T - 2, 0)
                tile(T - 1, 1, last=True)

            @block.vector
            def _(dve):
                def weights(t, j):
                    nc.vector.tensor_scalar(comb_t[:, j, :], at(comb, t), 1.0, None, ALU.mult)

                def up(g, j, v):
                    par, n = (NU * j + g) % 2, UNITS[g] * I1
                    dve.wait_ge(sg_ok, v + 1)
                    nc.vector.tensor_tensor(hh[:, par, 0:n], ps[:, G_B + 2 * par + 1, 0:n], sg[:, par, 0:n],
                                            ALU.mult).then_inc(hh_raw, 1)

                def out(t):
                    dve.wait_ge(dn_mm, NU * t + NU)
                    nc.vector.tensor_tensor(at(k.x, t), ps[:, ACC, 0:D], at(k.x, t), ALU.add).then_inc(x_ok, 1)

                def tile(t, j, first=False, last=False, last2=False):
                    for g in range(NU):
                        v = NU * t + g
                        if g < NU - 1:
                            up(g + 1, j, v + 1)
                        elif not last:
                            up(0, 1 - j, v + 1)
                        if g == 0 and not first:
                            out(t - 1)
                        if g == 0 and not last:
                            weights(t + 1, 1 - j)
                        if g == 2 and not last and not last2:
                            dve.wait_ge(xt_mm, t + 2)
                            normalise(nc, k, xn[:, :], t + 2).then_inc(xn_ok, 1)

                normalise(nc, k, xn[:, :], 0).then_inc(xn_ok, 1)
                weights(0, 0)
                up(0, 0, 0)
                dve.wait_ge(xt_mm, 1)
                normalise(nc, k, xn[:, :], 1).then_inc(xn_ok, 1)
                tile(0, 0, first=True)
                with dve.Fori(0, T // 2 - 2) as i:
                    tile(2 * i + 1, 1)
                    tile(2 * i + 2, 0)
                tile(T - 3, 1)
                tile(T - 2, 0, last2=True)
                tile(T - 1, 1, last=True)
                out(T - 1)

            @block.gpsimd
            def _(pool):
                def weigh(g, j, v):
                    par, n = (NU * j + g) % 2, UNITS[g]
                    pool.wait_ge(hh_raw, v + 1)
                    h = hh[:, par, 0:n * I1].rearrange("p (e i) -> p e i", e=n)
                    nc.gpsimd.tensor_tensor(h, h, comb_t[:, j, EG * g:EG * g + n, None].to_broadcast([P, n, I1]),
                                            ALU.mult).then_inc(hh_ok, 1)

                with pool.Fori(0, T // 2) as i:
                    for j in range(2):
                        for g in range(NU):
                            weigh(g, j, NU * (2 * i + j) + g)


def stage_store(nc, k, out_dram):
    with ExitStack() as ctx:
        stored = k.sem("stored")
        block = ctx.enter_context(nc.Block())

        @block.sync
        def _(sp):
            sp.dma_start(out_dram.rearrange("(t p) d -> p t d", p=P), k.x[:, :, :]).then_inc(stored, 16)
            sp.wait_ge(stored, 16)


def program(nc, d, out):
    with ExitStack() as ctx:
        k = Core(nc, ctx)
        stage_load(nc, k, d["x"], d["ident"])
        stage_xattn(nc, k, "l0", {n[3:]: a for n, a in d.items() if n.startswith("a0_")},
                    d["ctx_t"], d["ctx_k"], d["ctx_x"])
        stage_performer(nc, k, {n[2:]: a for n, a in d.items() if n.startswith("e_")})
        stage_moe0(nc, k, {n[2:]: a for n, a in d.items() if n.startswith("m_")})
        k.clear_sems()
        stage_xattn(nc, k, "l1", {n[3:]: a for n, a in d.items() if n.startswith("a1_")},
                    d["ctx_t"], d["ctx_k"], d["ctx_x"])
        stage_alibi(nc, k, {n[2:]: a for n, a in d.items() if n.startswith("s_")})
        stage_moe1(nc, k, {n[2:]: a for n, a in d.items() if n.startswith("g_")})
        stage_store(nc, k, out)


def layout(v):
    f = np.float32
    rows = lambda a, n=P: np.broadcast_to(np.asarray(a), (n, np.asarray(a).shape[-1]))
    x = np.asarray(v["x"]).reshape(B * N, D)
    c = np.asarray(v["ctx_768"])
    ca = np.concatenate([c, np.ones((B, NK, 1), f)], axis=2).reshape(T, SEQ, NK, CA)
    ctx_t = ca.transpose(0, 3, 1, 2).reshape(T, CA, SEQ * NK)
    ctx_k = ca[:, :, :256].reshape(T, SEQ, 2, P, CA).transpose(0, 3, 1, 2, 4).reshape(T, P, SEQ * 2 * CA)
    ctx_x = np.zeros((T, SEQ, SEQ, CA), f)
    for b in range(SEQ):
        ctx_x[:, b, b] = ca[:, b, 256]
    pad = lambda a: np.concatenate([a, np.zeros((a.shape[0], 1), f)], axis=1)
    two = lambda a: a.reshape(H // 2, P, a.shape[1]).transpose(1, 0, 2)
    d = {"x": x, "ident": np.eye(P, dtype=f), "ctx_t": ctx_t, "ctx_k": ctx_k, "ctx_x": ctx_x.reshape(T, SEQ, SEQ * CA)}
    d["a0_wqT"] = two(np.asarray(v["L0_xattn_Wq"]).T)
    d["a0_wkT"] = two(pad(np.asarray(v["L0_xattn_Wk"]).T))
    d["a0_wvT"] = two(pad(np.asarray(v["L0_xattn_Wv"]).T))
    d["a0_wo"] = two(np.asarray(v["L0_xattn_Wo"]))
    d["a0_bo"] = rows(v["L0_xattn_bo"])
    kv = np.concatenate([np.asarray(v["L1_xattn_kv_w"]), np.asarray(v["L1_xattn_kv_b"])[None]], axis=0).T
    d["a1_wqT"] = np.asarray(v["L1_xattn_q_w"]).T
    d["a1_kaT"], d["a1_vaT"] = kv[:D], kv[D:]
    d["a1_wo"] = np.asarray(v["L1_xattn_proj_w"])
    d["a1_head_mask"] = np.repeat(np.eye(H, dtype=f), DH1, axis=0)
    d["a1_qb"] = np.asarray(v["L1_xattn_q_b"])[:, None]
    d["a1_bo"] = rows(v["L1_xattn_proj_b"])
    flat = lambda n: np.asarray(v[n]).reshape(D, H * DH0)
    same = lambda n, size: np.repeat(np.repeat(np.eye(n, dtype=f), size, 0), size, 1)
    d["e_wq"], d["e_wk"], d["e_wv"] = flat("L0_attn_Wq"), flat("L0_attn_Wk"), flat("L0_attn_Wv")
    d["e_wqT"], d["e_wkT"] = two(flat("L0_attn_Wq").T), two(flat("L0_attn_Wk").T)
    d["e_projT"] = np.tile(np.asarray(v["L0_attn_proj"]).T, (2, 1))
    d["e_wo"] = two(np.asarray(v["L0_attn_Wo"]).reshape(H * DH0, D))
    d["e_blocks"] = same(2, DH0) * f(-0.5 * DH0 ** -0.5)
    d["e_mask"] = same(SEQ, N)
    d["e_w1"] = np.asarray(v["L0_attn_W1"])
    d["e_w2"] = np.asarray(v["L0_attn_W2"]).reshape(FF // P, P, D).transpose(1, 0, 2)
    d["e_b1"] = np.asarray(v["L0_attn_b1"]).reshape(FF // P, P).T
    d["e_rows"] = np.stack([rows(v[n]) for n in ("L0_attn_ln1_g", "L0_attn_ln1_b", "L0_attn_b2", "L0_attn_ln2_g",
                                                 "L0_attn_ln2_b")], axis=1)
    lower = np.broadcast_to(np.tril(np.ones((8, 8), f), -1), (P, 8, 8))
    up = lambda n: np.asarray(v[n]).transpose(2, 0, 1).reshape(D, -1)
    for n in ("w1", "w2", "w3"):
        d["m_" + n] = up("L0_ffn_" + n)
    for n in ("b1", "b2", "b3"):
        d["m_" + n] = rows(np.asarray(v["L0_ffn_" + n]).reshape(-1))
    d["m_gate"], d["m_lower"] = np.asarray(v["L0_ffn_gate_w"]).T, lower
    d["m_sw12"] = np.concatenate([np.asarray(v["L0_ffn_sw1"]), np.asarray(v["L0_ffn_sw2"])]).T
    d["m_sw3"] = np.asarray(v["L0_ffn_sw3"]).T.reshape(2, P, D).transpose(1, 0, 2)
    for n in "qkvo":
        d["s_w" + n] = np.asarray(v["L1_attn_W" + n]).T
    d["s_bo"] = rows(v["L1_attn_bo"])
    start = 2.0 ** (-2.0 ** (-(np.log2(H) - 3)))
    slopes = np.array([start * start ** i for i in range(H)], f)
    rel = np.abs(np.arange(N)[None, :] - np.arange(N)[:, None]).astype(f)
    d["s_alibi"] = np.tile(-slopes[None, :, None] * rel[:, None, :], (SEQ, 1, 1))
    d["s_hm"], d["s_bm"] = d["a1_head_mask"], np.repeat(np.eye(SEQ, dtype=f), N, axis=0)
    both = lambda e, sh: np.concatenate([np.asarray(v[e]).reshape(E1 * I1, D), np.asarray(v[sh])]).T
    d["g_gate"], d["g_lower"] = np.asarray(v["L1_ffn_gate_w"]).T, lower
    d["g_wg"] = both("L1_ffn_expert_gate", "L1_ffn_shared_gate_w")
    d["g_wu"] = both("L1_ffn_expert_up", "L1_ffn_shared_up_w")
    wd = np.zeros(((E1 + 2) * I1, D), f)
    wd[:E1 * I1] = np.asarray(v["L1_ffn_expert_down"]).transpose(0, 2, 1).reshape(E1 * I1, D)
    wd[E1 * I1:(E1 + 1) * I1] = np.asarray(v["L1_ffn_shared_down_w"]).T
    d["g_wd"] = wd.reshape(E1 // 2 + 1, P, D).transpose(1, 0, 2)
    return {n: np.ascontiguousarray(a) for n, a in d.items()}


def kernel(**inputs):
    import concourse.bacc as bacc
    from concourse.bass_utils import run_bass_kernel_spmd

    nc = bacc.Bacc("TRN2", target_bir_lowering=False, num_devices=1)
    arrays = layout(inputs)
    aps = {n: nc.dram_tensor(f"in_{n}", a.shape, mybir.dt.from_np(a.dtype), kind="ExternalInput").ap()
           for n, a in arrays.items()}
    out = nc.dram_tensor("out_x", (B * N, D), F32, kind="ExternalOutput").ap()
    program(nc, aps, out)
    r = run_bass_kernel_spmd(nc, [{f"in_{n}": a for n, a in arrays.items()}], core_ids=[0])
    return r.results[0]["out_x"].reshape(B, N, D)
```

```python
from contextlib import ExitStack

import numpy as np
import concourse.bass as bass
from concourse import mybir

F32 = mybir.dt.float32
ACT = mybir.ActivationFunctionType
ALU = mybir.AluOpType
AX = mybir.AxisListType

B, N, D = 128, 32, 128
P = 128
T = B * N // P
SEQ = P // N
C, CA = 96, 97
NK = 257
H = 16
HG = 4
DH0 = 64
DH1 = D // H
EPS_LN = 1e-5
EPS_ENC = 1e-6
EPS_KERN = 1e-6
FF = 512
E0, E1 = 8, 32
I1 = 64


def at(ap, t):
    return ap[:, bass.ds(t, 1), :].rearrange("p t n -> p (t n)")


class Chain:

    def __init__(self, eng, sem, per_tile):
        self.eng, self.sem, self.per, self.base, self.n = eng, sem, per_tile, 0, 0

    def tile(self, t):
        self.base, self.n = t * self.per, 0

    def done(self, ins):
        self.n += 1
        ins.then_inc(self.sem, 1)
        self.eng.wait_ge(self.sem, self.base + self.n)

    def end(self):
        assert self.n == self.per, (self.n, self.per)


class Core:

    def __init__(self, nc, ctx):
        self.nc = nc
        sb = lambda n, s: ctx.enter_context(nc.sbuf_tensor(n, s, F32))
        self.x = sb("x", [P, T, D])
        self.stats = sb("stats", [P, T, 6])
        self.mean = sb("mean", [P, T])
        self.half = sb("half", [P, 5, T])
        self.var_eps = sb("var_eps", [P, T])
        self.std = sb("std", [P, T])
        self.rstd = sb("rstd", [P, T])
        self.ident = sb("ident", [P, P])
        self.sems = []
        self.ps = ctx.enter_context(nc.psum_tensor("ps", [P, 8, 512], F32))

    def sem(self, name):
        self.sems.append(self.nc.alloc_semaphore(name))
        return self.sems[-1]

    def clear_sems(self):
        self.nc.clear_and_free_semaphores(self.sems)
        self.nc.all_engine_barrier()
        self.sems = []


def add_to_x_and_count(nc, k, chain, t, psum, bias, xs=None):
    xt = at(k.x, t)
    chain.done(nc.vector.tensor_tensor(xt, psum, xt, ALU.add))
    chain.done(nc.vector.tensor_tensor(xt, xt, bias, ALU.add))
    nc.vector.nop(nofuse=True)
    return nc.vector.bn_stats(at(k.stats, t), xt)


def stage_load(nc, k, x_dram, ident_dram):
    with ExitStack() as ctx:
        x_in = k.sem("x_in")
        id_in = k.sem("id_in")
        steps = k.sem("load_steps")
        block = ctx.enter_context(nc.Block())

        @block.sync
        def _(sp):
            sp.dma_start(k.x[:, :, :], x_dram.rearrange("(t p) d -> p t d", p=P)).then_inc(x_in, 16)
            sp.dma_start(k.ident[:, :], ident_dram).then_inc(id_in, 16)
            sp.wait_ge(id_in, 16)

        @block.vector
        def _(dve):
            dve.wait_ge(x_in, 16)
            with dve.Fori(0, T) as t:
                nc.vector.bn_stats(at(k.stats, t), at(k.x, t)).then_inc(steps, 1)
            dve.wait_ge(steps, T)


def rstd_dve(nc, k, dve, ln, eps):
    col = lambda n: k.stats[:, :, n:n + 1].rearrange("p t o -> p (t o)")
    h = k.half
    nc.vector.tensor_tensor(h[:, 0, :], col(1), col(4), ALU.add)
    nc.vector.tensor_tensor(h[:, 1, :], col(1), col(4), ALU.subtract)
    nc.vector.tensor_tensor(h[:, 2, :], col(2), col(5), ALU.add).then_inc(ln, 1)
    dve.wait_ge(ln, 1)
    nc.vector.tensor_scalar(k.mean[:, :], h[:, 0, :], 0.5, None, ALU.mult)
    nc.vector.tensor_tensor(h[:, 3, :], h[:, 1, :], h[:, 1, :], ALU.mult)
    nc.vector.tensor_scalar(h[:, 4, :], h[:, 2, :], 1.0 / D, eps, ALU.mult, ALU.add).then_inc(ln, 1)
    dve.wait_ge(ln, 2)
    nc.vector.scalar_tensor_tensor(k.var_eps[:, :], h[:, 3, :], 0.25, h[:, 4, :], ALU.mult, ALU.add).then_inc(ln, 1)
    dve.wait_ge(ln, 4)
    nc.vector.reciprocal(k.rstd[:, :], k.std[:, :]).then_inc(ln, 1)
    dve.wait_ge(ln, 5)


def rstd_act(nc, k, act, ln):
    act.wait_ge(ln, 3)
    nc.scalar.activation(k.std[:, :], k.var_eps[:, :], ACT.Sqrt).then_inc(ln, 1)


def normalise(nc, k, out, t):
    return nc.vector.tensor_scalar(out, at(k.x, t), k.mean[:, bass.ds(t, 1)], k.rstd[:, bass.ds(t, 1)],
                                   ALU.subtract, ALU.mult)


def stage_xattn(nc, k, name, w, ctx_t, ctx_k, ctx_l, last_mask, scratch):
    first = name == "l0"
    with ExitStack() as ctx:
        sb = lambda n, s: ctx.enter_context(nc.sbuf_tensor(f"{name}_{n}", s, F32))
        sem = lambda n: k.sem(f"{name}_{n}")
        A = sb("A", [P, H, CA])
        U = sb("U", [CA, H, D])
        qbias = sb("qbias", [CA, H])
        bo = sb("bo", [P, D])
        W = sb("W", [B, H, D])
        w_in = sem("w_in")
        ps = k.ps

        with ExitStack() as prep:
            psb = lambda n, s: prep.enter_context(nc.sbuf_tensor(f"{name}_{n}", s, F32))
            psem = lambda n: k.sem(f"{name}_{n}")
            made = psem("made")
            moved = psem("moved")
            masked = psem("masked")
            u_sb = psem("u_sb")
            ctxl = psb("ctxl", [CA, B])
            if first:
                wqT, wkT = psb("wqT", [P, H // 2, D]), psb("wkT", [P, H // 2, CA])
                wvT, wo = psb("wvT", [P, H // 2, CA]), psb("wo", [P, H // 2, D])
                scale = DH0 ** -0.5
                loads = [(wqT, w["wqT"]), (wkT, w["wkT"]), (wvT, w["wvT"]), (wo, w["wo"])]
            else:
                wqT, kaT, vaT, wo = psb("wqT", [P, D]), psb("kaT", [P, CA]), psb("vaT", [P, CA]), psb("wo", [P, D])
                hm, qb = psb("hm", [P, H]), psb("qb", [P, 1])
                kam, vam, qbm = psb("kam", [P, H, CA]), psb("vam", [P, H, CA]), psb("qbm", [P, H])
                scale = DH1 ** -0.5
                loads = [(wqT, w["wqT"]), (kaT, w["kaT"]), (vaT, w["vaT"]), (wo, w["wo"]),
                         (hm, w["head_mask"]), (qb, w["qb"])]
            block = prep.enter_context(nc.Block())

            @block.sync
            def _(sp):
                for dst, src in loads + [(bo, w["bo"]), (ctxl, ctx_l)]:
                    sp.dma_start(dst[:], src).then_inc(w_in, 16)
                sp.wait_ge(w_in, 16 * (len(loads) + 2))

            @block.vector
            def _(dve):
                if first:
                    nc.vector.memset(qbias[:, :], 0.0).then_inc(masked, 1)
                else:
                    dve.wait_ge(w_in, 16 * (len(loads) + 2))
                    for dst, src in ((kam, kaT), (vam, vaT)):
                        nc.vector.tensor_tensor(dst[:, :, :], src[:, None, :].to_broadcast([P, H, CA]),
                                                hm[:, :, None].to_broadcast([P, H, CA]),
                                                ALU.mult).then_inc(masked, 1)
                    nc.vector.tensor_scalar(qbm[:, :], hm[:, :], qb[:, 0:1], None, ALU.mult).then_inc(masked, 1)

            @block.tensor
            def _(pe):
                pe.wait_ge(w_in, 16 * (len(loads) + 2))
                if first:
                    for h in range(H):
                        c, r = h // 2, 64 * (h % 2)
                        bank = 2 * (h % 2) + c // 4
                        last = nc.tensor.matmul(ps[:, bank, (c % 4) * P:(c % 4) * P + CA], wqT[r:r + 64, c, :],
                                                wkT[r:r + 64, c, :], start=True, stop=True)
                    last.then_inc(made, 1)
                    for h in range(H):
                        c, r = h // 2, 64 * (h % 2)
                        bank = 4 + 2 * (h % 2) + c // 4
                        last = nc.tensor.matmul(ps[0:CA, bank, (c % 4) * P:(c % 4) * P + P], wvT[r:r + 64, c, :],
                                                wo[r:r + 64, c, :], start=True, stop=True)
                    last.then_inc(made, 1)
                else:
                    pe.wait_ge(masked, 3)
                    for g in range(4):
                        last = nc.tensor.matmul(ps[:, g, 0:HG * CA], wqT[:, :], kam[:, HG * g:HG * g + HG, :],
                                                start=True, stop=True)
                    last.then_inc(made, 1)
                    for h in range(H):
                        last = nc.tensor.matmul(ps[0:CA, 4 + h // 4, (h % 4) * P:(h % 4) * P + P], vam[:, h, :],
                                                wo[:, :], start=True, stop=True)
                    last.then_inc(made, 1)
                    pe.wait_ge(moved, 1)
                    nc.tensor.matmul(ps[0:CA, 0, 0:H], kaT[:, :], qbm[:, :], start=True, stop=True).then_inc(made, 1)
                pe.wait_ge(u_sb, 4)
                for g in range(4):
                    last = nc.tensor.matmul(ps[:, 4 + g, :], ctxl[:, :], U[:, HG * g:HG * g + HG, :],
                                            start=True, stop=True)
                last.then_inc(made, 1)

            @block.scalar
            def _(act):
                act.wait_ge(made, 1)
                if first:
                    for par in range(2):
                        for g in range(2):
                            nc.scalar.mul(A[:, 8 * g + par:8 * g + 8:2, :],
                                          ps[:, 2 * par + g, :].rearrange("p (c n) -> p c n", c=4)[:, :, 0:CA], scale)
                else:
                    for g in range(4):
                        last = nc.scalar.mul(A[:, HG * g:HG * g + HG, :], ps[:, g, 0:HG * CA].rearrange(
                            "p (c n) -> p c n", c=4), scale)
                    last.then_inc(moved, 1)
                act.wait_ge(made, 2)
                for par in range(2):
                    for g in range(2):
                        if first:
                            nc.scalar.copy(U[:, 8 * g + par:8 * g + 8:2, :],
                                           ps[0:CA, 4 + 2 * par + g, :].rearrange("p (c n) -> p c n", c=4)
                                           ).then_inc(u_sb, 1)
                        else:
                            nc.scalar.copy(U[:, 4 * (2 * par + g):4 * (2 * par + g) + 4, :],
                                           ps[0:CA, 4 + 2 * par + g, :].rearrange("p (c n) -> p c n", c=4)
                                           ).then_inc(u_sb, 1)
                if not first:
                    act.wait_ge(made, 3)
                    nc.scalar.mul(qbias[:, :], ps[0:CA, 0, 0:H], scale)
                act.wait_ge(made, 3 if first else 4)
                for g in range(4):
                    nc.scalar.copy(W[:, HG * g:HG * g + HG, :], ps[:, 4 + g, :].rearrange("p (c n) -> p c n", c=HG))

        ctxT = sb("ctxT", [CA, 2, SEQ * NK])
        ctxK = sb("ctxK", [P, 2, SEQ * 2 * CA])
        xn = sb("xn", [P, D])
        xnT = sb("xnT", [P, P])
        q1 = sb("q1", [CA, 2, HG, SEQ, HG * N])
        probs = sb("probs", [P, 2, HG, NK])
        nmax = sb("nmax", [P, 2, HG])
        den = sb("den", [P, 2, HG])
        rden = sb("rden", [P, 2, HG])
        pT = sb("pT", [P, 2, HG * P])
        last_p = sb("last_p", [P, N])
        last_pT = sb("last_pT", [P, N])
        last_bd = sb("last_bd", [P, 2, SEQ, N])
        last_m = sb("last_m", [P, SEQ])
        last_w = sb("last_w", [P, T, D])
        oT = sb("oT", [CA, 2, H, SEQ, N])
        S_B, T_B, A_B, O_B = 0, 4, 6, 7

        ln, xn_ok, xt_mm, xt_sb = sem("ln"), sem("xn_ok"), sem("xt_mm"), sem("xt_sb")
        q_mm, q_sb, s_mm, nm_ok = sem("q_mm"), sem("q_sb"), sem("s_mm"), sem("nm_ok")
        exp_ok, norm_ok, t_mm = sem("exp_ok"), sem("norm_ok"), sem("t_mm")
        pt_a, pt_v, o_mm, o_sb = sem("pt_a"), sem("pt_v"), sem("o_mm"), sem("o_sb")
        out_mm, x_ok, steps, last_ok = sem("out_mm"), sem("x_ok"), sem("steps"), sem("last_ok")
        m_in, cleared, w_out, lw_in = sem("m_in"), sem("cleared"), sem("w_out"), sem("lw_in")
        ctx_in = [sem("ctx_in0"), sem("ctx_in1")]
        block = ctx.enter_context(nc.Block())

        def tiles(eng, tile):
            tile(0, 0, 1, first=True)
            with eng.Fori(0, (T - 4) // 2) as i:
                tile(2 * i + 1, 1, i + 2)
                tile(2 * i + 2, 0, i + 2)
            tile(T - 3, 1, T // 2)
            tile(T - 2, 0, T // 2, x_after=False)
            tile(T - 1, 1, None, x_after=False, last=True)

        @block.sync
        def _(sp):
            def load(t, j):
                for dst, src in ((ctxT, ctx_t), (ctxK, ctx_k)):
                    sp.dma_start(dst[:, j, :], src[bass.ds(t, 1), :, :].rearrange(
                        "t c n -> c (t n)")).then_inc(ctx_in[j], 16)

            load(0, 0)
            sp.dma_start(last_m[:, :], last_mask).then_inc(m_in, 16)
            sp.dma_start(scratch, W[:, :, :].rearrange("p h d -> p (h d)")).then_inc(w_out, 16)
            load(1, 1)
            sp.wait_ge(w_out, 16)
            sp.wait_ge(cleared, 1)
            for h4 in range(HG):
                for b in range(SEQ):
                    row = N * h4 + HG * b
                    sp.dma_start(last_w[row:row + HG, :, :],
                                 scratch.rearrange("(t b) (g h d) -> b h g t d", b=SEQ, g=HG, h=HG)[b, h4]
                                 ).then_inc(lw_in, 16)
            with sp.Fori(1, T // 2) as i:
                for j in range(2):
                    sp.wait_ge(o_mm, 4 * (2 * i + j) - 4)
                    load(2 * i + j, j)

        @block.tensor
        def _(pe):
            def turn_x(t):
                pe.wait_ge(xn_ok, t + 1)
                nc.tensor.transpose(ps[:, T_B + 1, 0:P], xn[:, :], k.ident[:, :]).then_inc(xt_mm, 1)

            def queries(hg):
                for h in range(HG):
                    last_i = nc.tensor.matmul(ps[0:CA, T_B, h * P:h * P + P], A[:, HG * hg + h, :], xnT[:, :],
                                              start=True, stop=True)
                last_i.then_inc(q_mm, 1)

            def scores(b, j, after):
                for hg in range(HG):
                    if after is not None:
                        pe.wait_ge(exp_ok, 4 * after + hg + 1)
                    last_i = nc.tensor.matmul(ps[:, S_B + hg, 0:NK], q1[:, j, hg, b, :],
                                              ctxT[:, j, b * NK:b * NK + NK], start=True, stop=True)
                    if hg % 2:
                        last_i.then_inc(s_mm, 1)

            def sum_heads(b, j, t):
                if b == 0:
                    pe.wait_ge(o_sb, 4 * t + 5)
                    pe.wait_ge(x_ok, t + 1)
                for h in range(HG * b, HG * b + HG):
                    nc.tensor.matmul(ps[:, A_B, 0:D], oT[:, j, h, :, :].rearrange("c b n -> c (b n)"), U[:, h, :],
                                     start=h == 0, stop=False)
                if b == SEQ - 1:
                    pe.wait_ge(last_ok, t + 1)
                    pe.nop(nofuse=True)
                    nc.tensor.matmul(ps[:, A_B, 0:D], last_bd[:, j, :, :].rearrange("p b n -> p (b n)"),
                                     at(last_w, t), start=False, stop=True).then_inc(out_mm, 1)

            def tile(t, j, fills, first=False, x_after=True, last=False):
                for b in range(SEQ):
                    u = 4 * t + b
                    if b < SEQ - 1:
                        scores(b + 1, j, u)
                    elif not last:
                        pe.wait_ge(q_sb, 4 * t + 8)
                        pe.wait_ge(ctx_in[1 - j], 32 * fills)
                        scores(0, 1 - j, u)
                    pe.wait_ge(norm_ok, u + 1)
                    if not last:
                        pe.wait_ge(q_sb, u + 5)
                    if b == SEQ - 1 and x_after:
                        pe.wait_ge(xt_sb, t + 3)
                    for kt in range(2):
                        for hg in range(HG):
                            last_i = nc.tensor.transpose(ps[:, T_B + kt, hg * P:hg * P + P],
                                                         probs[:, b % 2, hg, kt * P:kt * P + P], k.ident[:, :])
                    last_i.then_inc(t_mm, 1)
                    if not first:
                        sum_heads(b, 1 - j, t - 1)
                    pe.wait_ge(pt_a, u + 1)
                    pe.wait_ge(pt_v, u + 1)
                    pe.wait_ge(o_sb, u + 1)
                    for kt in range(2):
                        at_k = (b * 2 + kt) * CA
                        last_i = nc.tensor.matmul(ps[0:CA, O_B, :], ctxK[:, j, at_k:at_k + CA], pT[:, kt, :],
                                                  start=kt == 0, stop=kt == 1)
                    last_i.then_inc(o_mm, 1)
                    if b < SEQ - 1 and not last:
                        queries(b + 1)
                    elif x_after:
                        queries(0)
                    if b == SEQ - 2 and x_after:
                        turn_x(t + 2)

            turn_x(0)
            pe.wait_ge(xt_sb, 1)
            for hg in range(HG):
                if hg:
                    pe.wait_ge(q_sb, hg)
                queries(hg)
            turn_x(1)
            pe.wait_ge(q_sb, HG)
            pe.wait_ge(ctx_in[0], 32)
            scores(0, 0, None)
            pe.wait_ge(xt_sb, 2)
            queries(0)
            pe.wait_ge(lw_in, 16 * HG * SEQ)
            tiles(pe, tile)
            for b in range(SEQ):
                sum_heads(b, (T - 1) % 2, T - 1)

        @block.vector
        def _(dve):
            def queries(n, j, hg):
                dve.wait_ge(q_mm, n + 1)
                nc.vector.tensor_tensor(q1[:, j, hg, :, :].rearrange("c b (h n) -> c h b n", h=HG),
                                        ps[0:CA, T_B, :].rearrange("c (h b n) -> c h b n", h=HG, b=SEQ),
                                        qbias[:, HG * hg:HG * hg + HG, None, None].to_broadcast([CA, HG, SEQ, N]),
                                        ALU.add).then_inc(q_sb, 1)

            def maxima(u, par):
                for half in range(2):
                    dve.wait_ge(s_mm, 2 * u + half + 1)
                    nc.vector.tensor_reduce(nmax[:, par, 2 * half:2 * half + 2],
                                            ps[:, S_B + 2 * half:S_B + 2 * half + 2, 0:NK], AX.X, ALU.max,
                                            negate=True).then_inc(nm_ok, 1)

            def divide(u, b):
                par = b % 2
                dve.wait_ge(exp_ok, 4 * u + 4)
                chain.done(nc.vector.reciprocal(rden[:, par, :], den[:, par, :]))
                nc.vector.tensor_tensor(last_p[:, HG * b:HG * b + HG], probs[:, par, :, NK - 1], rden[:, par, :],
                                        ALU.mult)
                for hg in range(HG):
                    pr = probs[:, par, hg, 0:NK - 1]
                    last_i = nc.vector.tensor_scalar(pr, pr, rden[:, par, hg:hg + 1], None, ALU.mult)
                last_i.then_inc(norm_ok, 1)

            def residual(t):
                dve.wait_ge(out_mm, t + 1)
                add_to_x_and_count(nc, k, chain, t, ps[:, A_B, 0:D], bo[:, :]).then_inc(x_ok, 1)

            def tile(t, j, fills, first=False, x_after=True, last=False):
                chain.tile(1 if first else 8 * t - 1)
                for b in range(SEQ):
                    u = 4 * t + b
                    if b < SEQ - 1 or not last:
                        maxima(u + 1, (b + 1) % 2)
                    dve.wait_ge(t_mm, u + 1)
                    nc.vector.tensor_copy(pT[:, 1, :], ps[:, T_B + 1, :]).then_inc(pt_v, 1)
                    if b == SEQ - 1:
                        chain.done(nc.vector.transpose(last_pT[:, :], last_p[:, :]))
                        chain.done(nc.vector.tensor_tensor(last_bd[:, j, :, :],
                                                           last_pT[:, None, :].to_broadcast([P, SEQ, N]),
                                                           last_m[:, :, None].to_broadcast([P, SEQ, N]), ALU.mult))
                        dve.sem_inc(last_ok, 1)
                    if b < SEQ - 1 or not last:
                        divide(u + 1, (b + 1) % SEQ)
                    if b == 1 and x_after:
                        normalise(nc, k, xn[:, :], t + 2).then_inc(xn_ok, 1)
                    if b < SEQ - 1 and not last:
                        queries(u + 5, 1 - j, b + 1)
                    elif x_after:
                        queries(u + 5, j, 0)
                    if b == SEQ - 1 and not first:
                        residual(t - 1)

            dve.sem_inc(x_ok, 1)
            nc.vector.memset(last_p[:, :], 0.0)
            rstd_dve(nc, k, dve, ln, EPS_LN)
            normalise(nc, k, xn[:, :], 0).then_inc(xn_ok, 1)
            chain = Chain(dve, steps, 1)
            for hg in range(HG):
                queries(hg, 0, hg)
            dve.wait_ge(xt_mm, 1)
            normalise(nc, k, xn[:, :], 1).then_inc(xn_ok, 1)
            maxima(0, 0)
            queries(HG, 1, 0)
            divide(0, 0)
            dve.wait_ge(m_in, 16)
            tiles(dve, tile)
            residual(T - 1)

        @block.scalar
        def _(act):
            def turned(t):
                act.wait_ge(xt_mm, t + 1)
                nc.scalar.copy(xnT[:, :], ps[:, T_B + 1, 0:P]).then_inc(xt_sb, 1)

            def exps(u, par):
                for hg in range(HG):
                    if hg % 2 == 0:
                        act.wait_ge(nm_ok, 2 * u + hg // 2 + 1)
                    nc.scalar.activation(probs[:, par, hg, :], ps[:, S_B + hg, 0:NK], ACT.Exp,
                                         bias=nmax[:, par, hg:hg + 1], accum_out=den[:, par, hg:hg + 1]
                                         ).then_inc(exp_ok, 1)

            def tile(t, j, fills, first=False, x_after=True, last=False):
                for b in range(SEQ):
                    u = 4 * t + b
                    if b < SEQ - 1 or not last:
                        exps(u + 1, (b + 1) % 2)
                    act.wait_ge(t_mm, u + 1)
                    nc.scalar.copy(pT[:, 0, :], ps[:, T_B, :]).then_inc(pt_a, 1)
                    act.wait_ge(o_mm, u + 1)
                    nc.scalar.copy(oT[:, j, :, b, :], ps[0:CA, O_B, :].rearrange("c (h n) -> c h n", h=H)
                                   ).then_inc(o_sb, 1)
                    if b == SEQ - 2 and x_after:
                        turned(t + 2)

            act.sem_inc(o_sb, 1)
            rstd_act(nc, k, act, ln)
            turned(0)
            turned(1)
            exps(0, 0)
            tiles(act, tile)

        @block.gpsimd
        def _(pool):
            nc.gpsimd.memset(last_w[:, :, :], 0.0).then_inc(cleared, 1)


def stage_performer(nc, k, w):
    HALF = 8 * DH0
    dn = float(DH0) ** -0.25
    with ExitStack() as ctx:
        sb = lambda n, s: ctx.enter_context(nc.sbuf_tensor(f"enc_{n}", s, F32))
        ps = k.ps
        res = sb("res", [P, T, D])
        negmx = sb("negmx", [P, 1])

        with ExitStack() as att:
            sb = lambda n, s: att.enter_context(nc.sbuf_tensor(f"enc_{n}", s, F32))
            sem = lambda n: k.sem(f"enc_{n}")
            wq, wk, wv = sb("wq", [P, H * DH0]), sb("wk", [P, H * DH0]), sb("wv", [P, H * DH0])
            pq, pk = sb("pq", [P, H * DH0]), sb("pk", [P, H * DH0])
            wo = sb("wo", [P, H // 2, D])
            blocks = sb("blocks", [P, P])
            mask = sb("mask", [P, P])
            ones = sb("ones", [1, P])

            with ExitStack() as prep:
                psb = lambda n, s: prep.enter_context(nc.sbuf_tensor(f"enc_{n}", s, F32))
                psem = lambda n: k.sem(f"enc_{n}")
                wqT, wkT, projT = psb("wqT", [P, H // 2, D]), psb("wkT", [P, H // 2, D]), psb("projT", [P, DH0])
                xn4 = psb("xn4", [P, 2, 4, D])
                xnT4 = psb("xnT4", [P, 2, 4 * P])
                tmp, acc = psb("tmp", [P, 2]), psb("acc", [P, 2])
                rowmax = psb("rowmax", [P, 1])
                allmax = psb("allmax", [1, 1])
                w_in, w_in2, made, moved, ln = psem("w_in"), psem("w_in2"), psem("made"), psem("moved"), psem("ln_a")
                xn_ok, xt_mm, xt_sb = psem("xn_ok_a"), psem("xt_mm_a"), psem("xt_sb_a")
                d_mm, max_ok, steps, fin = psem("d_mm"), psem("max_ok"), psem("steps_a"), psem("fin")
                block = prep.enter_context(nc.Block())
                loads = [(wqT, w["wqT"]), (wkT, w["wkT"]), (projT, w["projT"])]
                loads2 = [(wq, w["wq"]), (wk, w["wk"]), (wv, w["wv"]), (wo, w["wo"]), (blocks, w["blocks"]),
                          (mask, w["mask"])]

                @block.sync
                def _(sp):
                    for dst, src in loads:
                        sp.dma_start(dst[:], src).then_inc(w_in, 16)
                    for dst, src in loads2:
                        sp.dma_start(dst[:], src).then_inc(w_in2, 16)
                    sp.wait_ge(w_in2, 16 * len(loads2))

                @block.tensor
                def _(pe):
                    pe.wait_ge(w_in, 16 * len(loads))
                    for n, wT in ((0, wqT), (1, wkT)):
                        for h in range(H):
                            c, r = h // 2, 64 * (h % 2)
                            last = nc.tensor.matmul(ps[:, 2 * n + h % 2, c * DH0:c * DH0 + DH0], wT[r:r + 64, c, :],
                                                    projT[r:r + 64, :], start=True, stop=True)
                        last.then_inc(made, 1)
                    pe.wait_ge(moved, 2)
                    with pe.Fori(0, T // 8) as i:
                        for j in range(2):
                            g = 2 * i + j
                            pe.wait_ge(xn_ok, g + 1)
                            for n in range(4):
                                last = nc.tensor.transpose(ps[:, 4 + j, n * P:n * P + P], xn4[:, j, n, :], k.ident[:, :])
                            last.then_inc(xt_mm, 1)
                            pe.wait_ge(xt_sb, g + 1)
                            for s in range(4):
                                pe.wait_ge(max_ok, 4 * g + s + 1)
                                for c in range(2):
                                    last = nc.tensor.matmul(ps[:, 2 * (s % 2) + c, :],
                                                            pk[:, (2 * s + c) * P:(2 * s + c) * P + P], xnT4[:, j, :],
                                                            start=True, stop=True)
                                last.then_inc(d_mm, 1)
                    pe.wait_ge(fin, 1)
                    nc.tensor.transpose(ps[0:1, 6, 0:P], rowmax[:, :], k.ident[:, :]).then_inc(made, 1)
                    pe.wait_ge(fin, 2)
                    nc.tensor.matmul(ps[:, 7, 0:1], ones[:, :], allmax[:, :], start=True, stop=True).then_inc(made, 1)

                @block.vector
                def _(dve):
                    dve.sem_inc(max_ok, 2)
                    nc.vector.memset(ones[:, :], 1.0)
                    nc.vector.memset(acc[:, :], -3.0e38).then_inc(steps, 1)
                    dve.wait_ge(steps, 1)
                    rstd_dve(nc, k, dve, ln, EPS_LN)
                    
                    with dve.Fori(0, T // 8) as i:
                        for j in range(2):
                            g = 2 * i + j
                            for n in range(4):
                                last = normalise(nc, k, xn4[:, j, n, :], 4 * g + n)
                            last.then_inc(xn_ok, 1)
                            for s in range(4):
                                dve.wait_ge(d_mm, 4 * g + s + 1)
                                b = 2 * (s % 2)
                                nc.vector.tensor_reduce(tmp[:, :], ps[:, b:b + 2, :], AX.X, ALU.max).then_inc(max_ok, 1)
                                dve.wait_ge(max_ok, 4 * g + s + 3)
                                nc.vector.tensor_tensor(acc[:, :], acc[:, :], tmp[:, :], ALU.max).then_inc(steps, 1)
                                dve.wait_ge(steps, 4 * g + s + 2)
                    nc.vector.tensor_reduce(rowmax[:, :], acc[:, :], AX.X, ALU.max).then_inc(fin, 1)
                    dve.wait_ge(made, 3)
                    nc.vector.tensor_reduce(allmax[:, :], ps[0:1, 6, 0:P], AX.X, ALU.max, negate=True).then_inc(fin, 1)
                    dve.wait_ge(made, 4)
                    nc.vector.tensor_copy(negmx[:, :], ps[:, 7, 0:1])

                @block.scalar
                def _(act):
                    for n, dst in ((0, pq), (1, pk)):
                        act.wait_ge(made, n + 1)
                        for par in range(2):
                            last = nc.scalar.mul(dst[:, :].rearrange("p (c r m) -> p r c m", r=2, m=DH0)[:, par],
                                                 ps[:, 2 * n + par, :].rearrange("p (c m) -> p c m", m=DH0), dn)
                        last.then_inc(moved, 1)
                    rstd_act(nc, k, act, ln)
                    with act.Fori(0, T // 8) as i:
                        for j in range(2):
                            act.wait_ge(xt_mm, 2 * i + j + 1)
                            nc.scalar.copy(xnT4[:, j, :], ps[:, 4 + j, :]).then_inc(xt_sb, 1)

            xn, xr = sb("xn", [P, D]), sb("xr", [P, D])
            xnT = sb("xnT", [P, P])
            ksq, qsq = sb("ksq", [P, 1024]), sb("qsq", [P, 1024])
            eq, kf = sb("eq", [P, 1024]), sb("kf", [P, 1024])
            qfT = sb("qfT", [P, 1024])
            va = sb("va", [P, H, DH0 + 1])
            sm = sb("sm", [P, 4, 512])
            at_sb, atT = sb("at", [P, 1024]), sb("atT", [P, 1024])
            diag, mx, cc = sb("diag", [P, H]), sb("mx", [P, H]), sb("cc", [P, H])
            rden = sb("rden", [P, H])
            eps_col, eps_ok = sb("eps_col", [P, 1]), sem("eps_ok")
            FA, FB, RA, RB = 0, 2, 4, 6
            (xn_ok, xt_mm, xt_sb, k_mm, ksq_ok, q_mm, qsq_ok, dq_mm, sub_ok, eq_ok, dk_mm, kf_raw, kf_ok, v_mm, v_ok,
             qt_mm, qt_ok, s_mm, sm_ok, o_mm, at_ok, at_mm, atT_ok, wo_mm, res_ok, xr_ok, steps, steps_d) = [sem(n) for n in (
                 "xn_ok xt_mm xt_sb k_mm ksq_ok q_mm qsq_ok dq_mm sub_ok eq_ok dk_mm kf_raw kf_ok v_mm v_ok "
                 "qt_mm qt_ok s_mm sm_ok o_mm at_ok at_mm atT_ok wo_mm res_ok xr_ok steps steps_d").split()]
            block = att.enter_context(nc.Block())
            both = lambda pair: ps[:, pair:pair + 2, :].rearrange("p a b -> p (a b)")

            def feature_major(pair, wt, sem):
                for c in range(8):
                    last = nc.tensor.matmul(ps[:, pair + c // 4, (c % 4) * P:(c % 4) * P + P], wt[:, c * P:c * P + P],
                                            xnT[:, :], start=True, stop=True)
                last.then_inc(sem, 1)

            def token_major(pair, wt, sem):
                for c in range(2):
                    last = nc.tensor.matmul(ps[:, pair + c, :], xnT[:, :], wt[:, c * 512:c * 512 + 512],
                                            start=True, stop=True)
                last.then_inc(sem, 1)

            def pe_front(pe, t, part):
                if part == 0:
                    pe.wait_ge(xt_sb, t + 1)
                    feature_major(FA, wk, k_mm)
                elif part == 1:
                    token_major(FB, wq, q_mm)
                elif part == 2:
                    pe.wait_ge(ksq_ok, t + 1)
                    token_major(FA, pq, dq_mm)
                elif part == 3:
                    pe.wait_ge(qsq_ok, t + 1)
                    for c in range(8):
                        out = ps[:, FB + c // 4, (c % 4) * P:(c % 4) * P + P]
                        nc.tensor.matmul(out, pk[:, c * P:c * P + P], xnT[:, :], start=True, stop=False)
                        last = nc.tensor.matmul(out, blocks[:, :], ksq[:, c * P:c * P + P], start=False, stop=True)
                    last.then_inc(dk_mm, 1)
                else:
                    pe.wait_ge(sub_ok, t + 1)
                    token_major(FA, wv, v_mm)

            def pe_rear(pe, t, part, nxt=True):
                if part == 0:
                    pe.wait_ge(eq_ok, t + 1)
                    for c in range(8):
                        last = nc.tensor.transpose(ps[:, RA + c // 4, (c % 4) * P:(c % 4) * P + P],
                                                   eq[:, c * P:c * P + P], k.ident[:, :])
                    last.then_inc(qt_mm, 1)
                elif part in (1, 2):
                    if part == 1:
                        pe.wait_ge(kf_ok, t + 1)
                        pe.wait_ge(qt_ok, t + 1)
                    base = RB if part == 1 else RA
                    for n in range(4):
                        for par in range(2):
                            c, r = 4 * (part - 1) + n, 64 * par
                            last = nc.tensor.matmul(ps[:, base + par, n * P:n * P + P], kf[r:r + 64, c * P:c * P + P],
                                                    qfT[r:r + 64, c * P:c * P + P], start=True, stop=True)
                    last.then_inc(s_mm, 1)
                elif part == 3:
                    pe.wait_ge(v_ok, t + 1)
                    for half in range(2):
                        pe.wait_ge(sm_ok, 2 * t + half + 1)
                        if half:
                            pe.wait_ge(sm_ok, 2 * t + 2)
                        base = (RB, RA)[half]
                        for n in range(4):
                            for par in range(2):
                                h = 8 * half + 2 * n + par
                                last = nc.tensor.matmul(ps[:, base + par, n * 65:n * 65 + 65],
                                                        sm[:, 2 * half + par, n * P:n * P + P], va[:, h, :],
                                                        start=True, stop=True)
                        last.then_inc(o_mm, 1)
                elif part == 4:
                    pe.wait_ge(at_ok, 2 * t + 2)
                    for c in range(8):
                        last = nc.tensor.transpose(ps[:, RB + c // 4, (c % 4) * P:(c % 4) * P + P],
                                                   at_sb[:, c * P:c * P + P], k.ident[:, :])
                    last.then_inc(at_mm, 1)
                else:
                    pe.wait_ge(atT_ok, t + 1)
                    for c in range(8):
                        last = nc.tensor.matmul(ps[:, RA, 0:D], atT[:, c * P:c * P + P], wo[:, c, :],
                                                start=c == 0, stop=c == 7)
                    last.then_inc(wo_mm, 1)

            def pe_next_xT(pe, t):
                pe.wait_ge(xn_ok, t + 1)
                nc.tensor.transpose(ps[:, RA + 1, 0:P], xn[:, :], k.ident[:, :]).then_inc(xt_mm, 1)

            @block.tensor
            def _(pe):
                pe_next_xT(pe, 0)
                for part in range(5):
                    pe_front(pe, 0, part)
                pe_next_xT(pe, 1)

                def step(t, front=True, x_after=True):
                    if front:
                        pe.wait_ge(xt_sb, t + 2)
                    pe.wait_ge(res_ok, t + 1)
                    for part in range(5):
                        pe_rear(pe, t, part)
                        if front:
                            if part == 0:
                                pe.wait_ge(v_ok, t + 1)
                            if part == 1:
                                pe.wait_ge(kf_raw, t + 1)
                            pe_front(pe, t + 1, part)
                    pe_rear(pe, t, 5)
                    if x_after:
                        pe_next_xT(pe, t + 2)

                with pe.Fori(0, T - 2) as t:
                    step(t)
                step(T - 2, x_after=False)
                step(T - 1, front=False, x_after=False)

            @block.scalar
            def _(act):
                def front(t, part):
                    if part == 0:
                        act.wait_ge(k_mm, t + 1)
                        nc.scalar.activation(ksq[:, :], both(FA), ACT.Square).then_inc(ksq_ok, 1)
                    elif part == 1:
                        act.wait_ge(q_mm, t + 1)
                        nc.scalar.activation(qsq[:, :], both(FB), ACT.Square).then_inc(qsq_ok, 1)
                    elif part == 2:
                        act.wait_ge(sub_ok, t + 1)
                        nc.scalar.activation(eq[:, :], eq[:, :], ACT.Exp).then_inc(eq_ok, 1)
                    elif part == 3:
                        act.wait_ge(dk_mm, t + 1)
                        nc.scalar.activation(kf[:, :], both(FB), ACT.Exp, bias=negmx[:, 0:1]).then_inc(kf_raw, 1)
                    else:
                        act.wait_ge(v_mm, t + 1)
                        nc.scalar.copy(va[:, :, 0:DH0], both(FA).rearrange("p (h d) -> p h d", h=H)).then_inc(v_ok, 1)

                def x_next(t):
                    act.wait_ge(xt_mm, t + 1)
                    nc.scalar.copy(xnT[:, :], ps[:, RA + 1, 0:P]).then_inc(xt_sb, 1)

                def step(t, fr=True, x_after=True):
                    act.wait_ge(qt_mm, t + 1)
                    nc.scalar.activation(qfT[:, :], both(RA), ACT.Copy, bias=EPS_KERN).then_inc(qt_ok, 1)
                    if fr:
                        for part in range(4):
                            front(t + 1, part)
                    act.wait_ge(at_mm, t + 1)
                    nc.scalar.copy(atT[:, :], both(RB)).then_inc(atT_ok, 1)
                    if fr:
                        front(t + 1, 4)
                    if x_after:
                        x_next(t + 2)

                x_next(0)
                for part in range(5):
                    front(0, part)
                x_next(1)
                with act.Fori(0, T - 2) as t:
                    step(t)
                step(T - 2, x_after=False)
                step(T - 1, fr=False, x_after=False)

            @block.vector
            def _(dve):
                nc.vector.memset(va[:, :, DH0:DH0 + 1], 1.0)
                dve.sem_inc(res_ok, 1)
                q_steps, d_steps = Chain(dve, steps, 2), Chain(dve, steps_d, 2)
                heads = lambda ap: ap.rearrange("p (h d) -> p h d", h=H)

                def x_norm(t):
                    normalise(nc, k, xn[:, :], t).then_inc(xn_ok, 1)

                def front_q(t):
                    q_steps.tile(t)
                    dve.wait_ge(qsq_ok, t + 1)
                    nc.vector.tensor_reduce(diag[:, :], heads(qsq[:, :]), AX.X, ALU.add)
                    dve.wait_ge(dq_mm, t + 1)
                    q_steps.done(nc.vector.tensor_reduce(mx[:, :], heads(both(FA)), AX.X, ALU.max))
                    q_steps.done(nc.vector.scalar_tensor_tensor(cc[:, :], diag[:, :], dn * dn / 2, mx[:, :],
                                                                ALU.mult, ALU.add))
                    nc.vector.tensor_tensor(heads(eq[:, :]), heads(both(FA)),
                                            cc[:, :, None].to_broadcast([P, H, DH0]), ALU.subtract).then_inc(sub_ok, 1)

                def mask_s(t, half):
                    dve.wait_ge(s_mm, 2 * t + half + 1)
                    pair = (RB, RA)[half]
                    nc.vector.tensor_tensor(sm[:, 2 * half:2 * half + 2, :].rearrange("p a (n q) -> p (a n) q", q=P),
                                            ps[:, pair:pair + 2, :].rearrange("p a (n q) -> p (a n) q", q=P),
                                            mask[:, None, :].to_broadcast([P, 8, P]), ALU.mult).then_inc(sm_ok, 1)

                def divide(t, half):
                    dve.wait_ge(o_mm, 2 * t + half + 1)
                    pair = (RB, RA)[half]
                    for par in range(2):
                        src = ps[:, pair + par, 0:260].rearrange("p (n e) -> p n e", e=65)
                        rd = rden[:, 8 * half + 4 * par:8 * half + 4 * par + 4]
                        nc.vector.reciprocal(rd[:, :, None], src[:, :, 64:65]).then_inc(steps_d, 1)
                    dve.wait_ge(steps_d, 4 * t + 2 * half + 2)
                    for par in range(2):
                        src = ps[:, pair + par, 0:260].rearrange("p (n e) -> p n e", e=65)
                        rd = rden[:, 8 * half + 4 * par:8 * half + 4 * par + 4]
                        last = nc.vector.tensor_tensor(at_sb[:, 512 * half:512 * half + 512].rearrange(
                            "p (n r d) -> p r n d", r=2, d=DH0)[:, par], src[:, :, 0:64],
                            rd[:, :, None].to_broadcast([P, 4, DH0]), ALU.mult)
                    last.then_inc(at_ok, 1)

                def residual(t):
                    normalise(nc, k, xr[:, :], t).then_inc(xr_ok, 1)
                    dve.wait_ge(xr_ok, t + 1)
                    dve.wait_ge(wo_mm, t + 1)
                    nc.vector.tensor_tensor(at(res, t), ps[:, RA, 0:D], xr[:, :], ALU.add).then_inc(res_ok, 1)
                    dve.wait_ge(res_ok, t + 2)
                    nc.vector.nop(nofuse=True)
                    nc.vector.bn_stats(at(k.stats, t), at(res, t))

                def step(t, fr=True, x_after=True):
                    mask_s(t, 0)
                    mask_s(t, 1)
                    if fr:
                        front_q(t + 1)
                    if x_after:
                        dve.wait_ge(xt_mm, t + 2)
                        x_norm(t + 2)
                    divide(t, 0)
                    divide(t, 1)
                    residual(t)

                x_norm(0)
                front_q(0)
                dve.wait_ge(xt_mm, 1)
                x_norm(1)
                with dve.Fori(0, T - 2) as t:
                    step(t)
                step(T - 2, x_after=False)
                step(T - 1, fr=False, x_after=False)

            @block.gpsimd
            def _(pool):
                nc.gpsimd.memset(eps_col[:, :], EPS_KERN).then_inc(eps_ok, 1)
                pool.wait_ge(eps_ok, 1)
                with pool.Fori(0, T) as t:
                    pool.wait_ge(kf_raw, t + 1)
                    nc.gpsimd.tensor_tensor(kf[:, :], kf[:, :], eps_col[:, 0:1].to_broadcast([P, 1024]),
                                            ALU.add).then_inc(kf_ok, 1)

        with ExitStack() as net:
            sb = lambda n, s: net.enter_context(nc.sbuf_tensor(f"net_{n}", s, F32))
            sem = lambda n: k.sem(f"net_{n}")
            NF = FF // P
            PART = 4
            w1, w2, b1 = sb("w1", [P, FF]), sb("w2", [P, NF, D]), sb("b1", [P, NF])
            rows = sb("rows", [P, 5, D])
            out1 = sb("out1", [P, T, D])
            o1T = sb("o1T", [P, P])
            z, ez = sb("z", [P, 2, FF]), sb("ez", [P, FF])
            hT = sb("hT", [P, 2, FF])
            staged = sb("staged", [P, 2, D])
            stage_ok = sem("stage_ok")
            w_in, ln, n1, n2, o1_ok = sem("w_in"), sem("ln"), sem("n1"), sem("n2"), sem("o1_ok")
            tr_mm, tr_ok, h_mm, z_ok, e_ok, em_ok, h_ok, y_mm, y_ok, st_ok = [sem(n) for n in (
                "tr_mm tr_ok h_mm z_ok e_ok em_ok h_ok y_mm y_ok st_ok").split()]
            block = net.enter_context(nc.Block())
            loads = [(w1, w["w1"]), (w2, w["w2"]), (b1, w["b1"]), (rows, w["rows"])]

            @block.sync
            def _(sp):
                for dst, src in loads:
                    sp.dma_start(dst[:], src).then_inc(w_in, 16)
                sp.wait_ge(w_in, 16 * len(loads))

            @block.tensor
            def _(pe):
                pe.wait_ge(w_in, 16 * len(loads))

                def turn(t, j):
                    pe.wait_ge(stage_ok, t + 1)
                    nc.tensor.transpose(ps[:, 0, 0:P], staged[:, j, :], k.ident[:, :]).then_inc(tr_mm, 1)

                def up(t, j):
                    pe.wait_ge(tr_ok, t + 1)
                    for c in range(NF):
                        last = nc.tensor.matmul(ps[:, 2 + j, c * P:c * P + P], w1[:, c * P:c * P + P], o1T[:, :],
                                                start=True, stop=True)
                    last.then_inc(h_mm, 1)

                def down(t, j):
                    pe.wait_ge(h_ok, t + 1)
                    for c in range(NF):
                        last = nc.tensor.matmul(ps[:, 4 + j, 0:D], hT[:, j, c * P:c * P + P], w2[:, c, :],
                                                start=c == 0, stop=c == NF - 1)
                    last.then_inc(y_mm, 1)

                def part(i, last=False):
                    for n in range(PART):
                        t = PART * i + n
                        if n < PART - 1 or not last:
                            up(t + 1, (n + 1) % 2)
                        if n < PART - 2 or not last:
                            turn(t + 2, n % 2)
                        down(t, n % 2)

                turn(0, 0)
                up(0, 0)
                turn(1, 1)
                with pe.Fori(0, T // PART - 1) as i:
                    part(i)
                part(T // PART - 1, last=True)

            @block.vector
            def _(dve):
                rstd_dve(nc, k, dve, ln, EPS_ENC)
                with dve.Fori(0, T) as t:
                    nc.vector.tensor_scalar(at(res, t), at(res, t), k.mean[:, bass.ds(t, 1)], k.rstd[:, bass.ds(t, 1)],
                                            ALU.subtract, ALU.mult).then_inc(n1, 1)
                dve.wait_ge(w_in, 16 * len(loads))

                def exponent(t, j):
                    dve.wait_ge(h_mm, t + 1)
                    nc.vector.tensor_tensor(z[:, j, :].rearrange("p (c q) -> p c q", c=NF),
                                            ps[:, 2 + j, :].rearrange("p (c q) -> p c q", c=NF),
                                            b1[:, :, None].to_broadcast([P, NF, P]), ALU.add).then_inc(z_ok, 1)

                def elu(t, j):
                    dve.wait_ge(e_ok, t + 1)
                    nc.vector.tensor_scalar(ez[:, :], ez[:, :], 1.0, -1.0, ALU.min, ALU.add).then_inc(em_ok, 1)
                    dve.wait_ge(em_ok, t + 1)
                    nc.vector.scalar_tensor_tensor(hT[:, j, :], z[:, j, :], 0.0, ez[:, :], ALU.max, ALU.add).then_inc(h_ok, 1)

                def result(t, j):
                    dve.wait_ge(y_mm, t + 1)
                    nc.vector.tensor_tensor(at(res, t), ps[:, 4 + j, 0:D], at(res, t), ALU.add).then_inc(y_ok, 1)

                def count(t):
                    dve.wait_ge(y_ok, t + 1)
                    nc.vector.nop(nofuse=True)
                    nc.vector.bn_stats(at(k.stats, t), at(res, t))

                exponent(0, 0)
                elu(0, 0)
                dve.wait_ge(n2, 3 * T // PART)
                with dve.Fori(0, T // 2 - 1) as i:
                    for j in range(2):
                        t = 2 * i + j
                        exponent(t + 1, 1 - j)
                        result(t, j)
                        elu(t + 1, 1 - j)
                        count(t)
                exponent(T - 1, 1)
                result(T - 2, 0)
                elu(T - 1, 1)
                count(T - 2)
                result(T - 1, 1)
                count(T - 1)

            @block.scalar
            def _(act):
                rstd_act(nc, k, act, ln)

                def turn(t):
                    act.wait_ge(tr_mm, t + 1)
                    nc.scalar.copy(o1T[:, :], ps[:, 0, 0:P]).then_inc(tr_ok, 1)

                def expo(t, j):
                    act.wait_ge(z_ok, t + 1)
                    nc.scalar.activation(ez[:, :], z[:, j, :], ACT.Exp).then_inc(e_ok, 1)

                def stage(t, j, part):
                    act.wait_ge(o1_ok, part + 1)
                    act.nop(nofuse=True)
                    nc.scalar.copy(staged[:, j, :], at(out1, t)).then_inc(stage_ok, 1)

                def part(i, last=False):
                    for n in range(PART):
                        t = PART * i + n
                        if n < PART - 2 or not last:
                            turn(t + 2)
                        if not last:
                            stage(t + PART, n % 2, i + 1)
                        if n < PART - 1 or not last:
                            expo(t + 1, (n + 1) % 2)

                stage(0, 0, 0)
                stage(1, 1, 0)
                turn(0)
                stage(2, 0, 0)
                turn(1)
                stage(3, 1, 0)
                expo(0, 0)
                with act.Fori(0, T // PART - 1) as i:
                    part(i)
                part(T // PART - 1, last=True)

            @block.gpsimd
            def _(pool):
                pool.wait_ge(w_in, 16 * len(loads))
                wide = [P, PART, D]
                for i in range(T // PART):
                    o, r = [a[:, PART * i:PART * i + PART, :] for a in (out1, res)]
                    pool.wait_ge(n1, PART * i + PART)
                    nc.gpsimd.tensor_tensor(o, r, rows[:, 0:1, :].to_broadcast(wide), ALU.mult).then_inc(n2, 1)
                    pool.wait_ge(n2, 3 * i + 1)
                    nc.gpsimd.tensor_tensor(o, o, rows[:, 1:2, :].to_broadcast(wide), ALU.add).then_inc(n2, 1)
                    pool.wait_ge(n2, 3 * i + 2)
                    pool.sem_inc(o1_ok, 1)
                    nc.gpsimd.tensor_tensor(r, o, rows[:, 2:3, :].to_broadcast(wide), ALU.add).then_inc(n2, 1)
                for i in range(T // PART):
                    xs = k.x[:, PART * i:PART * i + PART, :]
                    nc.gpsimd.tensor_tensor(xs, xs, rows[:, 4:5, :].to_broadcast(wide), ALU.add)

        with ExitStack() as end:
            sem = lambda n: k.sem(f"fin_{n}")
            rows = end.enter_context(nc.sbuf_tensor("fin_rows", [P, 5, D], F32))
            w_in, ln, sub, gained, st = sem("w_in"), sem("ln"), sem("sub"), sem("gained"), sem("st")
            block = end.enter_context(nc.Block())
            PARTS = 8
            TP = T // PARTS

            @block.sync
            def _(sp):
                sp.dma_start(rows[:, :, :], w["rows"]).then_inc(w_in, 16)
                sp.wait_ge(w_in, 16)

            @block.scalar
            def _(act):
                rstd_act(nc, k, act, ln)

            @block.gpsimd
            def _(pool):
                pool.wait_ge(w_in, 16)
                for n in range(PARTS):
                    r = res[:, n * TP:n * TP + TP, :]
                    pool.wait_ge(sub, n * TP + TP)
                    nc.gpsimd.tensor_tensor(r, r, rows[:, 3:4, :].to_broadcast([P, TP, D]), ALU.mult).then_inc(gained, 1)

            @block.vector
            def _(dve):
                rstd_dve(nc, k, dve, ln, EPS_ENC)
                with dve.Fori(0, T) as t:
                    nc.vector.tensor_scalar(at(res, t), at(res, t), k.mean[:, bass.ds(t, 1)], k.rstd[:, bass.ds(t, 1)],
                                            ALU.subtract, ALU.mult).then_inc(sub, 1)

                def counts(n):
                    dve.wait_ge(st, n + 1)
                    for t in range(n * TP, n * TP + TP):
                        nc.vector.bn_stats(k.stats[:, t, :], k.x[:, t, :])

                for n in range(PARTS):
                    s = slice(n * TP, n * TP + TP)
                    dve.wait_ge(gained, n + 1)
                    nc.vector.tensor_tensor(k.x[:, s, :], k.x[:, s, :], res[:, s, :], ALU.add).then_inc(st, 1)
                    if n:
                        counts(n - 1)
                counts(PARTS - 1)


def ranked_mask(nc, dve, count, s, gt, eq, lower, mask, n, keep, base):
    shape = [P, T, n, n]
    mine, other = s[:, :, :, None].to_broadcast(shape), s[:, :, None, :].to_broadcast(shape)
    nc.vector.tensor_tensor(gt, other, mine, ALU.is_gt)
    nc.vector.tensor_tensor(eq, other, mine, ALU.is_equal).then_inc(count, 1)
    dve.wait_ge(count, base + 1)
    nc.vector.tensor_tensor(eq, eq, lower[:, None, :, :].to_broadcast(shape), ALU.mult).then_inc(count, 1)
    dve.wait_ge(count, base + 2)
    nc.vector.tensor_tensor(gt, gt, eq, ALU.add).then_inc(count, 1)
    dve.wait_ge(count, base + 3)
    nc.vector.tensor_reduce(mask, gt, AX.X, ALU.add).then_inc(count, 1)
    dve.wait_ge(count, base + 4)
    nc.vector.tensor_scalar(mask, mask, float(keep), None, ALU.is_lt).then_inc(count, 1)
    dve.wait_ge(count, base + 5)


def router_logits(nc, k, ctx, name, gate, gate_in, n_experts, logits, sb, sem):
    xn, xnT = sb("xn_r", [P, 2, D]), sb("xnT_r", [P, 2, P])
    xn_ok, xt_mm, xt_sb, lg_mm = sem("xn_ok_r"), sem("xt_mm_r"), sem("xt_sb_r"), sem("lg_mm")
    ps = k.ps

    def tensor(pe):
        pe.sem_inc(xt_mm, 2)
        pe.sem_inc(lg_mm, 2)
        with pe.Fori(0, T // 2) as i:
            for j in range(2):
                pe.wait_ge(xn_ok, 2 * i + j + 1)
                nc.tensor.transpose(ps[:, j, 0:P], xn[:, j, :], k.ident[:, :]).then_inc(xt_mm, 1)
            for j in range(2):
                pe.wait_ge(xt_sb, 2 * i + j + 1)
                nc.tensor.matmul(logits[:, bass.ds((2 * i + j) * n_experts, n_experts)], xnT[:, j, :], gate,
                                 start=True, stop=True).then_inc(lg_mm, 1)

    def vector(dve):
        with dve.Fori(0, T // 2) as i:
            for j in range(2):
                dve.wait_ge(xt_mm, 2 * i + j + 1)
                normalise(nc, k, xn[:, j, :], 2 * i + j).then_inc(xn_ok, 1)

    def scalar(act):
        with act.Fori(0, T // 2) as i:
            for j in range(2):
                act.wait_ge(xt_mm, 2 * i + j + 3)
                act.wait_ge(lg_mm, 2 * i + j + 1)
                nc.scalar.copy(xnT[:, j, :], ps[:, j, 0:P]).then_inc(xt_sb, 1)

    return tensor, vector, scalar, lg_mm


def stage_moe0(nc, k, w):
    ED = E0 * D
    with ExitStack() as ctx:
        sb = lambda n, s: ctx.enter_context(nc.sbuf_tensor(f"m0_{n}", s, F32))
        ps = k.ps
        score, mask = sb("score", [P, T, E0]), sb("mask", [P, T, E0])
        gain = sb("gain", [P, T, E0])
        w1, w2, w3 = sb("w1", [P, ED]), sb("w2", [P, ED]), sb("w3", [P, ED])
        b1, b2, b3 = sb("b1", [P, ED]), sb("b2", [P, ED]), sb("b3", [P, ED])
        sw12, sw3 = sb("sw12", [P, 4 * P]), sb("sw3", [P, 2, D])
        loads = [(w1, w["w1"]), (w2, w["w2"]), (w3, w["w3"]), (b1, w["b1"]), (b2, w["b2"]), (b3, w["b3"]),
                 (sw12, w["sw12"]), (sw3, w["sw3"])]

        with ExitStack() as r:
            rsb = lambda n, s: r.enter_context(nc.sbuf_tensor(f"m0_{n}", s, F32))
            rsem = lambda n: k.sem(f"m0_{n}")
            gate, lower = rsb("gate", [P, E0]), rsb("lower", [P, E0, E0])
            lg, mx = rsb("lg", [P, T, E0]), rsb("mx", [P, T])
            gt, eq = rsb("gt", [P, T, E0, E0]), rsb("eq", [P, T, E0, E0])
            g_in, w_in, ln, st, ex = rsem("g_in"), rsem("w_in"), rsem("ln"), rsem("st"), rsem("ex")
            logits = ps[:, 4, :]
            tensor, vector, scalar, lg_mm = router_logits(nc, k, r, "m0", gate[:, :], g_in, E0, logits, rsb, rsem)
            block = r.enter_context(nc.Block())

            @block.sync
            def _(sp):
                sp.dma_start(gate[:, :], w["gate"]).then_inc(g_in, 16)
                sp.dma_start(lower[:, :, :], w["lower"]).then_inc(g_in, 16)
                for dst, src in loads:
                    sp.dma_start(dst[:], src).then_inc(w_in, 16)
                sp.wait_ge(g_in, 32)
                sp.wait_ge(w_in, 16 * len(loads))

            @block.tensor
            def _(pe):
                pe.wait_ge(g_in, 32)
                tensor(pe)

            @block.scalar
            def _(act):
                rstd_act(nc, k, act, ln)
                scalar(act)
                act.wait_ge(st, 2)
                nc.scalar.activation(lg[:, :, :], lg[:, :, :], ACT.Exp).then_inc(ex, 1)

            @block.vector
            def _(dve):
                rstd_dve(nc, k, dve, ln, EPS_LN)
                vector(dve)
                wide = [P, T, E0]
                dve.wait_ge(lg_mm, T + 2)
                all_lg = logits[:, 0:T * E0].rearrange("p (t e) -> p t e", e=E0)
                nc.vector.tensor_reduce(mx[:, :], all_lg, AX.X, ALU.max).then_inc(st, 1)
                dve.wait_ge(st, 1)
                nc.vector.tensor_tensor(lg[:, :, :], all_lg, mx[:, :, None].to_broadcast(wide),
                                        ALU.subtract).then_inc(st, 1)
                dve.wait_ge(ex, 1)
                nc.vector.tensor_reduce(mx[:, :], lg[:, :, :], AX.X, ALU.add).then_inc(st, 1)
                dve.wait_ge(st, 3)
                nc.vector.reciprocal(mx[:, :], mx[:, :]).then_inc(st, 1)
                dve.wait_ge(st, 4)
                nc.vector.tensor_tensor(score[:, :, :], lg[:, :, :], mx[:, :, None].to_broadcast(wide),
                                        ALU.mult).then_inc(st, 1)
                dve.wait_ge(st, 5)
                dve.wait_ge(g_in, 32)
                ranked_mask(nc, dve, st, score, gt[:, :, :, :], eq[:, :, :, :], lower, mask[:, :, :], E0, 2, 5)
                nc.vector.tensor_tensor(gain[:, :, :], mask[:, :, :], score[:, :, :], ALU.mult)

        with ExitStack() as m:
            sb = lambda n, s: m.enter_context(nc.sbuf_tensor(f"m0_{n}", s, F32))
            sem = lambda n: k.sem(f"m0_{n}")
            xn, xnT = sb("xn", [P, D]), sb("xnT", [P, P])
            z, hT, g3, mb3, x2 = sb("z", [P, ED]), sb("hT", [P, ED]), sb("g3", [P, ED]), sb("mb3", [P, ED]), sb("x2", [P, ED])
            sa, sh, y = sb("sa", [P, 2 * P]), sb("sh", [P, 2 * P]), sb("y", [P, D])
            (xn_ok, xt_mm, xt_sb, h1_mm, z_raw, z_ok, h_ok, ht_mm, ht_ok, x3_mm, g3_raw, g3_ok, x2_mm, x2_ok, up_mm, sa_ok,
             sh_ok, zo_mm, x_ok, steps, mb3_ok) = [sem(n) for n in (
                 "xn_ok xt_mm xt_sb h1_mm z_raw z_ok h_ok ht_mm ht_ok x3_mm g3_raw g3_ok x2_mm x2_ok up_mm sa_ok "
                 "sh_ok zo_mm x_ok steps mb3_ok").split()]
            H1, X3, HT, UP, XT = 0, 2, 4, 6, 7
            both = lambda pair: ps[:, pair:pair + 2, :].rearrange("p a b -> p (a b)")
            ex = lambda ap: ap.rearrange("p (e d) -> p e d", e=E0)
            col = lambda a, t: at(a, t)[:, :, None].to_broadcast([P, E0, D])
            block = m.enter_context(nc.Block())

            @block.tensor
            def _(pe):
                def turn(t):
                    pe.wait_ge(xn_ok, t + 1)
                    nc.tensor.transpose(ps[:, XT, 0:P], xn[:, :], k.ident[:, :]).then_inc(xt_mm, 1)

                def wide(pair, wt, s):
                    for c in range(2):
                        last = nc.tensor.matmul(ps[:, pair + c, :], xnT[:, :], wt[:, 512 * c:512 * c + 512],
                                                start=True, stop=True)
                    last.then_inc(s, 1)

                def shared_up():
                    for c in range(4):
                        last = nc.tensor.matmul(ps[:, UP, c * P:c * P + P], sw12[:, c * P:c * P + P], xnT[:, :],
                                                start=True, stop=True)
                    last.then_inc(up_mm, 1)

                def step(t, nxt=True):
                    pe.wait_ge(x_ok, t + 1)
                    if nxt:
                        turn(t + 1)
                    pe.wait_ge(h_ok, t + 1)
                    for e in range(E0):
                        last = nc.tensor.transpose(ps[:, HT + e // 4, (e % 4) * P:(e % 4) * P + P],
                                                   z[:, e * P:e * P + P], k.ident[:, :])
                    last.then_inc(ht_mm, 1)
                    if nxt:
                        pe.wait_ge(xt_sb, t + 2)
                    pe.wait_ge(sh_ok, t + 1)
                    for c in range(2):
                        last = nc.tensor.matmul(ps[:, XT, P:P + D], sh[:, c * P:c * P + P], sw3[:, c, :],
                                                start=c == 0, stop=c == 1)
                    last.then_inc(zo_mm, 1)
                    if nxt:
                        wide(H1, w1, h1_mm)
                        shared_up()
                    pe.wait_ge(ht_ok, t + 1)
                    for e in range(E0):
                        last = nc.tensor.matmul(ps[:, HT + e // 4, (e % 4) * P:(e % 4) * P + P],
                                                hT[:, e * P:e * P + P], w2[:, e * D:e * D + D], start=True, stop=True)
                    last.then_inc(x2_mm, 1)
                    if nxt:
                        pe.wait_ge(g3_raw, t + 1)
                        wide(X3, w3, x3_mm)

                turn(0)
                pe.wait_ge(xt_sb, 1)
                wide(H1, w1, h1_mm)
                shared_up()
                wide(X3, w3, x3_mm)
                with pe.Fori(0, T - 1) as t:
                    step(t)
                step(T - 1, nxt=False)

            @block.scalar
            def _(act):
                def turn(t):
                    act.wait_ge(xt_mm, t + 1)
                    nc.scalar.copy(xnT[:, :], ps[:, XT, 0:P]).then_inc(xt_sb, 1)

                def silus(t):
                    act.wait_ge(up_mm, t + 1)
                    nc.scalar.activation(sa[:, :], ps[:, UP, 0:2 * P], ACT.Silu).then_inc(sa_ok, 1)
                    act.wait_ge(z_ok, t + 1)
                    nc.scalar.activation(z[:, :], z[:, :], ACT.Silu).then_inc(h_ok, 1)

                def step(t, nxt=True):
                    if nxt:
                        turn(t + 1)
                    act.wait_ge(ht_mm, t + 1)
                    nc.scalar.copy(hT[:, :], both(HT)).then_inc(ht_ok, 1)
                    if nxt:
                        silus(t + 1)

                turn(0)
                silus(0)
                with act.Fori(0, T - 1) as t:
                    step(t)
                step(T - 1, nxt=False)

            @block.vector
            def _(dve):
                dve.sem_inc(x_ok, 1)
                chain = Chain(dve, steps, 4)

                def weigh(t):
                    dve.wait_ge(h1_mm, t + 1)
                    nc.vector.tensor_tensor(ex(z[:, :]), ex(both(H1)), col(score, t), ALU.mult).then_inc(z_raw, 1)
                    dve.wait_ge(sa_ok, t + 1)
                    nc.vector.tensor_tensor(sh[:, :], ps[:, UP, 2 * P:4 * P], sa[:, :], ALU.mult).then_inc(sh_ok, 1)

                def step(t, nxt=True, nxt2=True):
                    chain.tile(t)
                    dve.wait_ge(x3_mm, t + 1)
                    nc.vector.tensor_tensor(ex(g3[:, :]), ex(both(X3)), col(gain, t), ALU.mult).then_inc(g3_raw, 1)
                    if nxt:
                        weigh(t + 1)
                    if nxt2:
                        dve.wait_ge(xt_mm, t + 2)
                        normalise(nc, k, xn[:, :], t + 2).then_inc(xn_ok, 1)
                    dve.wait_ge(x2_mm, t + 1)
                    chain.done(nc.vector.tensor_tensor(x2[:, :], both(HT), b2[:, :], ALU.add))
                    dve.wait_ge(g3_ok, t + 1)
                    chain.done(nc.vector.tensor_tensor(x2[:, :], x2[:, :], g3[:, :], ALU.mult))
                    nc.vector.tensor_reduce(y[:, :], x2[:, :].rearrange("p (e d) -> p d e", e=E0), AX.X,
                                            ALU.add).then_inc(x2_ok, 1)
                    dve.wait_ge(x2_ok, t + 1)
                    dve.wait_ge(zo_mm, t + 1)
                    add_to_x_and_count(nc, k, chain, t, ps[:, XT, P:P + D], y[:, :]).then_inc(x_ok, 1)
                    chain.end()

                normalise(nc, k, xn[:, :], 0).then_inc(xn_ok, 1)
                weigh(0)
                dve.wait_ge(xt_mm, 1)
                normalise(nc, k, xn[:, :], 1).then_inc(xn_ok, 1)
                with dve.Fori(0, T - 2) as t:
                    step(t)
                step(T - 2, nxt2=False)
                step(T - 1, nxt=False, nxt2=False)

            @block.gpsimd
            def _(pool):
                def bias1(t):
                    pool.wait_ge(z_raw, t + 1)
                    nc.gpsimd.tensor_tensor(z[:, :], z[:, :], b1[:, :], ALU.add).then_inc(z_ok, 1)

                def step(t, nxt=True):
                    nc.gpsimd.tensor_tensor(ex(mb3[:, :]), ex(b3[:, :]), col(mask, t), ALU.mult).then_inc(mb3_ok, 1)
                    pool.wait_ge(mb3_ok, t + 1)
                    pool.wait_ge(g3_raw, t + 1)
                    nc.gpsimd.tensor_tensor(g3[:, :], g3[:, :], mb3[:, :], ALU.add).then_inc(g3_ok, 1)
                    pool.wait_ge(g3_ok, t + 1)
                    if nxt:
                        bias1(t + 1)

                bias1(0)
                with pool.Fori(0, T - 1) as t:
                    step(t)
                step(T - 1, nxt=False)


def stage_alibi(nc, k, w):
    with ExitStack() as ctx:
        sb = lambda n, s: ctx.enter_context(nc.sbuf_tensor(f"al_{n}", s, F32))
        sem = lambda n: k.sem(f"al_{n}")
        ps = k.ps
        wq, wk, wv, wo, bo = [sb(n, [P, D]) for n in ("wq", "wk", "wv", "wo", "bo")]
        alibi = sb("alibi", [P, H, N])
        hm, bm = sb("hm", [P, H]), sb("bm", [P, SEQ])
        xn, xnT = sb("xn", [P, D]), sb("xnT", [P, P])
        qT, vs = sb("qT", [P, P]), sb("vs", [P, 2, D])
        kbd = sb("kbd", [P, SEQ, H, N])
        e, pT = sb("e", [P, H, N]), sb("pT", [P, H, N])
        pbd = sb("pbd", [P, 2, H, SEQ, N])
        mx, den, rec = sb("mx", [P, H]), sb("den", [P, H]), sb("rec", [P, 2, H])
        a, aT = sb("a", [P, D]), sb("aT", [P, P])
        loads = [(wq, w["wq"]), (wk, w["wk"]), (wv, w["wv"]), (wo, w["wo"]), (bo, w["bo"]), (alibi, w["alibi"]),
                 (hm, w["hm"]), (bm, w["bm"])]
        (w_in, ln, xn_ok, xt_mm, xt_sb, qkv_mm, k_ok, qv_ok, s_mm, sub_ok, exp_ok, pt_ok, pbd_ok, o_mm, a_ok, at_mm, at_ok,
         wo_mm, x_ok, steps, steps_x) = [sem(n) for n in (
             "w_in ln xn_ok xt_mm xt_sb qkv_mm k_ok qv_ok s_mm sub_ok exp_ok pt_ok pbd_ok o_mm a_ok at_mm at_ok "
             "wo_mm x_ok steps steps_x").split()]
        XT, K_B, QV, S_B, O_B, AT, WO = 0, 1, 2, 3, 4, 5, 6
        block = ctx.enter_context(nc.Block())

        def tiles(eng, step):
            step(0, 0, first=True)
            with eng.Fori(0, (T - 4) // 2) as i:
                for j in (1, 0):
                    step(2 * i + 2 - j, j)
            step(T - 3, 1, nxt3=False)
            step(T - 2, 0, nxt2=False, nxt3=False)
            step(T - 1, 1, nxt=False, nxt2=False, nxt3=False)

        @block.sync
        def _(sp):
            for dst, src in loads:
                sp.dma_start(dst[:], src).then_inc(w_in, 16)
            sp.wait_ge(w_in, 16 * len(loads))

        @block.tensor
        def _(pe):
            pe.wait_ge(w_in, 16 * len(loads))

            def turn(t):
                pe.wait_ge(xn_ok, t + 1)
                nc.tensor.transpose(ps[:, XT, 0:P], xn[:, :], k.ident[:, :]).then_inc(xt_mm, 1)

            def front(t):
                pe.wait_ge(xt_sb, t + 1)
                nc.tensor.matmul(ps[:, K_B, 0:P], wk[:, :], xnT[:, :], start=True, stop=True)
                nc.tensor.matmul(ps[:, QV, 0:P], wq[:, :], xnT[:, :], start=True, stop=True)
                nc.tensor.matmul(ps[:, QV, P:2 * P], xnT[:, :], wv[:, :], start=True, stop=True).then_inc(qkv_mm, 1)

            def scores(t):
                pe.wait_ge(qv_ok, t + 1)
                pe.wait_ge(k_ok, t + 1)
                for b in range(SEQ):
                    last = nc.tensor.matmul(ps[N * b:N * b + N, S_B, :], qT[:, N * b:N * b + N],
                                            kbd[:, b, :, :], start=True, stop=True)
                last.then_inc(s_mm, 1)

            def values(t, j):
                pe.wait_ge(pbd_ok, t + 2)
                for h in range(H):
                    last = nc.tensor.matmul(ps[:, O_B, DH1 * h:DH1 * h + DH1], pbd[:, j, h, :, :],
                                            vs[:, j, DH1 * h:DH1 * h + DH1], start=True, stop=True)
                last.then_inc(o_mm, 1)

            def turn_a(t):
                pe.wait_ge(a_ok, t + 1)
                nc.tensor.transpose(ps[:, AT, 0:P], a[:, :], k.ident[:, :]).then_inc(at_mm, 1)

            def out(t):
                pe.wait_ge(at_ok, t + 1)
                pe.wait_ge(x_ok, t + 1)
                nc.tensor.matmul(ps[:, WO, 0:D], aT[:, :], wo[:, :], start=True, stop=True).then_inc(wo_mm, 1)

            def step(t, j, first=False, nxt=True, nxt2=True, nxt3=True):
                if nxt:
                    front(t + 1)
                    if nxt2:
                        turn(t + 2)
                    pe.wait_ge(sub_ok, 2 * t + 2)
                    scores(t + 1)
                if not first:
                    turn_a(t - 1)
                values(t, j)
                if not first:
                    out(t - 1)

            pe.sem_inc(o_mm, 2)
            turn(0)
            front(0)
            turn(1)
            scores(0)
            tiles(pe, step)
            turn_a(T - 1)
            out(T - 1)

        @block.scalar
        def _(act):
            act.wait_ge(w_in, 16 * len(loads))
            rstd_act(nc, k, act, ln)

            def turn(t):
                act.wait_ge(xt_mm, t + 1)
                nc.scalar.copy(xnT[:, :], ps[:, XT, 0:P]).then_inc(xt_sb, 1)

            def front(t, j):
                act.wait_ge(qkv_mm, t + 1)
                nc.scalar.mul(qT[:, :], ps[:, QV, 0:P], DH1 ** -0.5)
                nc.scalar.copy(vs[:, j, :], ps[:, QV, P:2 * P]).then_inc(qv_ok, 1)

            def expo(t):
                act.wait_ge(sub_ok, 2 * t + 2)
                nc.scalar.activation(e[:, :, :], e[:, :, :], ACT.Exp).then_inc(exp_ok, 1)

            def turned_a(t):
                act.wait_ge(at_mm, t + 1)
                nc.scalar.copy(aT[:, :], ps[:, AT, 0:P]).then_inc(at_ok, 1)

            def step(t, j, first=False, nxt=True, nxt2=True, nxt3=True):
                if nxt:
                    front(t + 1, 1 - j)
                    if nxt2:
                        turn(t + 2)
                if not first:
                    turned_a(t - 1)
                if nxt:
                    expo(t + 1)

            turn(0)
            front(0, 0)
            turn(1)
            expo(0)
            tiles(act, step)
            turned_a(T - 1)

        @block.vector
        def _(dve):
            dve.sem_inc(x_ok, 1)
            dve.wait_ge(w_in, 16 * len(loads))
            rstd_dve(nc, k, dve, ln, EPS_LN)
            soft, outs = Chain(dve, steps, 3), Chain(dve, steps_x, 2)
            hk = [P, H, N]

            def keys(t):
                dve.wait_ge(qkv_mm, t + 1)
                shape = [P, SEQ, H, N]
                nc.vector.tensor_tensor(kbd[:, :, :, :], ps[:, K_B, 0:P].rearrange("p (b n) -> p b n", b=SEQ)[
                    :, :, None, :].to_broadcast(shape), hm[:, None, :, None].to_broadcast(shape), ALU.mult).then_inc(k_ok, 1)

            def softmax(t, j):
                soft.tile(t)
                dve.wait_ge(s_mm, t + 1)
                nc.vector.tensor_tensor(e[:, :, :], ps[:, S_B, :].rearrange("p (h n) -> p h n", h=H), alibi[:, :, :],
                                        ALU.add).then_inc(sub_ok, 1)
                dve.wait_ge(sub_ok, 2 * t + 1)
                soft.done(nc.vector.tensor_reduce(mx[:, :], e[:, :, :], AX.X, ALU.max))
                nc.vector.tensor_tensor(e[:, :, :], e[:, :, :], mx[:, :, None].to_broadcast(hk),
                                        ALU.subtract).then_inc(sub_ok, 1)
                dve.wait_ge(exp_ok, t + 1)
                dve.wait_ge(pbd_ok, t + 1)
                nc.vector.transpose(pT[:, :, :].rearrange("p h n -> p (h n)"),
                                    e[:, :, :].rearrange("p h n -> p (h n)")).then_inc(pt_ok, 1)
                soft.done(nc.vector.tensor_reduce(den[:, :], e[:, :, :], AX.X, ALU.add))
                soft.done(nc.vector.reciprocal(rec[:, j, :], den[:, :]))
                soft.end()

            def attention(t, j):
                dve.wait_ge(o_mm, t + 3)
                nc.vector.tensor_tensor(a[:, :].rearrange("p (h d) -> p h d", h=H),
                                        ps[:, O_B, 0:D].rearrange("p (h d) -> p h d", h=H),
                                        rec[:, j, :, None].to_broadcast([P, H, DH1]), ALU.mult).then_inc(a_ok, 1)

            def residual(t):
                outs.tile(t)
                dve.wait_ge(wo_mm, t + 1)
                add_to_x_and_count(nc, k, outs, t, ps[:, WO, 0:D], bo[:, :]).then_inc(x_ok, 1)

            def step(t, j, first=False, nxt=True, nxt2=True, nxt3=True):
                if nxt:
                    keys(t + 1)
                if nxt3:
                    dve.wait_ge(xt_mm, t + 3)
                    normalise(nc, k, xn[:, :], t + 3).then_inc(xn_ok, 1)
                if nxt:
                    softmax(t + 1, 1 - j)
                attention(t, j)
                if not first:
                    residual(t - 1)

            normalise(nc, k, xn[:, :], 0).then_inc(xn_ok, 1)
            dve.wait_ge(xt_mm, 1)
            normalise(nc, k, xn[:, :], 1).then_inc(xn_ok, 1)
            keys(0)
            dve.wait_ge(xt_mm, 2)
            normalise(nc, k, xn[:, :], 2).then_inc(xn_ok, 1)
            softmax(0, 0)
            tiles(dve, step)
            residual(T - 1)

        @block.gpsimd
        def _(pool):
            pool.sem_inc(pbd_ok, 1)
            shape = [P, H, SEQ, N]
            with pool.Fori(0, T // 2) as i:
                for j in range(2):
                    t = 2 * i + j
                    pool.wait_ge(pt_ok, t + 1)
                    pool.wait_ge(o_mm, t + 1)
                    nc.gpsimd.tensor_tensor(pbd[:, j, :, :, :], pT[:, :, None, :].to_broadcast(shape),
                                            bm[:, None, :, None].to_broadcast(shape), ALU.mult).then_inc(pbd_ok, 1)


def stage_moe1(nc, k, w):
    EG = 8
    UNITS = [8, 8, 8, 8, 1]
    NU = len(UNITS)
    COLS = (E1 + 1) * I1
    NPAIR = E1 // 2
    with ExitStack() as ctx:
        sb = lambda n, s: ctx.enter_context(nc.sbuf_tensor(f"m1_{n}", s, F32))
        ps = k.ps
        comb = sb("comb", [P, T, E1 + 1])
        wg, wu, wd = sb("wg", [P, COLS]), sb("wu", [P, COLS]), sb("wd", [P, NPAIR + 1, D])
        loads = [(wg, w["wg"]), (wu, w["wu"]), (wd, w["wd"])]

        with ExitStack() as r:
            rsb = lambda n, s: r.enter_context(nc.sbuf_tensor(f"m1_{n}", s, F32))
            rsem = lambda n: k.sem(f"m1_{n}")
            gate, lower = rsb("gate", [P, E1]), rsb("lower", [P, 8, 8])
            sc, rest = rsb("sc", [P, T, E1]), rsb("rest", [P, T, E1])
            gs, gm = rsb("gs", [P, T, 8]), rsb("gm", [P, T, 8])
            top = rsb("top", [P, T, 8])
            tot = rsb("tot", [P, T])
            gt, eq = rsb("gt", [P, T, 8, 8]), rsb("eq", [P, T, 8, 8])
            g_in, w_in, ln, st, sg = rsem("g_in"), rsem("w_in"), rsem("ln"), rsem("st"), rsem("sg")
            logits = ps[:, 4:6, :].rearrange("p a b -> p (a b)")
            tensor, vector, scalar, lg_mm = router_logits(nc, k, r, "m1", gate[:, :], g_in, E1, logits, rsb, rsem)
            block = r.enter_context(nc.Block())

            @block.sync
            def _(sp):
                sp.dma_start(gate[:, :], w["gate"]).then_inc(g_in, 16)
                sp.dma_start(lower[:, :, :], w["lower"]).then_inc(g_in, 16)
                for dst, src in loads:
                    sp.dma_start(dst[:], src).then_inc(w_in, 16)
                sp.wait_ge(g_in, 32)
                sp.wait_ge(w_in, 16 * len(loads))

            @block.tensor
            def _(pe):
                pe.wait_ge(g_in, 32)
                tensor(pe)

            @block.scalar
            def _(act):
                rstd_act(nc, k, act, ln)
                scalar(act)
                act.wait_ge(lg_mm, T + 2)
                nc.scalar.activation(sc[:, :, :].rearrange("p t e -> p (t e)"), logits, ACT.Sigmoid).then_inc(sg, 1)

            @block.vector
            def _(dve):
                rstd_dve(nc, k, dve, ln, EPS_LN)
                vector(dve)
                dve.wait_ge(g_in, 32)
                dve.wait_ge(sg, 1)
                four = sc[:, :, :].rearrange("p t (g e) -> p t g e", g=8)
                nc.vector.tensor_reduce(gs[:, :, :], four, AX.X, ALU.add).then_inc(st, 1)
                dve.wait_ge(st, 1)
                ranked_mask(nc, dve, st, gs, gt[:, :, :, :], eq[:, :, :, :], lower, gm[:, :, :], 8, 4, 1)
                nc.vector.tensor_tensor(four, four, gm[:, :, :, None].to_broadcast([P, T, 8, 4]), ALU.mult).then_inc(st, 1)
                dve.wait_ge(st, 7)
                for t in range(T):
                    last = nc.vector.max(top[:, t, :], sc[:, t, :])
                last.then_inc(st, 1)
                dve.wait_ge(st, 8)
                for t in range(T):
                    last = nc.vector.match_replace(out=rest[:, t, :], in_to_replace=top[:, t, :], in_values=sc[:, t, :],
                                                   imm_value=-1.0)
                last.then_inc(st, 1)
                dve.wait_ge(st, 9)
                nc.vector.scalar_tensor_tensor(rest[:, :, :], rest[:, :, :], 0.0, sc[:, :, :], ALU.is_lt,
                                               ALU.mult).then_inc(st, 1)
                dve.wait_ge(st, 10)
                nc.vector.tensor_reduce(tot[:, :], rest[:, :, :], AX.X, ALU.add).then_inc(st, 1)
                dve.wait_ge(st, 11)
                nc.vector.tensor_scalar(tot[:, :], tot[:, :], 1e-12, None, ALU.max).then_inc(st, 1)
                dve.wait_ge(st, 12)
                nc.vector.reciprocal(tot[:, :], tot[:, :]).then_inc(st, 1)
                dve.wait_ge(st, 13)
                nc.vector.memset(comb[:, :, E1:E1 + 1], 1.0)
                nc.vector.tensor_tensor(comb[:, :, 0:E1], rest[:, :, :], tot[:, :, None].to_broadcast([P, T, E1]), ALU.mult)

        with ExitStack() as m:
            sb = lambda n, s: m.enter_context(nc.sbuf_tensor(f"m1_{n}", s, F32))
            sem = lambda n: k.sem(f"m1_{n}")
            xn, xnT = sb("xn", [P, D]), sb("xnT", [P, 2, P])
            sg, hh, hT = sb("sg", [P, 2, 512]), sb("hh", [P, 2, 512]), sb("hT", [P, 2, 512])
            comb_t = sb("comb_t", [P, 2, E1 + 1])
            (xn_ok, xt_mm, xt_sb, gu_mm, sg_ok, hh_raw, hh_ok, tr_mm, tr_ok, dn_mm, out_mm, x_ok, steps) = [sem(n) for n in (
                "xn_ok xt_mm xt_sb gu_mm sg_ok hh_raw hh_ok tr_mm tr_ok dn_mm out_mm x_ok steps").split()]
            G_B, T_B, ACC, XT = 0, 4, 6, 7
            block = m.enter_context(nc.Block())

            @block.tensor
            def _(pe):
                def turn(t):
                    pe.wait_ge(xn_ok, t + 1)
                    nc.tensor.transpose(ps[:, XT, 0:P], xn[:, :], k.ident[:, :]).then_inc(xt_mm, 1)

                def gates(g, j, v):
                    n, c = UNITS[g] * I1, EG * I1 * g
                    b = G_B + 2 * ((NU * j + g) % 2)
                    nc.tensor.matmul(ps[:, b, 0:n], xnT[:, j, :], wg[:, c:c + n], start=True, stop=True)
                    nc.tensor.matmul(ps[:, b + 1, 0:n], xnT[:, j, :], wu[:, c:c + n], start=True, stop=True).then_inc(gu_mm, 1)

                def turn_h(g, j, v):
                    par = (NU * j + g) % 2
                    pe.wait_ge(hh_ok, v + 1)
                    if UNITS[g] == 1:
                        nc.tensor.nop(nofuse=True)
                    for c in range(max(UNITS[g] // 2, 1)):
                        n = min(P, UNITS[g] * I1)
                        last = nc.tensor.transpose(ps[0:n, T_B + par, c * P:c * P + P], hh[:, par, c * P:c * P + n],
                                                   k.ident[:, :])
                    last.then_inc(tr_mm, 1)

                def down(g, j, v):
                    par = (NU * j + g) % 2
                    pe.wait_ge(tr_ok, v + 1)
                    for c in range(max(UNITS[g] // 2, 1)):
                        n = min(P, UNITS[g] * I1)
                        last = nc.tensor.matmul(ps[:, ACC, 0:D], hT[0:n, par, c * P:c * P + P], wd[0:n, 4 * g + c, :],
                                                start=g == 0 and c == 0, stop=g == NU - 1)
                    last.then_inc(dn_mm, 1)

                def tile(t, j, first=False, last=False):
                    for g in range(NU):
                        v = NU * t + g
                        if g < NU - 1:
                            gates(g + 1, j, v + 1)
                        elif not last:
                            pe.wait_ge(xt_sb, t + 2)
                            gates(0, 1 - j, v + 1)
                        if g == 1 and not last:
                            turn(t + 1)
                        if g > 0:
                            if g == 1 and not first:
                                pe.wait_ge(x_ok, t)
                            down(g - 1, j, v - 1)
                        elif not first:
                            down(NU - 1, 1 - j, v - 1)
                        turn_h(g, j, v)

                turn(0)
                pe.wait_ge(xt_sb, 1)
                gates(0, 0, 0)
                tile(0, 0, first=True)
                with pe.Fori(0, T // 2 - 1) as i:
                    tile(2 * i + 1, 1)
                    tile(2 * i + 2, 0)
                tile(T - 1, 1, last=True)
                down(NU - 1, 1, NU * T - 1)

            @block.scalar
            def _(act):
                def turn(t, j):
                    act.wait_ge(xt_mm, t + 1)
                    nc.scalar.copy(xnT[:, j, :], ps[:, XT, 0:P]).then_inc(xt_sb, 1)

                def silu(g, j, v):
                    par, n = (NU * j + g) % 2, UNITS[g] * I1
                    act.wait_ge(gu_mm, v + 1)
                    nc.scalar.activation(sg[:, par, 0:n], ps[:, G_B + 2 * par, 0:n], ACT.Silu).then_inc(sg_ok, 1)

                def moved(g, j, v):
                    par = (NU * j + g) % 2
                    p, n = (P, 512) if UNITS[g] > 1 else (I1, P)
                    act.wait_ge(tr_mm, v + 1)
                    nc.scalar.copy(hT[0:p, par, 0:n], ps[0:p, T_B + par, 0:n]).then_inc(tr_ok, 1)

                def tile(t, j, last=False):
                    for g in range(NU):
                        v = NU * t + g
                        if g < NU - 1:
                            silu(g + 1, j, v + 1)
                        elif not last:
                            silu(0, 1 - j, v + 1)
                        if g == 1 and not last:
                            turn(t + 1, 1 - j)
                        moved(g, j, v)

                turn(0, 0)
                silu(0, 0, 0)
                with act.Fori(0, T // 2 - 1) as i:
                    tile(2 * i, 0)
                    tile(2 * i + 1, 1)
                tile(T - 2, 0)
                tile(T - 1, 1, last=True)

            @block.vector
            def _(dve):
                def weights(t, j):
                    nc.vector.tensor_scalar(comb_t[:, j, :], at(comb, t), 1.0, None, ALU.mult)

                def up(g, j, v):
                    par, n = (NU * j + g) % 2, UNITS[g] * I1
                    dve.wait_ge(sg_ok, v + 1)
                    nc.vector.tensor_tensor(hh[:, par, 0:n], ps[:, G_B + 2 * par + 1, 0:n], sg[:, par, 0:n],
                                            ALU.mult).then_inc(hh_raw, 1)

                def out(t):
                    dve.wait_ge(dn_mm, NU * t + NU)
                    nc.vector.tensor_tensor(at(k.x, t), ps[:, ACC, 0:D], at(k.x, t), ALU.add).then_inc(x_ok, 1)

                def tile(t, j, first=False, last=False, last2=False):
                    for g in range(NU):
                        v = NU * t + g
                        if g < NU - 1:
                            up(g + 1, j, v + 1)
                        elif not last:
                            up(0, 1 - j, v + 1)
                        if g == 0 and not first:
                            out(t - 1)
                        if g == 0 and not last:
                            weights(t + 1, 1 - j)
                        if g == 2 and not last and not last2:
                            dve.wait_ge(xt_mm, t + 2)
                            normalise(nc, k, xn[:, :], t + 2).then_inc(xn_ok, 1)

                normalise(nc, k, xn[:, :], 0).then_inc(xn_ok, 1)
                weights(0, 0)
                up(0, 0, 0)
                dve.wait_ge(xt_mm, 1)
                normalise(nc, k, xn[:, :], 1).then_inc(xn_ok, 1)
                tile(0, 0, first=True)
                with dve.Fori(0, T // 2 - 2) as i:
                    tile(2 * i + 1, 1)
                    tile(2 * i + 2, 0)
                tile(T - 3, 1)
                tile(T - 2, 0, last2=True)
                tile(T - 1, 1, last=True)
                out(T - 1)

            @block.gpsimd
            def _(pool):
                def weigh(g, j, v):
                    par, n = (NU * j + g) % 2, UNITS[g]
                    pool.wait_ge(hh_raw, v + 1)
                    h = hh[:, par, 0:n * I1].rearrange("p (e i) -> p e i", e=n)
                    nc.gpsimd.tensor_tensor(h, h, comb_t[:, j, EG * g:EG * g + n, None].to_broadcast([P, n, I1]),
                                            ALU.mult).then_inc(hh_ok, 1)

                with pool.Fori(0, T // 2) as i:
                    for j in range(2):
                        for g in range(NU):
                            weigh(g, j, NU * (2 * i + j) + g)


def stage_store(nc, k, out_dram):
    with ExitStack() as ctx:
        stored = k.sem("stored")
        block = ctx.enter_context(nc.Block())

        @block.sync
        def _(sp):
            sp.dma_start(out_dram.rearrange("(t p) d -> p t d", p=P), k.x[:, :, :]).then_inc(stored, 16)
            sp.wait_ge(stored, 16)


def program(nc, d, out, scratch):
    with ExitStack() as ctx:
        k = Core(nc, ctx)
        stage_load(nc, k, d["x"], d["ident"])
        stage_xattn(nc, k, "l0", {n[3:]: a for n, a in d.items() if n.startswith("a0_")},
                    d["ctx_t"], d["ctx_k"], d["ctx_l"], d["last_mask"], scratch)
        stage_performer(nc, k, {n[2:]: a for n, a in d.items() if n.startswith("e_")})
        stage_moe0(nc, k, {n[2:]: a for n, a in d.items() if n.startswith("m_")})
        k.clear_sems()
        stage_xattn(nc, k, "l1", {n[3:]: a for n, a in d.items() if n.startswith("a1_")},
                    d["ctx_t"], d["ctx_k"], d["ctx_l"], d["last_mask"], scratch)
        stage_alibi(nc, k, {n[2:]: a for n, a in d.items() if n.startswith("s_")})
        stage_moe1(nc, k, {n[2:]: a for n, a in d.items() if n.startswith("g_")})
        stage_store(nc, k, out)


def layout(v):
    f = np.float32
    rows = lambda a, n=P: np.broadcast_to(np.asarray(a), (n, np.asarray(a).shape[-1]))
    x = np.asarray(v["x"]).reshape(B * N, D)
    c = np.asarray(v["ctx_768"])
    ca = np.concatenate([c, np.ones((B, NK, 1), f)], axis=2).reshape(T, SEQ, NK, CA)
    ctx_t = ca.transpose(0, 3, 1, 2).reshape(T, CA, SEQ * NK)
    ctx_k = ca[:, :, :256].reshape(T, SEQ, 2, P, CA).transpose(0, 3, 1, 2, 4).reshape(T, P, SEQ * 2 * CA)
    ctx_l = ca[:, :, 256].reshape(B, CA).T
    last_mask = np.tile(np.repeat(np.eye(2 * SEQ, SEQ, dtype=f), HG, axis=0), (HG, 1))
    pad = lambda a: np.concatenate([a, np.zeros((a.shape[0], 1), f)], axis=1)
    two = lambda a: a.reshape(H // 2, P, a.shape[1]).transpose(1, 0, 2)
    d = {"x": x, "ident": np.eye(P, dtype=f), "ctx_t": ctx_t, "ctx_k": ctx_k, "ctx_l": ctx_l,
         "last_mask": last_mask}
    d["a0_wqT"] = two(np.asarray(v["L0_xattn_Wq"]).T)
    d["a0_wkT"] = two(pad(np.asarray(v["L0_xattn_Wk"]).T))
    d["a0_wvT"] = two(pad(np.asarray(v["L0_xattn_Wv"]).T))
    d["a0_wo"] = two(np.asarray(v["L0_xattn_Wo"]))
    d["a0_bo"] = rows(v["L0_xattn_bo"])
    kv = np.concatenate([np.asarray(v["L1_xattn_kv_w"]), np.asarray(v["L1_xattn_kv_b"])[None]], axis=0).T
    d["a1_wqT"] = np.asarray(v["L1_xattn_q_w"]).T
    d["a1_kaT"], d["a1_vaT"] = kv[:D], kv[D:]
    d["a1_wo"] = np.asarray(v["L1_xattn_proj_w"])
    d["a1_head_mask"] = np.repeat(np.eye(H, dtype=f), DH1, axis=0)
    d["a1_qb"] = np.asarray(v["L1_xattn_q_b"])[:, None]
    d["a1_bo"] = rows(v["L1_xattn_proj_b"])
    flat = lambda n: np.asarray(v[n]).reshape(D, H * DH0)
    same = lambda n, size: np.repeat(np.repeat(np.eye(n, dtype=f), size, 0), size, 1)
    d["e_wq"], d["e_wk"], d["e_wv"] = flat("L0_attn_Wq"), flat("L0_attn_Wk"), flat("L0_attn_Wv")
    d["e_wqT"], d["e_wkT"] = two(flat("L0_attn_Wq").T), two(flat("L0_attn_Wk").T)
    d["e_projT"] = np.tile(np.asarray(v["L0_attn_proj"]).T, (2, 1))
    d["e_wo"] = two(np.asarray(v["L0_attn_Wo"]).reshape(H * DH0, D))
    d["e_blocks"] = same(2, DH0) * f(-0.5 * DH0 ** -0.5)
    d["e_mask"] = same(SEQ, N)
    d["e_w1"] = np.asarray(v["L0_attn_W1"])
    d["e_w2"] = np.asarray(v["L0_attn_W2"]).reshape(FF // P, P, D).transpose(1, 0, 2)
    d["e_b1"] = np.asarray(v["L0_attn_b1"]).reshape(FF // P, P).T
    d["e_rows"] = np.stack([rows(v[n]) for n in ("L0_attn_ln1_g", "L0_attn_ln1_b", "L0_attn_b2", "L0_attn_ln2_g",
                                                 "L0_attn_ln2_b")], axis=1)
    lower = np.broadcast_to(np.tril(np.ones((8, 8), f), -1), (P, 8, 8))
    up = lambda n: np.asarray(v[n]).transpose(2, 0, 1).reshape(D, -1)
    for n in ("w1", "w2", "w3"):
        d["m_" + n] = up("L0_ffn_" + n)
    for n in ("b1", "b2", "b3"):
        d["m_" + n] = rows(np.asarray(v["L0_ffn_" + n]).reshape(-1))
    d["m_gate"], d["m_lower"] = np.asarray(v["L0_ffn_gate_w"]).T, lower
    d["m_sw12"] = np.concatenate([np.asarray(v["L0_ffn_sw1"]), np.asarray(v["L0_ffn_sw2"])]).T
    d["m_sw3"] = np.asarray(v["L0_ffn_sw3"]).T.reshape(2, P, D).transpose(1, 0, 2)
    for n in "qkvo":
        d["s_w" + n] = np.asarray(v["L1_attn_W" + n]).T
    d["s_bo"] = rows(v["L1_attn_bo"])
    start = 2.0 ** (-2.0 ** (-(np.log2(H) - 3)))
    slopes = np.array([start * start ** i for i in range(H)], f)
    rel = np.abs(np.arange(N)[None, :] - np.arange(N)[:, None]).astype(f)
    d["s_alibi"] = np.tile(-slopes[None, :, None] * rel[:, None, :], (SEQ, 1, 1))
    d["s_hm"], d["s_bm"] = d["a1_head_mask"], np.repeat(np.eye(SEQ, dtype=f), N, axis=0)
    both = lambda e, sh: np.concatenate([np.asarray(v[e]).reshape(E1 * I1, D), np.asarray(v[sh])]).T
    d["g_gate"], d["g_lower"] = np.asarray(v["L1_ffn_gate_w"]).T, lower
    d["g_wg"] = both("L1_ffn_expert_gate", "L1_ffn_shared_gate_w")
    d["g_wu"] = both("L1_ffn_expert_up", "L1_ffn_shared_up_w")
    wd = np.zeros(((E1 + 2) * I1, D), f)
    wd[:E1 * I1] = np.asarray(v["L1_ffn_expert_down"]).transpose(0, 2, 1).reshape(E1 * I1, D)
    wd[E1 * I1:(E1 + 1) * I1] = np.asarray(v["L1_ffn_shared_down_w"]).T
    d["g_wd"] = wd.reshape(E1 // 2 + 1, P, D).transpose(1, 0, 2)
    return {n: np.ascontiguousarray(a) for n, a in d.items()}


def kernel(**inputs):
    import concourse.bacc as bacc
    from concourse.bass_utils import run_bass_kernel_spmd

    nc = bacc.Bacc("TRN2", target_bir_lowering=False, num_devices=1)
    arrays = layout(inputs)
    aps = {n: nc.dram_tensor(f"in_{n}", a.shape, mybir.dt.from_np(a.dtype), kind="ExternalInput").ap()
           for n, a in arrays.items()}
    out = nc.dram_tensor("out_x", (B * N, D), F32, kind="ExternalOutput").ap()
    scratch = nc.dram_tensor("scratch", (B, H * D), F32, kind="Internal").ap()
    program(nc, aps, out, scratch)
    r = run_bass_kernel_spmd(nc, [{f"in_{n}": a for n, a in arrays.items()}], core_ids=[0])
    return r.results[0]["out_x"].reshape(B, N, D)
```

```python
from contextlib import ExitStack

import numpy as np
import concourse.bass as bass
from concourse import mybir

F32 = mybir.dt.float32
F32R = mybir.dt.float32r
ACT = mybir.ActivationFunctionType
ALU = mybir.AluOpType
AX = mybir.AxisListType

B, N, D = 128, 32, 128
P = 128
T = B * N // P
SEQ = P // N
C, CA = 96, 97
NK = 257
H = 16
HG = 4
DH0 = 64
DH1 = D // H
EPS_LN = 1e-5
EPS_ENC = 1e-6
EPS_KERN = 1e-6
FF = 512
E0, E1 = 8, 32
I1 = 64


def at(ap, t):
    return ap[:, bass.ds(t, 1), :].rearrange("p t n -> p (t n)")


class Chain:

    def __init__(self, eng, sem, per_tile):
        self.eng, self.sem, self.per, self.base, self.n = eng, sem, per_tile, 0, 0

    def tile(self, t):
        self.base, self.n = t * self.per, 0

    def done(self, ins):
        self.n += 1
        ins.then_inc(self.sem, 1)
        self.eng.wait_ge(self.sem, self.base + self.n)

    def end(self):
        assert self.n == self.per, (self.n, self.per)


class Core:

    def __init__(self, nc, ctx):
        self.nc = nc
        sb = lambda n, s: ctx.enter_context(nc.sbuf_tensor(n, s, F32))
        self.x = sb("x", [P, T, D])
        self.stats = sb("stats", [P, T, 6])
        self.mean = sb("mean", [P, T])
        self.half = sb("half", [P, 5, T])
        self.var_eps = sb("var_eps", [P, T])
        self.std = sb("std", [P, T])
        self.rstd = sb("rstd", [P, T])
        self.ident = sb("ident", [P, P])
        self.sems = []
        self.ps = ctx.enter_context(nc.psum_tensor("ps", [P, 8, 512], F32))

    def sem(self, name):
        self.sems.append(self.nc.alloc_semaphore(name))
        return self.sems[-1]

    def clear_sems(self):
        self.nc.clear_and_free_semaphores(self.sems)
        self.nc.all_engine_barrier()
        self.sems = []


def add_to_x_and_count(nc, k, chain, t, psum, bias, xs=None):
    xt = at(k.x, t)
    chain.done(nc.vector.tensor_tensor(xt, psum, xt, ALU.add))
    chain.done(nc.vector.tensor_tensor(xt, xt, bias, ALU.add))
    nc.vector.nop(nofuse=True)
    return nc.vector.bn_stats(at(k.stats, t), xt)


def rstd_dve(nc, k, dve, ln, eps):
    col = lambda n: k.stats[:, :, n:n + 1].rearrange("p t o -> p (t o)")
    h = k.half
    nc.vector.tensor_tensor(h[:, 0, :], col(1), col(4), ALU.add)
    nc.vector.tensor_tensor(h[:, 1, :], col(1), col(4), ALU.subtract)
    nc.vector.tensor_tensor(h[:, 2, :], col(2), col(5), ALU.add).then_inc(ln, 1)
    dve.wait_ge(ln, 1)
    nc.vector.tensor_scalar(k.mean[:, :], h[:, 0, :], 0.5, None, ALU.mult)
    nc.vector.tensor_tensor(h[:, 3, :], h[:, 1, :], h[:, 1, :], ALU.mult)
    nc.vector.tensor_scalar(h[:, 4, :], h[:, 2, :], 1.0 / D, eps, ALU.mult, ALU.add).then_inc(ln, 1)
    dve.wait_ge(ln, 2)
    nc.vector.scalar_tensor_tensor(k.var_eps[:, :], h[:, 3, :], 0.25, h[:, 4, :], ALU.mult, ALU.add).then_inc(ln, 1)
    dve.wait_ge(ln, 4)
    nc.vector.reciprocal(k.rstd[:, :], k.std[:, :]).then_inc(ln, 1)
    dve.wait_ge(ln, 5)


def rstd_act(nc, k, act, ln):
    act.wait_ge(ln, 3)
    nc.scalar.activation(k.std[:, :], k.var_eps[:, :], ACT.Sqrt).then_inc(ln, 1)


def normalise(nc, k, out, t):
    return nc.vector.tensor_scalar(out, at(k.x, t), k.mean[:, bass.ds(t, 1)], k.rstd[:, bass.ds(t, 1)],
                                   ALU.subtract, ALU.mult)


def split(nc, dve, hi, lo, src, count, n):
    nc.vector.tensor_copy(hi, src).then_inc(count, 1)
    dve.wait_ge(count, n + 1)
    return nc.vector.tensor_tensor(lo, src, hi.bitcast(F32), ALU.subtract)


def product(nc, out, left, right):
    nc.tensor.matmul(out, left[0], right[0], start=True, stop=False)
    nc.tensor.matmul(out, left[0], right[1], start=False, stop=False)
    return nc.tensor.matmul(out, left[1], right[0], start=False, stop=True)


def stage_xattn(nc, k, name, w, ctx_t, ctx_k, ctx_l, last_mask, scratch, next_loads,
                x_dram=None, ident=None):
    first = name == "l0"
    with ExitStack() as ctx:
        sb = lambda n, s: ctx.enter_context(nc.sbuf_tensor(f"{name}_{n}", s, F32))
        sem = lambda n: k.sem(f"{name}_{n}")
        A = sb("A", [P, H, CA])
        U = sb("U", [CA, H, D])
        qbias = sb("qbias", [CA, H])
        bo = sb("bo", [P, D])
        W = sb("W", [B, H, D])
        w_in = sem("w_in")
        ps = k.ps

        with ExitStack() as prep:
            psb = lambda n, s: prep.enter_context(nc.sbuf_tensor(f"{name}_{n}", s, F32))
            psem = lambda n: k.sem(f"{name}_{n}")
            made = psem("made")
            moved = psem("moved")
            masked = psem("masked")
            u_sb = psem("u_sb")
            ctxl = psb("ctxl", [CA, B])
            if first:
                wqT, wkT = psb("wqT", [P, H // 2, D]), psb("wkT", [P, H // 2, CA])
                wvT, wo = psb("wvT", [P, H // 2, CA]), psb("wo", [P, H // 2, D])
                scale = DH0 ** -0.5
                loads = [(wqT, w["wqT"]), (wkT, w["wkT"]), (wvT, w["wvT"]), (wo, w["wo"])]
            else:
                wqT, kaT, vaT, wo = psb("wqT", [P, D]), psb("kaT", [P, CA]), psb("vaT", [P, CA]), psb("wo", [P, D])
                hm, qb = psb("hm", [P, H]), psb("qb", [P, 1])
                kam, vam, qbm = psb("kam", [P, H, CA]), psb("vam", [P, H, CA]), psb("qbm", [P, H])
                scale = DH1 ** -0.5
                loads = [(wqT, w["wqT"]), (kaT, w["kaT"]), (vaT, w["vaT"]), (wo, w["wo"]),
                         (hm, w["head_mask"]), (qb, w["qb"])]
            n_loads = len(loads) + (3 if first else 2)
            x_in = [psem(f"x_in{q}") for q in range(4)] if first else None
            counted = psem("counted")
            block = prep.enter_context(nc.Block())

            @block.sync
            def _(sp):
                for dst, src in loads + [(bo, w["bo"]), (ctxl, ctx_l)]:
                    sp.dma_start(dst[:], src).then_inc(w_in, 16)
                if first:
                    sp.dma_start(k.ident[:, :], ident).then_inc(w_in, 16)
                    for q in range(4):
                        sp.dma_start(k.x[:, q * T // 4:(q + 1) * T // 4, :], x_dram.rearrange(
                            "(q t p) d -> q p t d", q=4, p=P)[q]).then_inc(x_in[q], 16)
                sp.wait_ge(w_in, 16 * n_loads)

            @block.vector
            def _(dve):
                if first:
                    nc.vector.memset(qbias[:, :], 0.0).then_inc(masked, 1)
                    for q in range(4):
                        dve.wait_ge(x_in[q], 16)
                        with dve.Fori(q * T // 4, (q + 1) * T // 4) as t:
                            nc.vector.bn_stats(at(k.stats, t), at(k.x, t)).then_inc(counted, 1)
                    dve.wait_ge(counted, T)
                else:
                    dve.wait_ge(w_in, 16 * n_loads)
                    for dst, src in ((kam, kaT), (vam, vaT)):
                        nc.vector.tensor_tensor(dst[:, :, :], src[:, None, :].to_broadcast([P, H, CA]),
                                                hm[:, :, None].to_broadcast([P, H, CA]),
                                                ALU.mult).then_inc(masked, 1)
                    nc.vector.tensor_scalar(qbm[:, :], hm[:, :], qb[:, 0:1], None, ALU.mult).then_inc(masked, 1)

            @block.tensor
            def _(pe):
                pe.wait_ge(w_in, 16 * n_loads)
                if first:
                    for h in range(H):
                        c, r = h // 2, 64 * (h % 2)
                        bank = 2 * (h % 2) + c // 4
                        last = nc.tensor.matmul(ps[:, bank, (c % 4) * P:(c % 4) * P + CA], wqT[r:r + 64, c, :],
                                                wkT[r:r + 64, c, :], start=True, stop=True)
                    last.then_inc(made, 1)
                    for h in range(H):
                        c, r = h // 2, 64 * (h % 2)
                        bank = 4 + 2 * (h % 2) + c // 4
                        last = nc.tensor.matmul(ps[0:CA, bank, (c % 4) * P:(c % 4) * P + P], wvT[r:r + 64, c, :],
                                                wo[r:r + 64, c, :], start=True, stop=True)
                    last.then_inc(made, 1)
                else:
                    pe.wait_ge(masked, 3)
                    for g in range(4):
                        last = nc.tensor.matmul(ps[:, g, 0:HG * CA], wqT[:, :], kam[:, HG * g:HG * g + HG, :],
                                                start=True, stop=True)
                    last.then_inc(made, 1)
                    for h in range(H):
                        last = nc.tensor.matmul(ps[0:CA, 4 + h // 4, (h % 4) * P:(h % 4) * P + P], vam[:, h, :],
                                                wo[:, :], start=True, stop=True)
                    last.then_inc(made, 1)
                    pe.wait_ge(moved, 1)
                    nc.tensor.matmul(ps[0:CA, 0, 0:H], kaT[:, :], qbm[:, :], start=True, stop=True).then_inc(made, 1)
                pe.wait_ge(u_sb, 4)
                for g in range(4):
                    last = nc.tensor.matmul(ps[:, 4 + g, :], ctxl[:, :], U[:, HG * g:HG * g + HG, :],
                                            start=True, stop=True)
                last.then_inc(made, 1)

            @block.scalar
            def _(act):
                act.wait_ge(made, 1)
                if first:
                    for par in range(2):
                        for g in range(2):
                            nc.scalar.mul(A[:, 8 * g + par:8 * g + 8:2, :],
                                          ps[:, 2 * par + g, :].rearrange("p (c n) -> p c n", c=4)[:, :, 0:CA], scale)
                else:
                    for g in range(4):
                        last = nc.scalar.mul(A[:, HG * g:HG * g + HG, :], ps[:, g, 0:HG * CA].rearrange(
                            "p (c n) -> p c n", c=4), scale)
                    last.then_inc(moved, 1)
                act.wait_ge(made, 2)
                for par in range(2):
                    for g in range(2):
                        if first:
                            nc.scalar.copy(U[:, 8 * g + par:8 * g + 8:2, :],
                                           ps[0:CA, 4 + 2 * par + g, :].rearrange("p (c n) -> p c n", c=4)
                                           ).then_inc(u_sb, 1)
                        else:
                            nc.scalar.copy(U[:, 4 * (2 * par + g):4 * (2 * par + g) + 4, :],
                                           ps[0:CA, 4 + 2 * par + g, :].rearrange("p (c n) -> p c n", c=4)
                                           ).then_inc(u_sb, 1)
                if not first:
                    act.wait_ge(made, 3)
                    nc.scalar.mul(qbias[:, :], ps[0:CA, 0, 0:H], scale)
                act.wait_ge(made, 3 if first else 4)
                for g in range(4):
                    nc.scalar.copy(W[:, HG * g:HG * g + HG, :], ps[:, 4 + g, :].rearrange("p (c n) -> p c n", c=HG))

        ctxT = sb("ctxT", [CA, 2, SEQ * NK])
        ctxK = sb("ctxK", [P, 2, SEQ * 2 * CA])
        xn = sb("xn", [P, D])
        xnT = sb("xnT", [P, P])
        q1 = sb("q1", [CA, 2, HG, SEQ, HG * N])
        probs = sb("probs", [P, 2, HG, NK])
        nmax = sb("nmax", [P, 2, HG])
        den = sb("den", [P, 2, HG])
        rden = sb("rden", [P, 2, HG])
        pT = sb("pT", [P, 2, HG * P])
        last_p = sb("last_p", [P, N])
        last_pT = sb("last_pT", [P, N])
        last_bd = sb("last_bd", [P, 2, SEQ, N])
        last_m = sb("last_m", [P, SEQ])
        last_w = sb("last_w", [P, T, D])
        oT = sb("oT", [CA, 2, H, SEQ, N])
        S_B, T_B, A_B, O_B = 0, 4, 6, 7

        ln, xn_ok, xt_mm, xt_sb = sem("ln"), sem("xn_ok"), sem("xt_mm"), sem("xt_sb")
        q_mm, q_sb, s_mm, nm_ok = sem("q_mm"), sem("q_sb"), sem("s_mm"), sem("nm_ok")
        exp_ok, norm_ok, t_mm = sem("exp_ok"), sem("norm_ok"), sem("t_mm")
        pt_a, pt_v, o_mm, o_sb = sem("pt_a"), sem("pt_v"), sem("o_mm"), sem("o_sb")
        out_mm, x_ok, steps, last_ok = sem("out_mm"), sem("x_ok"), sem("steps"), sem("last_ok")
        m_in, cleared, w_out, lw_in = sem("m_in"), sem("cleared"), sem("w_out"), sem("lw_in")
        next_in = sem("next_in")
        ctx_in = [sem("ctx_in0"), sem("ctx_in1")]
        block = ctx.enter_context(nc.Block())

        def tiles(eng, tile):
            tile(0, 0, 1, first=True)
            with eng.Fori(0, (T - 4) // 2) as i:
                tile(2 * i + 1, 1, i + 2)
                tile(2 * i + 2, 0, i + 2)
            tile(T - 3, 1, T // 2)
            tile(T - 2, 0, T // 2, x_after=False)
            tile(T - 1, 1, None, x_after=False, last=True)

        @block.sync
        def _(sp):
            def load(t, j):
                for dst, src in ((ctxT, ctx_t), (ctxK, ctx_k)):
                    sp.dma_start(dst[:, j, :], src[bass.ds(t, 1), :, :].rearrange(
                        "t c n -> c (t n)")).then_inc(ctx_in[j], 16)

            load(0, 0)
            sp.dma_start(last_m[:, :], last_mask).then_inc(m_in, 16)
            sp.dma_start(scratch, W[:, :, :].rearrange("p h d -> p (h d)")).then_inc(w_out, 16)
            load(1, 1)
            sp.wait_ge(w_out, 16)
            sp.wait_ge(cleared, 1)
            for h4 in range(HG):
                for b in range(SEQ):
                    row = N * h4 + HG * b
                    sp.dma_start(last_w[row:row + HG, :, :],
                                 scratch.rearrange("(t b) (g h d) -> b h g t d", b=SEQ, g=HG, h=HG)[b, h4]
                                 ).then_inc(lw_in, 16)
            for dst, src in next_loads:
                sp.dma_start(dst[:], src).then_inc(next_in, 16)
            with sp.Fori(1, T // 2) as i:
                for j in range(2):
                    sp.wait_ge(o_mm, 4 * (2 * i + j) - 4)
                    load(2 * i + j, j)
            sp.wait_ge(next_in, 16 * len(next_loads))

        @block.tensor
        def _(pe):
            def turn_x(t):
                pe.wait_ge(xn_ok, t + 1)
                nc.tensor.transpose(ps[:, T_B + 1, 0:P], xn[:, :], k.ident[:, :]).then_inc(xt_mm, 1)

            def queries(hg):
                for h in range(HG):
                    last_i = nc.tensor.matmul(ps[0:CA, T_B, h * P:h * P + P], A[:, HG * hg + h, :], xnT[:, :],
                                              start=True, stop=True)
                last_i.then_inc(q_mm, 1)

            def scores(b, j, after):
                for hg in range(HG):
                    if after is not None:
                        pe.wait_ge(exp_ok, 4 * after + hg + 1)
                    last_i = nc.tensor.matmul(ps[:, S_B + hg, 0:NK], q1[:, j, hg, b, :],
                                              ctxT[:, j, b * NK:b * NK + NK], start=True, stop=True)
                    if hg % 2:
                        last_i.then_inc(s_mm, 1)

            def sum_heads(b, j, t):
                if b == 0:
                    pe.wait_ge(o_sb, 4 * t + 5)
                    pe.wait_ge(x_ok, t + 1)
                for h in range(HG * b, HG * b + HG):
                    nc.tensor.matmul(ps[:, A_B, 0:D], oT[:, j, h, :, :].rearrange("c b n -> c (b n)"), U[:, h, :],
                                     start=h == 0, stop=False)
                if b == SEQ - 1:
                    pe.wait_ge(last_ok, t + 1)
                    pe.nop(nofuse=True)
                    nc.tensor.matmul(ps[:, A_B, 0:D], last_bd[:, j, :, :].rearrange("p b n -> p (b n)"),
                                     at(last_w, t), start=False, stop=True).then_inc(out_mm, 1)

            def tile(t, j, fills, first=False, x_after=True, last=False):
                for b in range(SEQ):
                    u = 4 * t + b
                    if b < SEQ - 1:
                        scores(b + 1, j, u)
                    elif not last:
                        pe.wait_ge(q_sb, 4 * t + 8)
                        pe.wait_ge(ctx_in[1 - j], 32 * fills)
                        scores(0, 1 - j, u)
                    pe.wait_ge(norm_ok, u + 1)
                    if not last:
                        pe.wait_ge(q_sb, u + 5)
                    if b == SEQ - 1 and x_after:
                        pe.wait_ge(xt_sb, t + 3)
                    for kt in range(2):
                        for hg in range(HG):
                            last_i = nc.tensor.transpose(ps[:, T_B + kt, hg * P:hg * P + P],
                                                         probs[:, b % 2, hg, kt * P:kt * P + P], k.ident[:, :])
                    last_i.then_inc(t_mm, 1)
                    if not first:
                        sum_heads(b, 1 - j, t - 1)
                    pe.wait_ge(pt_a, u + 1)
                    pe.wait_ge(pt_v, u + 1)
                    pe.wait_ge(o_sb, u + 1)
                    for kt in range(2):
                        at_k = (b * 2 + kt) * CA
                        last_i = nc.tensor.matmul(ps[0:CA, O_B, :], ctxK[:, j, at_k:at_k + CA], pT[:, kt, :],
                                                  start=kt == 0, stop=kt == 1)
                    last_i.then_inc(o_mm, 1)
                    if b < SEQ - 1 and not last:
                        queries(b + 1)
                    elif x_after:
                        queries(0)
                    if b == SEQ - 2 and x_after:
                        turn_x(t + 2)

            turn_x(0)
            pe.wait_ge(xt_sb, 1)
            for hg in range(HG):
                if hg:
                    pe.wait_ge(q_sb, hg)
                queries(hg)
            turn_x(1)
            pe.wait_ge(q_sb, HG)
            pe.wait_ge(ctx_in[0], 32)
            scores(0, 0, None)
            pe.wait_ge(xt_sb, 2)
            queries(0)
            pe.wait_ge(lw_in, 16 * HG * SEQ)
            tiles(pe, tile)
            for b in range(SEQ):
                sum_heads(b, (T - 1) % 2, T - 1)

        @block.vector
        def _(dve):
            def queries(n, j, hg):
                dve.wait_ge(q_mm, n + 1)
                nc.vector.tensor_tensor(q1[:, j, hg, :, :].rearrange("c b (h n) -> c h b n", h=HG),
                                        ps[0:CA, T_B, :].rearrange("c (h b n) -> c h b n", h=HG, b=SEQ),
                                        qbias[:, HG * hg:HG * hg + HG, None, None].to_broadcast([CA, HG, SEQ, N]),
                                        ALU.add).then_inc(q_sb, 1)

            def maxima(u, par):
                for half in range(2):
                    dve.wait_ge(s_mm, 2 * u + half + 1)
                    nc.vector.tensor_reduce(nmax[:, par, 2 * half:2 * half + 2],
                                            ps[:, S_B + 2 * half:S_B + 2 * half + 2, 0:NK], AX.X, ALU.max,
                                            negate=True).then_inc(nm_ok, 1)

            def divide(u, b):
                par = b % 2
                dve.wait_ge(exp_ok, 4 * u + 4)
                chain.done(nc.vector.reciprocal(rden[:, par, :], den[:, par, :]))
                nc.vector.tensor_tensor(last_p[:, HG * b:HG * b + HG], probs[:, par, :, NK - 1], rden[:, par, :],
                                        ALU.mult)
                for hg in range(HG):
                    pr = probs[:, par, hg, 0:NK - 1]
                    last_i = nc.vector.tensor_scalar(pr, pr, rden[:, par, hg:hg + 1], None, ALU.mult)
                last_i.then_inc(norm_ok, 1)

            def residual(t):
                dve.wait_ge(out_mm, t + 1)
                add_to_x_and_count(nc, k, chain, t, ps[:, A_B, 0:D], bo[:, :]).then_inc(x_ok, 1)

            def tile(t, j, fills, first=False, x_after=True, last=False):
                chain.tile(1 if first else 8 * t - 1)
                for b in range(SEQ):
                    u = 4 * t + b
                    if b < SEQ - 1 or not last:
                        maxima(u + 1, (b + 1) % 2)
                    dve.wait_ge(t_mm, u + 1)
                    nc.vector.tensor_copy(pT[:, 1, :], ps[:, T_B + 1, :]).then_inc(pt_v, 1)
                    if b == SEQ - 1:
                        chain.done(nc.vector.transpose(last_pT[:, :], last_p[:, :]))
                        chain.done(nc.vector.tensor_tensor(last_bd[:, j, :, :],
                                                           last_pT[:, None, :].to_broadcast([P, SEQ, N]),
                                                           last_m[:, :, None].to_broadcast([P, SEQ, N]), ALU.mult))
                        dve.sem_inc(last_ok, 1)
                    if b < SEQ - 1 or not last:
                        divide(u + 1, (b + 1) % SEQ)
                    if b == 1 and x_after:
                        normalise(nc, k, xn[:, :], t + 2).then_inc(xn_ok, 1)
                    if b < SEQ - 1 and not last:
                        queries(u + 5, 1 - j, b + 1)
                    elif x_after:
                        queries(u + 5, j, 0)
                    if b == SEQ - 1 and not first:
                        residual(t - 1)

            dve.sem_inc(x_ok, 1)
            nc.vector.memset(last_p[:, :], 0.0)
            rstd_dve(nc, k, dve, ln, EPS_LN)
            normalise(nc, k, xn[:, :], 0).then_inc(xn_ok, 1)
            chain = Chain(dve, steps, 1)
            for hg in range(HG):
                queries(hg, 0, hg)
            dve.wait_ge(xt_mm, 1)
            normalise(nc, k, xn[:, :], 1).then_inc(xn_ok, 1)
            maxima(0, 0)
            queries(HG, 1, 0)
            divide(0, 0)
            dve.wait_ge(m_in, 16)
            tiles(dve, tile)
            residual(T - 1)

        @block.scalar
        def _(act):
            def turned(t):
                act.wait_ge(xt_mm, t + 1)
                nc.scalar.copy(xnT[:, :], ps[:, T_B + 1, 0:P]).then_inc(xt_sb, 1)

            def exps(u, par):
                for hg in range(HG):
                    if hg % 2 == 0:
                        act.wait_ge(nm_ok, 2 * u + hg // 2 + 1)
                    nc.scalar.activation(probs[:, par, hg, :], ps[:, S_B + hg, 0:NK], ACT.Exp,
                                         bias=nmax[:, par, hg:hg + 1], accum_out=den[:, par, hg:hg + 1]
                                         ).then_inc(exp_ok, 1)

            def tile(t, j, fills, first=False, x_after=True, last=False):
                for b in range(SEQ):
                    u = 4 * t + b
                    if b < SEQ - 1 or not last:
                        exps(u + 1, (b + 1) % 2)
                    act.wait_ge(t_mm, u + 1)
                    nc.scalar.copy(pT[:, 0, :], ps[:, T_B, :]).then_inc(pt_a, 1)
                    act.wait_ge(o_mm, u + 1)
                    nc.scalar.copy(oT[:, j, :, b, :], ps[0:CA, O_B, :].rearrange("c (h n) -> c h n", h=H)
                                   ).then_inc(o_sb, 1)
                    if b == SEQ - 2 and x_after:
                        turned(t + 2)

            act.sem_inc(o_sb, 1)
            rstd_act(nc, k, act, ln)
            turned(0)
            turned(1)
            exps(0, 0)
            tiles(act, tile)

        @block.gpsimd
        def _(pool):
            nc.gpsimd.memset(last_w[:, :, :], 0.0).then_inc(cleared, 1)


def performer_weights(nc, ctx, w):
    sizes = {"wqT": [P, H // 2, D], "wkT": [P, H // 2, D], "projT": [P, DH0], "wq": [P, H * DH0], "wk": [P, H * DH0],
             "wv": [P, H * DH0], "wo": [P, H // 2, D],
             "blocks": [P, P],
             "mask": [P, P],
             "w1": [P, FF], "w2": [P, FF // P, D], "b1": [P, FF // P],
             "rows": [P, 5, D]}
    bufs = {n: ctx.enter_context(nc.sbuf_tensor(f"enc_{n}", size, F32)) for n, size in sizes.items()}
    return bufs, [(bufs[n], w[n]) for n in sizes]


def stage_performer(nc, k, bufs):
    HALF = 8 * DH0
    dn = float(DH0) ** -0.25
    with ExitStack() as ctx:
        sb = lambda n, s: ctx.enter_context(nc.sbuf_tensor(f"enc_{n}", s, F32))
        ps = k.ps
        res = sb("res", [P, T, D])
        negmx = sb("negmx", [P, 1])
        NF = FF // P
        w1, w2, b1, rows = [bufs[n] for n in ("w1", "w2", "b1", "rows")]

        with ExitStack() as att:
            sb = lambda n, s: att.enter_context(nc.sbuf_tensor(f"enc_{n}", s, F32))
            sem = lambda n: k.sem(f"enc_{n}")
            wq, wk, wv, wo, blocks, mask = [bufs[n] for n in ("wq", "wk", "wv", "wo", "blocks", "mask")]
            pq, pk = sb("pq", [P, H * DH0]), sb("pk", [P, H * DH0])
            wide = att.enter_context(nc.sbuf_tensor("enc_wide", [P, 6, H * DH0], F32R))
            ones = sb("ones", [1, P])
            halves = sem("halves")

            with ExitStack() as prep:
                psb = lambda n, s: prep.enter_context(nc.sbuf_tensor(f"enc_{n}", s, F32))
                psem = lambda n: k.sem(f"enc_{n}")
                wqT, wkT, projT = [bufs[n] for n in ("wqT", "wkT", "projT")]
                xn4 = psb("xn4", [P, 2, 4, D])
                xnT4 = psb("xnT4", [P, 2, 4 * P])
                tmp, acc = psb("tmp", [P, 2]), psb("acc", [P, 2])
                rowmax = psb("rowmax", [P, 1])
                allmax = psb("allmax", [1, 1])
                made, moved, ln = psem("made"), psem("moved"), psem("ln_a")
                xn_ok, xt_mm, xt_sb = psem("xn_ok_a"), psem("xt_mm_a"), psem("xt_sb_a")
                d_mm, max_ok, steps, fin = psem("d_mm"), psem("max_ok"), psem("steps_a"), psem("fin")
                block = prep.enter_context(nc.Block())
                @block.tensor
                def _(pe):
                    pe.sem_inc(xt_mm, 1)
                    for n, wT in ((0, wqT), (1, wkT)):
                        for h in range(H):
                            c, r = h // 2, 64 * (h % 2)
                            last = nc.tensor.matmul(ps[:, 2 * n + h % 2, c * DH0:c * DH0 + DH0], wT[r:r + 64, c, :],
                                                    projT[r:r + 64, :], start=True, stop=True)
                        last.then_inc(made, 1)
                    pe.wait_ge(moved, 2)

                    def turn(g, j):
                        pe.wait_ge(xn_ok, g + 1)
                        for n in range(4):
                            last = nc.tensor.transpose(ps[:, 4 + j, n * P:n * P + P], xn4[:, j, n, :], k.ident[:, :])
                        last.then_inc(xt_mm, 1)

                    def features(g, j, s):
                        pe.wait_ge(max_ok, 4 * g + s + 1)
                        for c in range(2):
                            last = nc.tensor.matmul(ps[:, 2 * (s % 2) + c, :], pk[:, (2 * s + c) * P:(2 * s + c) * P + P],
                                                    xnT4[:, j, :], start=True, stop=True)
                        last.then_inc(d_mm, 1)

                    def group(g, j, last=False):
                        pe.wait_ge(xt_sb, g + 1)
                        features(g, j, 0)
                        features(g, j, 1)
                        if not last:
                            turn(g + 1, 1 - j)
                        features(g, j, 2)
                        features(g, j, 3)

                    turn(0, 0)
                    with pe.Fori(0, T // 8 - 1) as i:
                        for j in range(2):
                            group(2 * i + j, j)
                    group(T // 4 - 2, 0)
                    group(T // 4 - 1, 1, last=True)
                    pe.wait_ge(fin, 1)
                    nc.tensor.transpose(ps[0:1, 6, 0:P], rowmax[:, :], k.ident[:, :]).then_inc(made, 1)
                    pe.wait_ge(fin, 2)
                    nc.tensor.matmul(ps[:, 7, 0:1], ones[:, :], allmax[:, :], start=True, stop=True).then_inc(made, 1)

                @block.vector
                def _(dve):
                    dve.sem_inc(max_ok, 2)
                    nc.vector.memset(ones[:, :], 1.0)
                    nc.vector.memset(acc[:, :], -3.0e38).then_inc(steps, 1)
                    dve.wait_ge(steps, 1)
                    rstd_dve(nc, k, dve, ln, EPS_LN)

                    def normal(g, j):
                        for n in range(4):
                            last = normalise(nc, k, xn4[:, j, n, :], 4 * g + n)
                        last.then_inc(xn_ok, 1)

                    def group(g, j, last=False):
                        if not last:
                            dve.wait_ge(xt_mm, g + 1)
                            normal(g + 1, 1 - j)
                        for s in range(4):
                            dve.wait_ge(d_mm, 4 * g + s + 1)
                            b = 2 * (s % 2)
                            nc.vector.tensor_reduce(tmp[:, :], ps[:, b:b + 2, :], AX.X, ALU.max).then_inc(max_ok, 1)
                            dve.wait_ge(max_ok, 4 * g + s + 3)
                            nc.vector.tensor_tensor(acc[:, :], acc[:, :], tmp[:, :], ALU.max).then_inc(steps, 1)
                            dve.wait_ge(steps, 4 * g + s + 2)

                    normal(0, 0)
                    with dve.Fori(0, T // 8 - 1) as i:
                        for j in range(2):
                            group(2 * i + j, j)
                    group(T // 4 - 2, 0)
                    group(T // 4 - 1, 1, last=True)
                    dve.wait_ge(moved, 2)
                    for n, src in enumerate((wq, pq, wv)):
                        split(nc, dve, wide[:, 2 * n, :], wide[:, 2 * n + 1, :], src[:, :], halves, n)
                    nc.vector.tensor_reduce(rowmax[:, :], acc[:, :], AX.X, ALU.max).then_inc(fin, 1)
                    dve.wait_ge(made, 3)
                    nc.vector.tensor_reduce(allmax[:, :], ps[0:1, 6, 0:P], AX.X, ALU.max, negate=True).then_inc(fin, 1)
                    dve.wait_ge(made, 4)
                    nc.vector.tensor_copy(negmx[:, :], ps[:, 7, 0:1])

                @block.scalar
                def _(act):
                    for n, dst in ((0, pq), (1, pk)):
                        act.wait_ge(made, n + 1)
                        for par in range(2):
                            last = nc.scalar.mul(dst[:, :].rearrange("p (c r m) -> p r c m", r=2, m=DH0)[:, par],
                                                 ps[:, 2 * n + par, :].rearrange("p (c m) -> p c m", m=DH0), dn)
                        last.then_inc(moved, 1)
                    rstd_act(nc, k, act, ln)
                    with act.Fori(0, T // 8) as i:
                        for j in range(2):
                            act.wait_ge(xt_mm, 2 * i + j + 2)
                            nc.scalar.copy(xnT4[:, j, :], ps[:, 4 + j, :]).then_inc(xt_sb, 1)

            xn, xr = sb("xn", [P, D]), sb("xr", [P, D])
            xnT = sb("xnT", [P, P])
            xh, xl = [att.enter_context(nc.sbuf_tensor(f"enc_{n}", [P, P], F32R)) for n in ("xh", "xl")]
            xh_ok, xs_ok = sem("xh_ok"), sem("xs_ok")
            ksq, qsq = sb("ksq", [P, 1024]), sb("qsq", [P, 1024])
            eq, kf = sb("eq", [P, 1024]), sb("kf", [P, 1024])
            qfT = sb("qfT", [P, 1024])
            va = sb("va", [P, H, DH0 + 1])
            sm = sb("sm", [P, 4, 512])
            at_sb, atT = sb("at", [P, 1024]), sb("atT", [P, 1024])
            diag, mx, cc = sb("diag", [P, H]), sb("mx", [P, H]), sb("cc", [P, H])
            rden = sb("rden", [P, H])
            eps_col, eps_ok = sb("eps_col", [P, 1]), sem("eps_ok")
            FA, FB, RA, RB = 0, 2, 4, 6
            (xn_ok, xt_mm, xt_sb, k_mm, ksq_ok, q_mm, qsq_ok, dq_mm, sub_ok, eq_ok, dk_mm, kf_raw, kf_ok, v_mm, v_ok,
             qt_mm, qt_ok, s_mm, sm_ok, o_mm, at_ok, at_mm, atT_ok, wo_mm, res_ok, xr_ok, steps, steps_d) = [sem(n) for n in (
                 "xn_ok xt_mm xt_sb k_mm ksq_ok q_mm qsq_ok dq_mm sub_ok eq_ok dk_mm kf_raw kf_ok v_mm v_ok "
                 "qt_mm qt_ok s_mm sm_ok o_mm at_ok at_mm atT_ok wo_mm res_ok xr_ok steps steps_d").split()]
            block = att.enter_context(nc.Block())
            both = lambda pair: ps[:, pair:pair + 2, :].rearrange("p a b -> p (a b)")

            def feature_major(pair, wt, sem):
                for c in range(8):
                    last = nc.tensor.matmul(ps[:, pair + c // 4, (c % 4) * P:(c % 4) * P + P], wt[:, c * P:c * P + P],
                                            xnT[:, :], start=True, stop=True)
                last.then_inc(sem, 1)

            def token_major(pair, n, sem):
                for c in range(2):
                    last = product(nc, ps[:, pair + c, :], (xh[:, :], xl[:, :]),
                                   [wide[:, 2 * n + m, c * 512:c * 512 + 512] for m in range(2)])
                last.then_inc(sem, 1)

            def pe_front(pe, t, part):
                if part == 0:
                    pe.wait_ge(xt_sb, t + 1)
                    feature_major(FA, wk, k_mm)
                elif part == 1:
                    pe.wait_ge(xs_ok, t + 1)
                    token_major(FB, 0, q_mm)
                elif part == 2:
                    pe.wait_ge(ksq_ok, t + 1)
                    token_major(FA, 1, dq_mm)
                elif part == 3:
                    pe.wait_ge(qsq_ok, t + 1)
                    for c in range(8):
                        out = ps[:, FB + c // 4, (c % 4) * P:(c % 4) * P + P]
                        nc.tensor.matmul(out, pk[:, c * P:c * P + P], xnT[:, :], start=True, stop=False)
                        last = nc.tensor.matmul(out, blocks[:, :], ksq[:, c * P:c * P + P], start=False, stop=True)
                    last.then_inc(dk_mm, 1)
                else:
                    pe.wait_ge(sub_ok, t + 1)
                    token_major(FA, 2, v_mm)

            def pe_rear(pe, t, part, nxt=True):
                if part == 0:
                    pe.wait_ge(eq_ok, t + 1)
                    for c in range(8):
                        last = nc.tensor.transpose(ps[:, RA + c // 4, (c % 4) * P:(c % 4) * P + P],
                                                   eq[:, c * P:c * P + P], k.ident[:, :])
                    last.then_inc(qt_mm, 1)
                elif part in (1, 2):
                    if part == 1:
                        pe.wait_ge(kf_ok, t + 1)
                        pe.wait_ge(qt_ok, t + 1)
                    base = RB if part == 1 else RA
                    for n in range(4):
                        for par in range(2):
                            c, r = 4 * (part - 1) + n, 64 * par
                            last = nc.tensor.matmul(ps[:, base + par, n * P:n * P + P], kf[r:r + 64, c * P:c * P + P],
                                                    qfT[r:r + 64, c * P:c * P + P], start=True, stop=True)
                    last.then_inc(s_mm, 1)
                elif part == 3:
                    pe.wait_ge(v_ok, t + 1)
                    for half in range(2):
                        pe.wait_ge(sm_ok, 2 * t + half + 1)
                        if half:
                            pe.wait_ge(sm_ok, 2 * t + 2)
                        base = (RB, RA)[half]
                        for n in range(4):
                            for par in range(2):
                                h = 8 * half + 2 * n + par
                                last = nc.tensor.matmul(ps[:, base + par, n * 65:n * 65 + 65],
                                                        sm[:, 2 * half + par, n * P:n * P + P], va[:, h, :],
                                                        start=True, stop=True)
                        last.then_inc(o_mm, 1)
                elif part == 4:
                    pe.wait_ge(at_ok, 2 * t + 2)
                    for c in range(8):
                        last = nc.tensor.transpose(ps[:, RB + c // 4, (c % 4) * P:(c % 4) * P + P],
                                                   at_sb[:, c * P:c * P + P], k.ident[:, :])
                    last.then_inc(at_mm, 1)
                else:
                    pe.wait_ge(atT_ok, t + 1)
                    for c in range(8):
                        last = nc.tensor.matmul(ps[:, RA, 0:D], atT[:, c * P:c * P + P], wo[:, c, :],
                                                start=c == 0, stop=c == 7)
                    last.then_inc(wo_mm, 1)

            def pe_next_xT(pe, t):
                pe.wait_ge(xn_ok, t + 1)
                nc.tensor.transpose(ps[:, RA + 1, 0:P], xn[:, :], k.ident[:, :]).then_inc(xt_mm, 1)

            @block.tensor
            def _(pe):
                pe_next_xT(pe, 0)
                for part in range(5):
                    pe_front(pe, 0, part)
                pe_next_xT(pe, 1)

                def step(t, front=True, x_after=True):
                    if front:
                        pe.wait_ge(xt_sb, t + 2)
                    pe.wait_ge(res_ok, t + 1)
                    for part in range(5):
                        pe_rear(pe, t, part)
                        if front:
                            if part == 0:
                                pe.wait_ge(v_ok, t + 1)
                            if part == 1:
                                pe.wait_ge(kf_raw, t + 1)
                            pe_front(pe, t + 1, part)
                    pe_rear(pe, t, 5)
                    if x_after:
                        pe_next_xT(pe, t + 2)

                with pe.Fori(0, T - 2) as t:
                    step(t)
                step(T - 2, x_after=False)
                step(T - 1, front=False, x_after=False)

            @block.scalar
            def _(act):
                def front(t, part):
                    if part == 0:
                        act.wait_ge(k_mm, t + 1)
                        nc.scalar.activation(ksq[:, :], both(FA), ACT.Square).then_inc(ksq_ok, 1)
                    elif part == 1:
                        act.wait_ge(q_mm, t + 1)
                        nc.scalar.activation(qsq[:, :], both(FB), ACT.Square).then_inc(qsq_ok, 1)
                    elif part == 2:
                        act.wait_ge(sub_ok, t + 1)
                        nc.scalar.activation(eq[:, :], eq[:, :], ACT.Exp).then_inc(eq_ok, 1)
                    elif part == 3:
                        act.wait_ge(dk_mm, t + 1)
                        nc.scalar.activation(kf[:, :], both(FB), ACT.Exp, bias=negmx[:, 0:1]).then_inc(kf_raw, 1)
                    else:
                        act.wait_ge(v_mm, t + 1)
                        nc.scalar.copy(va[:, :, 0:DH0], both(FA).rearrange("p (h d) -> p h d", h=H)).then_inc(v_ok, 1)

                def x_next(t):
                    act.wait_ge(xt_mm, t + 1)
                    nc.scalar.copy(xnT[:, :], ps[:, RA + 1, 0:P]).then_inc(xt_sb, 1)

                def step(t, fr=True, x_after=True):
                    act.wait_ge(qt_mm, t + 1)
                    nc.scalar.activation(qfT[:, :], both(RA), ACT.Copy, bias=EPS_KERN).then_inc(qt_ok, 1)
                    if fr:
                        for part in range(4):
                            front(t + 1, part)
                    act.wait_ge(at_mm, t + 1)
                    nc.scalar.copy(atT[:, :], both(RB)).then_inc(atT_ok, 1)
                    if fr:
                        front(t + 1, 4)
                    if x_after:
                        x_next(t + 2)

                x_next(0)
                for part in range(5):
                    front(0, part)
                x_next(1)
                with act.Fori(0, T - 2) as t:
                    step(t)
                step(T - 2, x_after=False)
                step(T - 1, fr=False, x_after=False)

            @block.vector
            def _(dve):
                nc.vector.memset(va[:, :, DH0:DH0 + 1], 1.0)
                dve.sem_inc(res_ok, 1)
                q_steps, d_steps = Chain(dve, steps, 2), Chain(dve, steps_d, 2)
                heads = lambda ap: ap.rearrange("p (h d) -> p h d", h=H)

                def x_norm(t):
                    normalise(nc, k, xn[:, :], t).then_inc(xn_ok, 1)

                def front_q(t):
                    q_steps.tile(t)
                    dve.wait_ge(qsq_ok, t + 1)
                    nc.vector.tensor_reduce(diag[:, :], heads(qsq[:, :]), AX.X, ALU.add)
                    dve.wait_ge(dq_mm, t + 1)
                    q_steps.done(nc.vector.tensor_reduce(mx[:, :], heads(both(FA)), AX.X, ALU.max))
                    q_steps.done(nc.vector.scalar_tensor_tensor(cc[:, :], diag[:, :], dn * dn / 2, mx[:, :],
                                                                ALU.mult, ALU.add))
                    nc.vector.tensor_tensor(heads(eq[:, :]), heads(both(FA)),
                                            cc[:, :, None].to_broadcast([P, H, DH0]), ALU.subtract).then_inc(sub_ok, 1)

                def mask_s(t, half):
                    dve.wait_ge(s_mm, 2 * t + half + 1)
                    pair = (RB, RA)[half]
                    nc.vector.tensor_tensor(sm[:, 2 * half:2 * half + 2, :].rearrange("p a (n q) -> p (a n) q", q=P),
                                            ps[:, pair:pair + 2, :].rearrange("p a (n q) -> p (a n) q", q=P),
                                            mask[:, None, :].to_broadcast([P, 8, P]), ALU.mult).then_inc(sm_ok, 1)

                def divide(t, half):
                    dve.wait_ge(o_mm, 2 * t + half + 1)
                    pair = (RB, RA)[half]
                    for par in range(2):
                        src = ps[:, pair + par, 0:260].rearrange("p (n e) -> p n e", e=65)
                        rd = rden[:, 8 * half + 4 * par:8 * half + 4 * par + 4]
                        nc.vector.reciprocal(rd[:, :, None], src[:, :, 64:65]).then_inc(steps_d, 1)
                    dve.wait_ge(steps_d, 4 * t + 2 * half + 2)
                    for par in range(2):
                        src = ps[:, pair + par, 0:260].rearrange("p (n e) -> p n e", e=65)
                        rd = rden[:, 8 * half + 4 * par:8 * half + 4 * par + 4]
                        last = nc.vector.tensor_tensor(at_sb[:, 512 * half:512 * half + 512].rearrange(
                            "p (n r d) -> p r n d", r=2, d=DH0)[:, par], src[:, :, 0:64],
                            rd[:, :, None].to_broadcast([P, 4, DH0]), ALU.mult)
                    last.then_inc(at_ok, 1)

                def residual(t):
                    normalise(nc, k, xr[:, :], t).then_inc(xr_ok, 1)
                    dve.wait_ge(xr_ok, t + 1)
                    dve.wait_ge(wo_mm, t + 1)
                    nc.vector.tensor_tensor(at(res, t), ps[:, RA, 0:D], xr[:, :], ALU.add).then_inc(res_ok, 1)
                    dve.wait_ge(res_ok, t + 2)
                    nc.vector.nop(nofuse=True)
                    nc.vector.bn_stats(at(k.stats, t), at(res, t))

                def parts(t):
                    dve.wait_ge(xt_sb, t + 1)
                    split(nc, dve, xh[:, :], xl[:, :], xnT[:, :], xh_ok, t).then_inc(xs_ok, 1)

                def step(t, fr=True, x_after=True):
                    if fr:
                        parts(t + 1)
                    mask_s(t, 0)
                    mask_s(t, 1)
                    if fr:
                        front_q(t + 1)
                    if x_after:
                        dve.wait_ge(xt_mm, t + 2)
                        x_norm(t + 2)
                    divide(t, 0)
                    divide(t, 1)
                    residual(t)

                x_norm(0)
                parts(0)
                front_q(0)
                dve.wait_ge(xt_mm, 1)
                x_norm(1)
                with dve.Fori(0, T - 2) as t:
                    step(t)
                step(T - 2, x_after=False)
                step(T - 1, fr=False, x_after=False)

            @block.gpsimd
            def _(pool):
                nc.gpsimd.memset(eps_col[:, :], EPS_KERN).then_inc(eps_ok, 1)
                pool.wait_ge(eps_ok, 1)
                with pool.Fori(0, T) as t:
                    pool.wait_ge(kf_raw, t + 1)
                    nc.gpsimd.tensor_tensor(kf[:, :], kf[:, :], eps_col[:, 0:1].to_broadcast([P, 1024]),
                                            ALU.add).then_inc(kf_ok, 1)

        with ExitStack() as net:
            sb = lambda n, s: net.enter_context(nc.sbuf_tensor(f"net_{n}", s, F32))
            sem = lambda n: k.sem(f"net_{n}")
            PART = 4
            out1 = sb("out1", [P, T, D])
            o1T = sb("o1T", [P, P])
            z, ez = sb("z", [P, 2, FF]), sb("ez", [P, FF])
            hT = sb("hT", [P, 2, FF])
            staged = sb("staged", [P, 2, D])
            stage_ok = sem("stage_ok")
            ln, n1, n2, o1_ok = sem("ln"), sem("n1"), sem("n2"), sem("o1_ok")
            tr_mm, tr_ok, h_mm, z_ok, e_ok, em_ok, h_ok, y_mm, y_ok, st_ok = [sem(n) for n in (
                "tr_mm tr_ok h_mm z_ok e_ok em_ok h_ok y_mm y_ok st_ok").split()]
            block = net.enter_context(nc.Block())
            @block.tensor
            def _(pe):
                def turn(t, j):
                    pe.wait_ge(stage_ok, t + 1)
                    nc.tensor.transpose(ps[:, 0, 0:P], staged[:, j, :], k.ident[:, :]).then_inc(tr_mm, 1)

                def up(t, j):
                    pe.wait_ge(tr_ok, t + 1)
                    for c in range(NF):
                        last = nc.tensor.matmul(ps[:, 2 + j, c * P:c * P + P], w1[:, c * P:c * P + P], o1T[:, :],
                                                start=True, stop=True)
                    last.then_inc(h_mm, 1)

                def down(t, j):
                    pe.wait_ge(h_ok, t + 1)
                    for c in range(NF):
                        last = nc.tensor.matmul(ps[:, 4 + j, 0:D], hT[:, j, c * P:c * P + P], w2[:, c, :],
                                                start=c == 0, stop=c == NF - 1)
                    last.then_inc(y_mm, 1)

                def part(i, last=False):
                    for n in range(PART):
                        t = PART * i + n
                        if n < PART - 1 or not last:
                            up(t + 1, (n + 1) % 2)
                        if n < PART - 2 or not last:
                            turn(t + 2, n % 2)
                        down(t, n % 2)

                turn(0, 0)
                up(0, 0)
                turn(1, 1)
                with pe.Fori(0, T // PART - 1) as i:
                    part(i)
                part(T // PART - 1, last=True)

            @block.vector
            def _(dve):
                rstd_dve(nc, k, dve, ln, EPS_ENC)
                with dve.Fori(0, T) as t:
                    nc.vector.tensor_scalar(at(res, t), at(res, t), k.mean[:, bass.ds(t, 1)], k.rstd[:, bass.ds(t, 1)],
                                            ALU.subtract, ALU.mult).then_inc(n1, 1)

                def exponent(t, j):
                    dve.wait_ge(h_mm, t + 1)
                    nc.vector.tensor_tensor(z[:, j, :].rearrange("p (c q) -> p c q", c=NF),
                                            ps[:, 2 + j, :].rearrange("p (c q) -> p c q", c=NF),
                                            b1[:, :, None].to_broadcast([P, NF, P]), ALU.add).then_inc(z_ok, 1)

                def elu(t, j):
                    dve.wait_ge(e_ok, t + 1)
                    nc.vector.tensor_scalar(ez[:, :], ez[:, :], 1.0, -1.0, ALU.min, ALU.add).then_inc(em_ok, 1)
                    dve.wait_ge(em_ok, t + 1)
                    nc.vector.scalar_tensor_tensor(hT[:, j, :], z[:, j, :], 0.0, ez[:, :], ALU.max, ALU.add).then_inc(h_ok, 1)

                def result(t, j):
                    dve.wait_ge(y_mm, t + 1)
                    nc.vector.tensor_tensor(at(res, t), ps[:, 4 + j, 0:D], at(res, t), ALU.add).then_inc(y_ok, 1)

                def count(t):
                    dve.wait_ge(y_ok, t + 1)
                    nc.vector.nop(nofuse=True)
                    nc.vector.bn_stats(at(k.stats, t), at(res, t))

                exponent(0, 0)
                elu(0, 0)
                dve.wait_ge(n2, 3 * T // PART)
                with dve.Fori(0, T // 2 - 1) as i:
                    for j in range(2):
                        t = 2 * i + j
                        exponent(t + 1, 1 - j)
                        result(t, j)
                        elu(t + 1, 1 - j)
                        count(t)
                exponent(T - 1, 1)
                result(T - 2, 0)
                elu(T - 1, 1)
                count(T - 2)
                result(T - 1, 1)
                count(T - 1)

            @block.scalar
            def _(act):
                rstd_act(nc, k, act, ln)

                def turn(t):
                    act.wait_ge(tr_mm, t + 1)
                    nc.scalar.copy(o1T[:, :], ps[:, 0, 0:P]).then_inc(tr_ok, 1)

                def expo(t, j):
                    act.wait_ge(z_ok, t + 1)
                    nc.scalar.activation(ez[:, :], z[:, j, :], ACT.Exp).then_inc(e_ok, 1)

                def stage(t, j, part):
                    act.wait_ge(o1_ok, part + 1)
                    act.nop(nofuse=True)
                    nc.scalar.copy(staged[:, j, :], at(out1, t)).then_inc(stage_ok, 1)

                def part(i, last=False):
                    for n in range(PART):
                        t = PART * i + n
                        if n < PART - 2 or not last:
                            turn(t + 2)
                        if not last:
                            stage(t + PART, n % 2, i + 1)
                        if n < PART - 1 or not last:
                            expo(t + 1, (n + 1) % 2)

                stage(0, 0, 0)
                stage(1, 1, 0)
                turn(0)
                stage(2, 0, 0)
                turn(1)
                stage(3, 1, 0)
                expo(0, 0)
                with act.Fori(0, T // PART - 1) as i:
                    part(i)
                part(T // PART - 1, last=True)

            @block.gpsimd
            def _(pool):
                wide = [P, PART, D]
                for i in range(T // PART):
                    o, r = [a[:, PART * i:PART * i + PART, :] for a in (out1, res)]
                    pool.wait_ge(n1, PART * i + PART)
                    nc.gpsimd.tensor_tensor(o, r, rows[:, 0:1, :].to_broadcast(wide), ALU.mult).then_inc(n2, 1)
                    pool.wait_ge(n2, 3 * i + 1)
                    nc.gpsimd.tensor_tensor(o, o, rows[:, 1:2, :].to_broadcast(wide), ALU.add).then_inc(n2, 1)
                    pool.wait_ge(n2, 3 * i + 2)
                    pool.sem_inc(o1_ok, 1)
                    nc.gpsimd.tensor_tensor(r, o, rows[:, 2:3, :].to_broadcast(wide), ALU.add).then_inc(n2, 1)
                for i in range(T // PART):
                    xs = k.x[:, PART * i:PART * i + PART, :]
                    nc.gpsimd.tensor_tensor(xs, xs, rows[:, 4:5, :].to_broadcast(wide), ALU.add)

        with ExitStack() as end:
            sem = lambda n: k.sem(f"fin_{n}")
            centred = end.enter_context(nc.sbuf_tensor("fin_centred", [P, 2, D], F32))
            ln, sub, st = sem("ln"), sem("sub"), sem("st")
            block = end.enter_context(nc.Block())

            @block.scalar
            def _(act):
                rstd_act(nc, k, act, ln)

            @block.vector
            def _(dve):
                rstd_dve(nc, k, dve, ln, EPS_ENC)

                def centre(t, j):
                    nc.vector.scalar_tensor_tensor(centred[:, j, :], at(res, t), k.mean[:, bass.ds(t, 1)], rows[:, 3, :],
                                                   ALU.subtract, ALU.mult).then_inc(sub, 1)

                def add(t, j):
                    dve.wait_ge(sub, t + 1)
                    nc.vector.scalar_tensor_tensor(at(k.x, t), centred[:, j, :], k.rstd[:, bass.ds(t, 1)], at(k.x, t),
                                                   ALU.mult, ALU.add).then_inc(st, 1)

                def count(t):
                    dve.wait_ge(st, t + 1)
                    nc.vector.nop(nofuse=True)
                    nc.vector.bn_stats(at(k.stats, t), at(k.x, t))

                centre(0, 0)
                centre(1, 1)
                add(0, 0)
                with dve.Fori(0, T // 2 - 1) as i:
                    for j in range(2):
                        add(2 * i + j + 1, 1 - j)
                        count(2 * i + j)
                        centre(2 * i + j + 2, j)
                add(T - 1, 1)
                count(T - 2)
                count(T - 1)


def ranked_mask(nc, dve, count, s, gt, eq, lower, mask, n, keep, base):
    shape = [P, T, n, n]
    mine, other = s[:, :, :, None].to_broadcast(shape), s[:, :, None, :].to_broadcast(shape)
    nc.vector.tensor_tensor(gt, other, mine, ALU.is_gt)
    nc.vector.tensor_tensor(eq, other, mine, ALU.is_equal).then_inc(count, 1)
    dve.wait_ge(count, base + 1)
    nc.vector.tensor_tensor(eq, eq, lower[:, None, :, :].to_broadcast(shape), ALU.mult).then_inc(count, 1)
    dve.wait_ge(count, base + 2)
    nc.vector.tensor_tensor(gt, gt, eq, ALU.add).then_inc(count, 1)
    dve.wait_ge(count, base + 3)
    nc.vector.tensor_reduce(mask, gt, AX.X, ALU.add).then_inc(count, 1)
    dve.wait_ge(count, base + 4)
    nc.vector.tensor_scalar(mask, mask, float(keep), None, ALU.is_lt).then_inc(count, 1)
    dve.wait_ge(count, base + 5)


def router_logits(nc, k, ctx, name, gate, gate_in, n_experts, logits, sb, sem):
    xn, xnT = sb("xn_r", [P, 2, D]), sb("xnT_r", [P, 2, P])
    xn_ok, xt_mm, xt_sb, lg_mm = sem("xn_ok_r"), sem("xt_mm_r"), sem("xt_sb_r"), sem("lg_mm")
    ps = k.ps

    def tensor(pe):
        pe.sem_inc(xt_mm, 2)
        pe.sem_inc(lg_mm, 2)
        with pe.Fori(0, T // 2) as i:
            for j in range(2):
                pe.wait_ge(xn_ok, 2 * i + j + 1)
                nc.tensor.transpose(ps[:, j, 0:P], xn[:, j, :], k.ident[:, :]).then_inc(xt_mm, 1)
            for j in range(2):
                pe.wait_ge(xt_sb, 2 * i + j + 1)
                nc.tensor.matmul(logits[:, bass.ds((2 * i + j) * n_experts, n_experts)], xnT[:, j, :], gate,
                                 start=True, stop=True).then_inc(lg_mm, 1)

    def vector(dve):
        with dve.Fori(0, T // 2) as i:
            for j in range(2):
                dve.wait_ge(xt_mm, 2 * i + j + 1)
                normalise(nc, k, xn[:, j, :], 2 * i + j).then_inc(xn_ok, 1)

    def scalar(act):
        with act.Fori(0, T // 2) as i:
            for j in range(2):
                act.wait_ge(xt_mm, 2 * i + j + 3)
                act.wait_ge(lg_mm, 2 * i + j + 1)
                nc.scalar.copy(xnT[:, j, :], ps[:, j, 0:P]).then_inc(xt_sb, 1)

    return tensor, vector, scalar, lg_mm


def stage_moe0(nc, k, w):
    ED = E0 * D
    with ExitStack() as ctx:
        sb = lambda n, s: ctx.enter_context(nc.sbuf_tensor(f"m0_{n}", s, F32))
        ps = k.ps
        score, mask = sb("score", [P, T, E0]), sb("mask", [P, T, E0])
        gain = sb("gain", [P, T, E0])
        w1, w2, w3 = sb("w1", [P, ED]), sb("w2", [P, ED]), sb("w3", [P, ED])
        b1, b2, b3 = sb("b1", [P, ED]), sb("b2", [P, ED]), sb("b3", [P, ED])
        sw12, sw3 = sb("sw12", [P, 4 * P]), sb("sw3", [P, 2, D])
        loads = [(w1, w["w1"]), (w2, w["w2"]), (w3, w["w3"]), (b1, w["b1"]), (b2, w["b2"]), (b3, w["b3"]),
                 (sw12, w["sw12"]), (sw3, w["sw3"])]

        with ExitStack() as r:
            rsb = lambda n, s: r.enter_context(nc.sbuf_tensor(f"m0_{n}", s, F32))
            rsem = lambda n: k.sem(f"m0_{n}")
            gate, lower = rsb("gate", [P, E0]), rsb("lower", [P, E0, E0])
            lg, mx = rsb("lg", [P, T, E0]), rsb("mx", [P, T])
            gt, eq = rsb("gt", [P, T, E0, E0]), rsb("eq", [P, T, E0, E0])
            g_in, w_in, ln, st, ex = rsem("g_in"), rsem("w_in"), rsem("ln"), rsem("st"), rsem("ex")
            logits = ps[:, 4, :]
            tensor, vector, scalar, lg_mm = router_logits(nc, k, r, "m0", gate[:, :], g_in, E0, logits, rsb, rsem)
            block = r.enter_context(nc.Block())

            @block.sync
            def _(sp):
                sp.dma_start(gate[:, :], w["gate"]).then_inc(g_in, 16)
                sp.dma_start(lower[:, :, :], w["lower"]).then_inc(g_in, 16)
                for dst, src in loads:
                    sp.dma_start(dst[:], src).then_inc(w_in, 16)
                sp.wait_ge(g_in, 32)
                sp.wait_ge(w_in, 16 * len(loads))

            @block.tensor
            def _(pe):
                pe.wait_ge(g_in, 32)
                tensor(pe)

            @block.scalar
            def _(act):
                rstd_act(nc, k, act, ln)
                scalar(act)
                act.wait_ge(st, 2)
                nc.scalar.activation(lg[:, :, :], lg[:, :, :], ACT.Exp).then_inc(ex, 1)

            @block.vector
            def _(dve):
                rstd_dve(nc, k, dve, ln, EPS_LN)
                vector(dve)
                wide = [P, T, E0]
                dve.wait_ge(lg_mm, T + 2)
                all_lg = logits[:, 0:T * E0].rearrange("p (t e) -> p t e", e=E0)
                nc.vector.tensor_reduce(mx[:, :], all_lg, AX.X, ALU.max).then_inc(st, 1)
                dve.wait_ge(st, 1)
                nc.vector.tensor_tensor(lg[:, :, :], all_lg, mx[:, :, None].to_broadcast(wide),
                                        ALU.subtract).then_inc(st, 1)
                dve.wait_ge(ex, 1)
                nc.vector.tensor_reduce(mx[:, :], lg[:, :, :], AX.X, ALU.add).then_inc(st, 1)
                dve.wait_ge(st, 3)
                nc.vector.reciprocal(mx[:, :], mx[:, :]).then_inc(st, 1)
                dve.wait_ge(st, 4)
                nc.vector.tensor_tensor(score[:, :, :], lg[:, :, :], mx[:, :, None].to_broadcast(wide),
                                        ALU.mult).then_inc(st, 1)
                dve.wait_ge(st, 5)
                dve.wait_ge(g_in, 32)
                ranked_mask(nc, dve, st, score, gt[:, :, :, :], eq[:, :, :, :], lower, mask[:, :, :], E0, 2, 5)
                nc.vector.tensor_tensor(gain[:, :, :], mask[:, :, :], score[:, :, :], ALU.mult)

        with ExitStack() as m:
            sb = lambda n, s: m.enter_context(nc.sbuf_tensor(f"m0_{n}", s, F32))
            sem = lambda n: k.sem(f"m0_{n}")
            xn, xnT = sb("xn", [P, D]), sb("xnT", [P, P])
            z, hT, g3, mb3, x2 = sb("z", [P, ED]), sb("hT", [P, ED]), sb("g3", [P, ED]), sb("mb3", [P, ED]), sb("x2", [P, ED])
            sa, sh, y = sb("sa", [P, 2 * P]), sb("sh", [P, 2 * P]), sb("y", [P, D])
            (xn_ok, xt_mm, xt_sb, h1_mm, z_raw, z_ok, h_ok, ht_mm, ht_ok, x3_mm, g3_raw, g3_ok, x2_mm, x2_ok, up_mm, sa_ok,
             sh_ok, zo_mm, x_ok, steps, mb3_ok, y2_ok) = [sem(n) for n in (
                 "xn_ok xt_mm xt_sb h1_mm z_raw z_ok h_ok ht_mm ht_ok x3_mm g3_raw g3_ok x2_mm x2_ok up_mm sa_ok "
                 "sh_ok zo_mm x_ok steps mb3_ok y2_ok").split()]
            H1, X3, HT, UP, XT = 0, 2, 4, 6, 7
            both = lambda pair: ps[:, pair:pair + 2, :].rearrange("p a b -> p (a b)")
            ex = lambda ap: ap.rearrange("p (e d) -> p e d", e=E0)
            col = lambda a, t: at(a, t)[:, :, None].to_broadcast([P, E0, D])
            block = m.enter_context(nc.Block())

            @block.tensor
            def _(pe):
                def turn(t):
                    pe.wait_ge(xn_ok, t + 1)
                    nc.tensor.transpose(ps[:, XT, 0:P], xn[:, :], k.ident[:, :]).then_inc(xt_mm, 1)

                def wide(pair, wt, s):
                    for c in range(2):
                        last = nc.tensor.matmul(ps[:, pair + c, :], xnT[:, :], wt[:, 512 * c:512 * c + 512],
                                                start=True, stop=True)
                    last.then_inc(s, 1)

                def shared_up():
                    for c in range(4):
                        last = nc.tensor.matmul(ps[:, UP, c * P:c * P + P], sw12[:, c * P:c * P + P], xnT[:, :],
                                                start=True, stop=True)
                    last.then_inc(up_mm, 1)

                def step(t, nxt=True):
                    pe.wait_ge(x_ok, t + 1)
                    if nxt:
                        turn(t + 1)
                    pe.wait_ge(y2_ok, t + 1)
                    pe.wait_ge(h_ok, t + 1)
                    for e in range(E0):
                        last = nc.tensor.transpose(ps[:, HT + e // 4, (e % 4) * P:(e % 4) * P + P],
                                                   z[:, e * P:e * P + P], k.ident[:, :])
                    last.then_inc(ht_mm, 1)
                    if nxt:
                        pe.wait_ge(xt_sb, t + 2)
                    pe.wait_ge(sh_ok, t + 1)
                    for c in range(2):
                        last = nc.tensor.matmul(ps[:, XT, P:P + D], sh[:, c * P:c * P + P], sw3[:, c, :],
                                                start=c == 0, stop=c == 1)
                    last.then_inc(zo_mm, 1)
                    if nxt:
                        wide(H1, w1, h1_mm)
                        shared_up()
                    pe.wait_ge(ht_ok, t + 1)
                    for e in range(E0):
                        last = nc.tensor.matmul(ps[:, HT + e // 4, (e % 4) * P:(e % 4) * P + P],
                                                hT[:, e * P:e * P + P], w2[:, e * D:e * D + D], start=True, stop=True)
                    last.then_inc(x2_mm, 1)
                    if nxt:
                        pe.wait_ge(g3_raw, t + 1)
                        wide(X3, w3, x3_mm)

                turn(0)
                pe.wait_ge(xt_sb, 1)
                wide(H1, w1, h1_mm)
                shared_up()
                wide(X3, w3, x3_mm)
                with pe.Fori(0, T - 1) as t:
                    step(t)
                step(T - 1, nxt=False)

            @block.scalar
            def _(act):
                def turn(t):
                    act.wait_ge(xt_mm, t + 1)
                    nc.scalar.copy(xnT[:, :], ps[:, XT, 0:P]).then_inc(xt_sb, 1)

                def silus(t):
                    act.wait_ge(up_mm, t + 1)
                    nc.scalar.activation(sa[:, :], ps[:, UP, 0:2 * P], ACT.Silu).then_inc(sa_ok, 1)
                    act.wait_ge(z_ok, t + 1)
                    nc.scalar.activation(z[:, :], z[:, :], ACT.Silu).then_inc(h_ok, 1)

                def step(t, nxt=True):
                    if nxt:
                        turn(t + 1)
                    act.wait_ge(ht_mm, t + 1)
                    nc.scalar.copy(hT[:, :], both(HT)).then_inc(ht_ok, 1)
                    if nxt:
                        silus(t + 1)

                turn(0)
                silus(0)
                with act.Fori(0, T - 1) as t:
                    step(t)
                step(T - 1, nxt=False)

            @block.vector
            def _(dve):
                dve.sem_inc(x_ok, 1)
                dve.sem_inc(y2_ok, 1)
                chain = Chain(dve, steps, 2)

                def weigh(t):
                    dve.wait_ge(h1_mm, t + 1)
                    nc.vector.tensor_tensor(ex(z[:, :]), ex(both(H1)), col(score, t), ALU.mult).then_inc(z_raw, 1)
                    dve.wait_ge(sa_ok, t + 1)
                    nc.vector.tensor_tensor(sh[:, :], ps[:, UP, 2 * P:4 * P], sa[:, :], ALU.mult).then_inc(sh_ok, 1)

                def step(t, nxt=True, nxt2=True):
                    chain.tile(t)
                    xt = at(k.x, t)
                    dve.wait_ge(zo_mm, t + 1)
                    nc.vector.tensor_tensor(xt, ps[:, XT, P:P + D], xt, ALU.add).then_inc(x_ok, 1)
                    dve.wait_ge(x3_mm, t + 1)
                    nc.vector.tensor_tensor(ex(g3[:, :]), ex(both(X3)), col(gain, t), ALU.mult).then_inc(g3_raw, 1)
                    if nxt:
                        weigh(t + 1)
                    if nxt2:
                        dve.wait_ge(xt_mm, t + 2)
                        normalise(nc, k, xn[:, :], t + 2).then_inc(xn_ok, 1)
                    dve.wait_ge(x2_mm, t + 1)
                    nc.vector.tensor_tensor(x2[:, :], both(HT), b2[:, :], ALU.add).then_inc(y2_ok, 1)
                    dve.wait_ge(y2_ok, t + 2)
                    dve.wait_ge(g3_ok, t + 1)
                    chain.done(nc.vector.tensor_tensor(x2[:, :], x2[:, :], g3[:, :], ALU.mult))
                    nc.vector.tensor_reduce(y[:, :], x2[:, :].rearrange("p (e d) -> p d e", e=E0), AX.X,
                                            ALU.add).then_inc(x2_ok, 1)
                    dve.wait_ge(x2_ok, t + 1)
                    chain.done(nc.vector.tensor_tensor(xt, xt, y[:, :], ALU.add))
                    nc.vector.nop(nofuse=True)
                    nc.vector.bn_stats(at(k.stats, t), xt)
                    chain.end()

                normalise(nc, k, xn[:, :], 0).then_inc(xn_ok, 1)
                weigh(0)
                dve.wait_ge(xt_mm, 1)
                normalise(nc, k, xn[:, :], 1).then_inc(xn_ok, 1)
                with dve.Fori(0, T - 2) as t:
                    step(t)
                step(T - 2, nxt2=False)
                step(T - 1, nxt=False, nxt2=False)

            @block.gpsimd
            def _(pool):
                def bias1(t):
                    pool.wait_ge(z_raw, t + 1)
                    nc.gpsimd.tensor_tensor(z[:, :], z[:, :], b1[:, :], ALU.add).then_inc(z_ok, 1)

                def step(t, nxt=True):
                    nc.gpsimd.tensor_tensor(ex(mb3[:, :]), ex(b3[:, :]), col(mask, t), ALU.mult).then_inc(mb3_ok, 1)
                    pool.wait_ge(mb3_ok, t + 1)
                    pool.wait_ge(g3_raw, t + 1)
                    nc.gpsimd.tensor_tensor(g3[:, :], g3[:, :], mb3[:, :], ALU.add).then_inc(g3_ok, 1)
                    pool.wait_ge(g3_ok, t + 1)
                    if nxt:
                        bias1(t + 1)

                bias1(0)
                with pool.Fori(0, T - 1) as t:
                    step(t)
                step(T - 1, nxt=False)


def alibi_weights(nc, ctx, w):
    sizes = [(n, [P, D]) for n in ("wq", "wk", "wv", "wo", "bo")] + [
        ("alibi", [P, H, N]), ("hm", [P, H]), ("bm", [P, SEQ])]
    bufs = [ctx.enter_context(nc.sbuf_tensor(f"al_{n}", size, F32)) for n, size in sizes]
    return bufs, [(b, w[n]) for b, (n, size) in zip(bufs, sizes)]


def stage_alibi(nc, k, bufs):
    with ExitStack() as ctx:
        sb = lambda n, s: ctx.enter_context(nc.sbuf_tensor(f"al_{n}", s, F32))
        sem = lambda n: k.sem(f"al_{n}")
        ps = k.ps
        wq, wk, wv, wo, bo, alibi, hm, bm = bufs
        xn, xnT = sb("xn", [P, D]), sb("xnT", [P, P])
        qT = sb("qT", [P, P])
        vbd = sb("vbd", [P, 2, H * (D + DH1)])
        kbd = sb("kbd", [P, SEQ, H, N])
        e, pT = sb("e", [P, H, N]), sb("pT", [P, H, N])
        pbd = sb("pbd", [P, 2, H, SEQ, N])
        mx, den, rec = sb("mx", [P, H]), sb("den", [P, H]), sb("rec", [P, H])
        aT = sb("aT", [P, P])
        zero_ok = sem("zero_ok")
        (ln, xn_ok, xt_mm, xt_sb, kq_mm, v_mm, k_ok, q_ok, v_ok, s_mm, sub_ok, exp_ok, pt_ok, pbd_ok, o_mm, at_ok,
         wo_mm, x_ok, steps, steps_x) = [sem(n) for n in (
             "ln xn_ok xt_mm xt_sb kq_mm v_mm k_ok q_ok v_ok s_mm sub_ok exp_ok pt_ok pbd_ok o_mm at_ok "
             "wo_mm x_ok steps steps_x").split()]
        XT, K_B, Q_B, S_B, O_B, WO, V_B = range(7)
        block = ctx.enter_context(nc.Block())

        def tiles(eng, step):
            step(0, 0, first=True)
            with eng.Fori(0, (T - 4) // 2) as i:
                for j in (1, 0):
                    step(2 * i + 2 - j, j)
            step(T - 3, 1, nxt3=False)
            step(T - 2, 0, nxt2=False, nxt3=False)
            step(T - 1, 1, nxt=False, nxt2=False, nxt3=False)

        @block.tensor
        def _(pe):

            def turn(t):
                pe.wait_ge(xn_ok, t + 1)
                nc.tensor.transpose(ps[:, XT, 0:P], xn[:, :], k.ident[:, :]).then_inc(xt_mm, 1)

            def keys_queries(t):
                pe.wait_ge(xt_sb, t + 1)
                nc.tensor.matmul(ps[:, K_B, 0:P], wk[:, :], xnT[:, :], start=True, stop=True)
                nc.tensor.matmul(ps[:, Q_B, 0:P], wq[:, :], xnT[:, :], start=True, stop=True).then_inc(kq_mm, 1)

            def value(t):
                nc.tensor.matmul(ps[:, V_B, 0:P], xnT[:, :], wv[:, :], start=True, stop=True).then_inc(v_mm, 1)

            def scores(t):
                pe.wait_ge(q_ok, t + 1)
                pe.wait_ge(k_ok, t + 1)
                for b in range(SEQ):
                    last = nc.tensor.matmul(ps[N * b:N * b + N, S_B, :], qT[:, N * b:N * b + N],
                                            kbd[:, b, :, :], start=True, stop=True)
                last.then_inc(s_mm, 1)

            def values(t, j):
                pe.wait_ge(pbd_ok, t + 2)
                pe.wait_ge(v_ok, t + 1)
                blocks = vbd[:, j, 0:H * D].rearrange("p (h c) -> p h c", h=H)
                for h in range(H):
                    last = nc.tensor.matmul(ps[:, O_B, 0:P], blocks[:, h, :],
                                            pbd[:, j, h, :, :].rearrange("p b n -> p (b n)"),
                                            start=h == 0, stop=h == H - 1)
                last.then_inc(o_mm, 1)

            def out(t):
                pe.wait_ge(at_ok, t + 1)
                pe.wait_ge(x_ok, t + 1)
                nc.tensor.matmul(ps[:, WO, 0:D], aT[:, :], wo[:, :], start=True, stop=True).then_inc(wo_mm, 1)

            def step(t, j, first=False, nxt=True, nxt2=True, nxt3=True):
                if nxt:
                    pe.wait_ge(sub_ok, 2 * t + 2)
                    scores(t + 1)
                if nxt2:
                    keys_queries(t + 2)
                if not first:
                    out(t - 1)
                values(t, j)
                if nxt2:
                    pe.wait_ge(v_ok, t + 2)
                    value(t + 2)
                if nxt3:
                    turn(t + 3)

            pe.sem_inc(o_mm, 2)
            turn(0)
            keys_queries(0)
            value(0)
            turn(1)
            scores(0)
            keys_queries(1)
            pe.wait_ge(v_ok, 1)
            value(1)
            turn(2)
            tiles(pe, step)
            out(T - 1)

        @block.scalar
        def _(act):
            rstd_act(nc, k, act, ln)

            def turn(t):
                act.wait_ge(xt_mm, t + 1)
                nc.scalar.copy(xnT[:, :], ps[:, XT, 0:P]).then_inc(xt_sb, 1)

            def query(t):
                act.wait_ge(kq_mm, t + 1)
                nc.scalar.mul(qT[:, :], ps[:, Q_B, 0:P], DH1 ** -0.5).then_inc(q_ok, 1)

            def value(t, j):
                act.wait_ge(v_mm, t + 1)
                nc.scalar.copy(vbd[:, j, :].rearrange("p (h c) -> p h c", h=H)[:, :, 0:DH1],
                               ps[:, V_B, 0:P].rearrange("p (h d) -> p h d", h=H)).then_inc(v_ok, 1)

            def expo(t):
                act.wait_ge(sub_ok, 2 * t + 2)
                nc.scalar.activation(e[:, :, :], e[:, :, :], ACT.Exp).then_inc(exp_ok, 1)

            def moved(t):
                act.wait_ge(o_mm, t + 3)
                nc.scalar.copy(aT[:, :], ps[:, O_B, 0:P]).then_inc(at_ok, 1)

            def step(t, j, first=False, nxt=True, nxt2=True, nxt3=True):
                if nxt2:
                    query(t + 2)
                if not first:
                    moved(t - 1)
                if nxt:
                    expo(t + 1)
                if nxt2:
                    value(t + 2, j)
                if nxt3:
                    turn(t + 3)

            turn(0)
            query(0)
            act.wait_ge(zero_ok, 1)
            value(0, 0)
            turn(1)
            query(1)
            expo(0)
            value(1, 1)
            turn(2)
            tiles(act, step)
            moved(T - 1)

        @block.vector
        def _(dve):
            dve.sem_inc(x_ok, 1)
            nc.vector.memset(vbd[:, :, :], 0.0).then_inc(zero_ok, 1)
            rstd_dve(nc, k, dve, ln, EPS_LN)
            soft, outs = Chain(dve, steps, 4), Chain(dve, steps_x, 2)
            hk = [P, H, N]

            def keys(t):
                dve.wait_ge(kq_mm, t + 1)
                shape = [P, SEQ, H, N]
                nc.vector.tensor_tensor(kbd[:, :, :, :], ps[:, K_B, 0:P].rearrange("p (b n) -> p b n", b=SEQ)[
                    :, :, None, :].to_broadcast(shape), hm[:, None, :, None].to_broadcast(shape), ALU.mult).then_inc(k_ok, 1)

            def exponents(t):
                soft.tile(t)
                dve.wait_ge(s_mm, t + 1)
                nc.vector.tensor_tensor(e[:, :, :], ps[:, S_B, :].rearrange("p (h n) -> p h n", h=H), alibi[:, :, :],
                                        ALU.add).then_inc(sub_ok, 1)
                dve.wait_ge(sub_ok, 2 * t + 1)
                soft.done(nc.vector.tensor_reduce(mx[:, :], e[:, :, :], AX.X, ALU.max))
                nc.vector.tensor_tensor(e[:, :, :], e[:, :, :], mx[:, :, None].to_broadcast(hk),
                                        ALU.subtract).then_inc(sub_ok, 1)

            def spread(t, j):
                dve.wait_ge(exp_ok, t + 1)
                soft.done(nc.vector.tensor_reduce(den[:, :], e[:, :, :], AX.X, ALU.add))
                soft.done(nc.vector.reciprocal(rec[:, :], den[:, :]))
                soft.done(nc.vector.tensor_tensor(e[:, :, :], e[:, :, :], rec[:, :, None].to_broadcast(hk), ALU.mult))
                dve.wait_ge(pbd_ok, t + 1)
                nc.vector.transpose(pT[:, :, :].rearrange("p h n -> p (h n)"),
                                    e[:, :, :].rearrange("p h n -> p (h n)")).then_inc(pt_ok, 1)
                soft.end()

            def residual(t):
                outs.tile(t)
                dve.wait_ge(wo_mm, t + 1)
                add_to_x_and_count(nc, k, outs, t, ps[:, WO, 0:D], bo[:, :]).then_inc(x_ok, 1)

            def step(t, j, first=False, nxt=True, nxt2=True, nxt3=True):
                if nxt:
                    dve.wait_ge(pt_ok, t + 1)
                    exponents(t + 1)
                if nxt2:
                    keys(t + 2)
                if nxt3:
                    dve.wait_ge(xt_mm, t + 3)
                    normalise(nc, k, xn[:, :], t + 3).then_inc(xn_ok, 1)
                if nxt:
                    spread(t + 1, 1 - j)
                if not first:
                    residual(t - 1)

            normalise(nc, k, xn[:, :], 0).then_inc(xn_ok, 1)
            dve.wait_ge(xt_mm, 1)
            normalise(nc, k, xn[:, :], 1).then_inc(xn_ok, 1)
            keys(0)
            dve.wait_ge(xt_mm, 2)
            normalise(nc, k, xn[:, :], 2).then_inc(xn_ok, 1)
            exponents(0)
            keys(1)
            spread(0, 0)
            tiles(dve, step)
            residual(T - 1)

        @block.gpsimd
        def _(pool):
            pool.sem_inc(pbd_ok, 1)
            shape = [P, H, SEQ, N]
            with pool.Fori(0, T // 2) as i:
                for j in range(2):
                    t = 2 * i + j
                    pool.wait_ge(pt_ok, t + 1)
                    pool.wait_ge(o_mm, t + 1)
                    nc.gpsimd.tensor_tensor(pbd[:, j, :, :, :], pT[:, :, None, :].to_broadcast(shape),
                                            bm[:, None, :, None].to_broadcast(shape), ALU.mult).then_inc(pbd_ok, 1)


def stage_moe1(nc, k, w):
    EG = 8
    UNITS = [8, 8, 8, 8, 1]
    NU = len(UNITS)
    COLS = (E1 + 1) * I1
    NPAIR = E1 // 2
    with ExitStack() as ctx:
        sb = lambda n, s: ctx.enter_context(nc.sbuf_tensor(f"m1_{n}", s, F32))
        ps = k.ps
        comb = sb("comb", [P, T, E1 + 1])
        wg, wu, wd = sb("wg", [P, COLS]), sb("wu", [P, COLS]), sb("wd", [P, NPAIR + 1, D])
        wide = ctx.enter_context(nc.sbuf_tensor("m1_wide", [P, 4, E1 * I1], F32R))
        loads = [(wg, w["wg"]), (wu, w["wu"]), (wd, w["wd"])]

        with ExitStack() as r:
            rsb = lambda n, s: r.enter_context(nc.sbuf_tensor(f"m1_{n}", s, F32))
            rsem = lambda n: k.sem(f"m1_{n}")
            gate, lower = rsb("gate", [P, E1]), rsb("lower", [P, 8, 8])
            sc, rest = rsb("sc", [P, T, E1]), rsb("rest", [P, T, E1])
            gs, gm = rsb("gs", [P, T, 8]), rsb("gm", [P, T, 8])
            top = rsb("top", [P, T, 8])
            tot = rsb("tot", [P, T])
            gt, eq = rsb("gt", [P, T, 8, 8]), rsb("eq", [P, T, 8, 8])
            halves = rsem("halves")
            g_in, w_in, ln, st, sg = rsem("g_in"), rsem("w_in"), rsem("ln"), rsem("st"), rsem("sg")
            logits = ps[:, 4:6, :].rearrange("p a b -> p (a b)")
            tensor, vector, scalar, lg_mm = router_logits(nc, k, r, "m1", gate[:, :], g_in, E1, logits, rsb, rsem)
            block = r.enter_context(nc.Block())

            @block.sync
            def _(sp):
                sp.dma_start(gate[:, :], w["gate"]).then_inc(g_in, 16)
                sp.dma_start(lower[:, :, :], w["lower"]).then_inc(g_in, 16)
                for dst, src in loads:
                    sp.dma_start(dst[:], src).then_inc(w_in, 16)
                sp.wait_ge(g_in, 32)
                sp.wait_ge(w_in, 16 * len(loads))

            @block.tensor
            def _(pe):
                pe.wait_ge(g_in, 32)
                tensor(pe)

            @block.scalar
            def _(act):
                rstd_act(nc, k, act, ln)
                scalar(act)
                act.wait_ge(lg_mm, T + 2)
                nc.scalar.activation(sc[:, :, :].rearrange("p t e -> p (t e)"), logits, ACT.Sigmoid).then_inc(sg, 1)

            @block.vector
            def _(dve):
                rstd_dve(nc, k, dve, ln, EPS_LN)
                vector(dve)
                dve.wait_ge(w_in, 16 * len(loads))
                for n, src in enumerate((wg, wu)):
                    split(nc, dve, wide[:, 2 * n, :], wide[:, 2 * n + 1, :], src[:, 0:E1 * I1], halves, n)
                dve.wait_ge(g_in, 32)
                dve.wait_ge(sg, 1)
                four = sc[:, :, :].rearrange("p t (g e) -> p t g e", g=8)
                nc.vector.tensor_reduce(gs[:, :, :], four, AX.X, ALU.add).then_inc(st, 1)
                dve.wait_ge(st, 1)
                ranked_mask(nc, dve, st, gs, gt[:, :, :, :], eq[:, :, :, :], lower, gm[:, :, :], 8, 4, 1)
                nc.vector.tensor_tensor(four, four, gm[:, :, :, None].to_broadcast([P, T, 8, 4]), ALU.mult).then_inc(st, 1)
                dve.wait_ge(st, 7)
                for t in range(T):
                    last = nc.vector.max(top[:, t, :], sc[:, t, :])
                last.then_inc(st, 1)
                dve.wait_ge(st, 8)
                for t in range(T):
                    last = nc.vector.match_replace(out=rest[:, t, :], in_to_replace=top[:, t, :], in_values=sc[:, t, :],
                                                   imm_value=-1.0)
                last.then_inc(st, 1)
                dve.wait_ge(st, 9)
                nc.vector.scalar_tensor_tensor(rest[:, :, :], rest[:, :, :], 0.0, sc[:, :, :], ALU.is_lt,
                                               ALU.mult).then_inc(st, 1)
                dve.wait_ge(st, 10)
                nc.vector.tensor_reduce(tot[:, :], rest[:, :, :], AX.X, ALU.add).then_inc(st, 1)
                dve.wait_ge(st, 11)
                nc.vector.tensor_scalar(tot[:, :], tot[:, :], 1e-12, None, ALU.max).then_inc(st, 1)
                dve.wait_ge(st, 12)
                nc.vector.reciprocal(tot[:, :], tot[:, :]).then_inc(st, 1)
                dve.wait_ge(st, 13)
                nc.vector.memset(comb[:, :, E1:E1 + 1], 1.0)
                nc.vector.tensor_tensor(comb[:, :, 0:E1], rest[:, :, :], tot[:, :, None].to_broadcast([P, T, E1]), ALU.mult)

        with ExitStack() as m:
            sb = lambda n, s: m.enter_context(nc.sbuf_tensor(f"m1_{n}", s, F32))
            sem = lambda n: k.sem(f"m1_{n}")
            xn, xnT = sb("xn", [P, D]), sb("xnT", [P, 2, P])
            xh, xl = [m.enter_context(nc.sbuf_tensor(f"m1_{n}", [P, 2, P], F32R)) for n in ("xh", "xl")]
            xh_ok, xs_ok = sem("xh_ok"), sem("xs_ok")
            sg, hh, hT = sb("sg", [P, 2, 512]), sb("hh", [P, 2, 512]), sb("hT", [P, 2, 512])
            comb_t = sb("comb_t", [P, 2, E1 + 1])
            (xn_ok, xt_mm, xt_sb, gu_mm, sg_ok, hh_raw, hh_ok, tr_mm, tr_ok, dn_mm, out_mm, x_ok, steps) = [sem(n) for n in (
                "xn_ok xt_mm xt_sb gu_mm sg_ok hh_raw hh_ok tr_mm tr_ok dn_mm out_mm x_ok steps").split()]
            G_B, T_B, ACC, XT = 0, 4, 6, 7
            block = m.enter_context(nc.Block())

            @block.tensor
            def _(pe):
                def turn(t):
                    pe.wait_ge(xn_ok, t + 1)
                    nc.tensor.transpose(ps[:, XT, 0:P], xn[:, :], k.ident[:, :]).then_inc(xt_mm, 1)

                def gates(g, j, v):
                    n, c = UNITS[g] * I1, EG * I1 * g
                    b = G_B + 2 * ((NU * j + g) % 2)
                    if UNITS[g] > 1:
                        for half in range(2):
                            last = product(nc, ps[:, b + half, 0:n], (xh[:, j, :], xl[:, j, :]),
                                           [wide[:, 2 * half + m, c:c + n] for m in range(2)])
                    else:
                        for half, wt in enumerate((wg, wu)):
                            last = nc.tensor.matmul(ps[:, b + half, 0:n], xnT[:, j, :], wt[:, c:c + n],
                                                    start=True, stop=True)
                    last.then_inc(gu_mm, 1)

                def turn_h(g, j, v):
                    par = (NU * j + g) % 2
                    pe.wait_ge(hh_ok, v + 1)
                    if UNITS[g] == 1:
                        nc.tensor.nop(nofuse=True)
                    for c in range(max(UNITS[g] // 2, 1)):
                        n = min(P, UNITS[g] * I1)
                        last = nc.tensor.transpose(ps[0:n, T_B + par, c * P:c * P + P], hh[:, par, c * P:c * P + n],
                                                   k.ident[:, :])
                    last.then_inc(tr_mm, 1)

                def down(g, j, v):
                    par = (NU * j + g) % 2
                    pe.wait_ge(tr_ok, v + 1)
                    for c in range(max(UNITS[g] // 2, 1)):
                        n = min(P, UNITS[g] * I1)
                        last = nc.tensor.matmul(ps[:, ACC, 0:D], hT[0:n, par, c * P:c * P + P], wd[0:n, 4 * g + c, :],
                                                start=g == 0 and c == 0, stop=g == NU - 1)
                    last.then_inc(dn_mm, 1)

                def tile(t, j, first=False, last=False):
                    for g in range(NU):
                        v = NU * t + g
                        if g < NU - 1:
                            gates(g + 1, j, v + 1)
                        elif not last:
                            pe.wait_ge(xs_ok, t + 2)
                            gates(0, 1 - j, v + 1)
                        if g == 1 and not last:
                            turn(t + 1)
                        if g > 0:
                            if g == 1 and not first:
                                pe.wait_ge(x_ok, t)
                            down(g - 1, j, v - 1)
                        elif not first:
                            down(NU - 1, 1 - j, v - 1)
                        turn_h(g, j, v)

                turn(0)
                pe.wait_ge(xs_ok, 1)
                gates(0, 0, 0)
                tile(0, 0, first=True)
                with pe.Fori(0, T // 2 - 1) as i:
                    tile(2 * i + 1, 1)
                    tile(2 * i + 2, 0)
                tile(T - 1, 1, last=True)
                down(NU - 1, 1, NU * T - 1)

            @block.scalar
            def _(act):
                def turn(t, j):
                    act.wait_ge(xt_mm, t + 1)
                    nc.scalar.copy(xnT[:, j, :], ps[:, XT, 0:P]).then_inc(xt_sb, 1)

                def silu(g, j, v):
                    par, n = (NU * j + g) % 2, UNITS[g] * I1
                    act.wait_ge(gu_mm, v + 1)
                    nc.scalar.activation(sg[:, par, 0:n], ps[:, G_B + 2 * par, 0:n], ACT.Silu).then_inc(sg_ok, 1)

                def moved(g, j, v):
                    par = (NU * j + g) % 2
                    p, n = (P, 512) if UNITS[g] > 1 else (I1, P)
                    act.wait_ge(tr_mm, v + 1)
                    nc.scalar.copy(hT[0:p, par, 0:n], ps[0:p, T_B + par, 0:n]).then_inc(tr_ok, 1)

                def tile(t, j, last=False):
                    for g in range(NU):
                        v = NU * t + g
                        if g < NU - 1:
                            silu(g + 1, j, v + 1)
                        elif not last:
                            silu(0, 1 - j, v + 1)
                        if g == 1 and not last:
                            turn(t + 1, 1 - j)
                        moved(g, j, v)

                turn(0, 0)
                silu(0, 0, 0)
                with act.Fori(0, T // 2 - 1) as i:
                    tile(2 * i, 0)
                    tile(2 * i + 1, 1)
                tile(T - 2, 0)
                tile(T - 1, 1, last=True)

            @block.vector
            def _(dve):
                def weights(t, j):
                    nc.vector.tensor_scalar(comb_t[:, j, :], at(comb, t), 1.0, None, ALU.mult)

                def up(g, j, v):
                    par, n = (NU * j + g) % 2, UNITS[g] * I1
                    dve.wait_ge(sg_ok, v + 1)
                    nc.vector.tensor_tensor(hh[:, par, 0:n], ps[:, G_B + 2 * par + 1, 0:n], sg[:, par, 0:n],
                                            ALU.mult).then_inc(hh_raw, 1)

                def parts(t, j):
                    dve.wait_ge(xt_sb, t + 1)
                    split(nc, dve, xh[:, j, :], xl[:, j, :], xnT[:, j, :], xh_ok, t).then_inc(xs_ok, 1)

                def out(t):
                    dve.wait_ge(dn_mm, NU * t + NU)
                    nc.vector.tensor_tensor(at(k.x, t), ps[:, ACC, 0:D], at(k.x, t), ALU.add).then_inc(x_ok, 1)

                def tile(t, j, first=False, last=False, last2=False):
                    for g in range(NU):
                        v = NU * t + g
                        if g < NU - 1:
                            up(g + 1, j, v + 1)
                        elif not last:
                            up(0, 1 - j, v + 1)
                        if g == 0 and not first:
                            out(t - 1)
                        if g == 0 and not last:
                            weights(t + 1, 1 - j)
                        if g == 1 and not last:
                            parts(t + 1, 1 - j)
                        if g == 2 and not last and not last2:
                            dve.wait_ge(xt_mm, t + 2)
                            normalise(nc, k, xn[:, :], t + 2).then_inc(xn_ok, 1)

                normalise(nc, k, xn[:, :], 0).then_inc(xn_ok, 1)
                weights(0, 0)
                parts(0, 0)
                up(0, 0, 0)
                dve.wait_ge(xt_mm, 1)
                normalise(nc, k, xn[:, :], 1).then_inc(xn_ok, 1)
                tile(0, 0, first=True)
                with dve.Fori(0, T // 2 - 2) as i:
                    tile(2 * i + 1, 1)
                    tile(2 * i + 2, 0)
                tile(T - 3, 1)
                tile(T - 2, 0, last2=True)
                tile(T - 1, 1, last=True)
                out(T - 1)

            @block.gpsimd
            def _(pool):
                def weigh(g, j, v):
                    par, n = (NU * j + g) % 2, UNITS[g]
                    pool.wait_ge(hh_raw, v + 1)
                    h = hh[:, par, 0:n * I1].rearrange("p (e i) -> p e i", e=n)
                    nc.gpsimd.tensor_tensor(h, h, comb_t[:, j, EG * g:EG * g + n, None].to_broadcast([P, n, I1]),
                                            ALU.mult).then_inc(hh_ok, 1)

                with pool.Fori(0, T // 2) as i:
                    for j in range(2):
                        for g in range(NU):
                            weigh(g, j, NU * (2 * i + j) + g)


def stage_store(nc, k, out_dram):
    with ExitStack() as ctx:
        stored = k.sem("stored")
        block = ctx.enter_context(nc.Block())

        @block.sync
        def _(sp):
            sp.dma_start(out_dram.rearrange("(t p) d -> p t d", p=P), k.x[:, :, :]).then_inc(stored, 16)
            sp.wait_ge(stored, 16)


def program(nc, d, out, scratch):
    with ExitStack() as ctx:
        k = Core(nc, ctx)
        with ExitStack() as layer0:
            enc, enc_loads = performer_weights(nc, layer0, {n[2:]: a for n, a in d.items() if n.startswith("e_")})
            stage_xattn(nc, k, "l0", {n[3:]: a for n, a in d.items() if n.startswith("a0_")},
                        d["ctx_t"], d["ctx_k"], d["ctx_l"], d["last_mask"], scratch, enc_loads, d["x"], d["ident"])
            stage_performer(nc, k, enc)
        stage_moe0(nc, k, {n[2:]: a for n, a in d.items() if n.startswith("m_")})
        k.clear_sems()
        with ExitStack() as layer1:
            al, al_loads = alibi_weights(nc, layer1, {n[2:]: a for n, a in d.items() if n.startswith("s_")})
            stage_xattn(nc, k, "l1", {n[3:]: a for n, a in d.items() if n.startswith("a1_")},
                        d["ctx_t"], d["ctx_k"], d["ctx_l"], d["last_mask"], scratch, al_loads)
            stage_alibi(nc, k, al)
        stage_moe1(nc, k, {n[2:]: a for n, a in d.items() if n.startswith("g_")})
        stage_store(nc, k, out)


def layout(v):
    f = np.float32
    rows = lambda a, n=P: np.broadcast_to(np.asarray(a), (n, np.asarray(a).shape[-1]))
    x = np.asarray(v["x"]).reshape(B * N, D)
    c = np.asarray(v["ctx_768"])
    ca = np.concatenate([c, np.ones((B, NK, 1), f)], axis=2).reshape(T, SEQ, NK, CA)
    ctx_t = ca.transpose(0, 3, 1, 2).reshape(T, CA, SEQ * NK)
    ctx_k = ca[:, :, :256].reshape(T, SEQ, 2, P, CA).transpose(0, 3, 1, 2, 4).reshape(T, P, SEQ * 2 * CA)
    ctx_l = ca[:, :, 256].reshape(B, CA).T
    last_mask = np.tile(np.repeat(np.eye(2 * SEQ, SEQ, dtype=f), HG, axis=0), (HG, 1))
    pad = lambda a: np.concatenate([a, np.zeros((a.shape[0], 1), f)], axis=1)
    two = lambda a: a.reshape(H // 2, P, a.shape[1]).transpose(1, 0, 2)
    d = {"x": x, "ident": np.eye(P, dtype=f), "ctx_t": ctx_t, "ctx_k": ctx_k, "ctx_l": ctx_l,
         "last_mask": last_mask}
    d["a0_wqT"] = two(np.asarray(v["L0_xattn_Wq"]).T)
    d["a0_wkT"] = two(pad(np.asarray(v["L0_xattn_Wk"]).T))
    d["a0_wvT"] = two(pad(np.asarray(v["L0_xattn_Wv"]).T))
    d["a0_wo"] = two(np.asarray(v["L0_xattn_Wo"]))
    d["a0_bo"] = rows(v["L0_xattn_bo"])
    kv = np.concatenate([np.asarray(v["L1_xattn_kv_w"]), np.asarray(v["L1_xattn_kv_b"])[None]], axis=0).T
    d["a1_wqT"] = np.asarray(v["L1_xattn_q_w"]).T
    d["a1_kaT"], d["a1_vaT"] = kv[:D], kv[D:]
    d["a1_wo"] = np.asarray(v["L1_xattn_proj_w"])
    d["a1_head_mask"] = np.repeat(np.eye(H, dtype=f), DH1, axis=0)
    d["a1_qb"] = np.asarray(v["L1_xattn_q_b"])[:, None]
    d["a1_bo"] = rows(v["L1_xattn_proj_b"])
    flat = lambda n: np.asarray(v[n]).reshape(D, H * DH0)
    same = lambda n, size: np.repeat(np.repeat(np.eye(n, dtype=f), size, 0), size, 1)
    d["e_wq"], d["e_wk"], d["e_wv"] = flat("L0_attn_Wq"), flat("L0_attn_Wk"), flat("L0_attn_Wv")
    d["e_wqT"], d["e_wkT"] = two(flat("L0_attn_Wq").T), two(flat("L0_attn_Wk").T)
    d["e_projT"] = np.tile(np.asarray(v["L0_attn_proj"]).T, (2, 1))
    d["e_wo"] = two(np.asarray(v["L0_attn_Wo"]).reshape(H * DH0, D))
    d["e_blocks"] = same(2, DH0) * f(-0.5 * DH0 ** -0.5)
    d["e_mask"] = same(SEQ, N)
    d["e_w1"] = np.asarray(v["L0_attn_W1"])
    d["e_w2"] = np.asarray(v["L0_attn_W2"]).reshape(FF // P, P, D).transpose(1, 0, 2)
    d["e_b1"] = np.asarray(v["L0_attn_b1"]).reshape(FF // P, P).T
    d["e_rows"] = np.stack([rows(v[n]) for n in ("L0_attn_ln1_g", "L0_attn_ln1_b", "L0_attn_b2", "L0_attn_ln2_g",
                                                 "L0_attn_ln2_b")], axis=1)
    lower = np.broadcast_to(np.tril(np.ones((8, 8), f), -1), (P, 8, 8))
    up = lambda n: np.asarray(v[n]).transpose(2, 0, 1).reshape(D, -1)
    for n in ("w1", "w2", "w3"):
        d["m_" + n] = up("L0_ffn_" + n)
    for n in ("b1", "b2", "b3"):
        d["m_" + n] = rows(np.asarray(v["L0_ffn_" + n]).reshape(-1))
    d["m_gate"], d["m_lower"] = np.asarray(v["L0_ffn_gate_w"]).T, lower
    d["m_sw12"] = np.concatenate([np.asarray(v["L0_ffn_sw1"]), np.asarray(v["L0_ffn_sw2"])]).T
    d["m_sw3"] = np.asarray(v["L0_ffn_sw3"]).T.reshape(2, P, D).transpose(1, 0, 2)
    for n in "qkvo":
        d["s_w" + n] = np.asarray(v["L1_attn_W" + n]).T
    d["s_bo"] = rows(v["L1_attn_bo"])
    start = 2.0 ** (-2.0 ** (-(np.log2(H) - 3)))
    slopes = np.array([start * start ** i for i in range(H)], f)
    rel = np.abs(np.arange(N)[None, :] - np.arange(N)[:, None]).astype(f)
    d["s_alibi"] = np.tile(-slopes[None, :, None] * rel[:, None, :], (SEQ, 1, 1))
    d["s_hm"], d["s_bm"] = d["a1_head_mask"], np.repeat(np.eye(SEQ, dtype=f), N, axis=0)
    both = lambda e, sh: np.concatenate([np.asarray(v[e]).reshape(E1 * I1, D), np.asarray(v[sh])]).T
    d["g_gate"], d["g_lower"] = np.asarray(v["L1_ffn_gate_w"]).T, lower
    d["g_wg"] = both("L1_ffn_expert_gate", "L1_ffn_shared_gate_w")
    d["g_wu"] = both("L1_ffn_expert_up", "L1_ffn_shared_up_w")
    wd = np.zeros(((E1 + 2) * I1, D), f)
    wd[:E1 * I1] = np.asarray(v["L1_ffn_expert_down"]).transpose(0, 2, 1).reshape(E1 * I1, D)
    wd[E1 * I1:(E1 + 1) * I1] = np.asarray(v["L1_ffn_shared_down_w"]).T
    d["g_wd"] = wd.reshape(E1 // 2 + 1, P, D).transpose(1, 0, 2)
    return {n: np.ascontiguousarray(a) for n, a in d.items()}


def kernel(**inputs):
    import concourse.bacc as bacc
    from concourse.bass_utils import run_bass_kernel_spmd

    nc = bacc.Bacc("TRN2", target_bir_lowering=False, num_devices=1)
    arrays = layout(inputs)
    aps = {n: nc.dram_tensor(f"in_{n}", a.shape, mybir.dt.from_np(a.dtype), kind="ExternalInput").ap()
           for n, a in arrays.items()}
    out = nc.dram_tensor("out_x", (B * N, D), F32, kind="ExternalOutput").ap()
    scratch = nc.dram_tensor("scratch", (B, H * D), F32, kind="Internal").ap()
    program(nc, aps, out, scratch)
    r = run_bass_kernel_spmd(nc, [{f"in_{n}": a for n, a in arrays.items()}], core_ids=[0])
    return r.results[0]["out_x"].reshape(B, N, D)
```
